# Optimizing a Trainium2 kernel written in Bass

```python
import numpy as np
import jax
import jax.numpy as jnp

def _softmax(x, axis=-1):
    return jax.nn.softmax(x, axis=axis)

def _gelu(x):
    return jax.nn.gelu(x, approximate=True)

def _silu(x):
    return jax.nn.silu(x)

def _sigmoid(x):
    return jax.nn.sigmoid(x)

def _layernorm(x, axis=-1, eps=1e-05):
    m = jnp.mean(x, axis=axis, keepdims=True)
    v = jnp.var(x, axis=axis, keepdims=True)
    return (x - m) / jnp.sqrt(v + eps)

def _scatter_add(tgt, idx, src, axis=0):
    return tgt.at[idx].add(src)

def _segment_sum(src, seg, n):
    return jax.ops.segment_sum(src, seg, n)
kernel_name = 'mk_hybrid_d2_jaxref_r8_49b8dd'

def setup_inputs(seed: int=0):
    np.random.seed(seed)
    _w = jnp.asarray

    def _L0_attn_a_setup():
        import jax, jax.numpy as jnp
        import numpy as np
        B, N, D, BS = (2, 512, 256, 32)

        def rms_norm(x):
            eps = jnp.asarray(jnp.finfo(x.dtype).eps, x.dtype)
            return x * jax.lax.rsqrt(jnp.mean(x * x, axis=-1, keepdims=True) + eps)

        def la_kernel(q, k, v, bs):
            b, n, d = q.shape
            T = n // bs
            qc = q.reshape(b, T, bs, d).transpose(1, 0, 2, 3)
            kc = k.reshape(b, T, bs, d).transpose(1, 0, 2, 3)
            vc = v.reshape(b, T, bs, d).transpose(1, 0, 2, 3)
            mask = jnp.tril(jnp.ones((bs, bs), q.dtype))

            def step(kv, qkv):
                qt, kt, vt = qkv
                s = jnp.einsum('bid,bjd->bij', qt, kt) * mask
                ot = jnp.einsum('bij,bjd->bid', s, vt) + jnp.einsum('bid,bde->bie', qt, kv)
                kv = kv + jnp.einsum('bjd,bje->bde', kt, vt)
                return (kv, ot)
            kv0 = jnp.zeros((b, d, d), q.dtype)
            _, o = jax.lax.scan(step, kv0, (qc, kc, vc))
            return o.transpose(1, 0, 2, 3).reshape(b, n, d)
        key = jax.random.key(seed)
        ks = jax.random.split(key, 6)
        scale = 0.02
        x = jax.random.normal(ks[0], (B, N, D), jnp.float32)
        Wq = jax.random.normal(ks[1], (D, D), jnp.float32) * scale
        Wk = jax.random.normal(ks[2], (D, D), jnp.float32) * scale
        Wv = jax.random.normal(ks[3], (D, D), jnp.float32) * scale
        Wg = jax.random.normal(ks[4], (D, D), jnp.float32) * scale
        Wp = jax.random.normal(ks[5], (D, D), jnp.float32) * scale
        return {'x': x, 'Wq': Wq, 'Wk': Wk, 'Wv': Wv, 'Wg': Wg, 'Wp': Wp}
    _L0_attn_a_in = _L0_attn_a_setup()

    def _L0_attn_b_setup():
        import jax, jax.numpy as jnp
        import numpy as np
        from jax import lax
        CHUNK = 32
        ROPE_BASE = 10000.0

        def _forward(x, norm_scale, conv_w, conv_b, in_proj_w, dt_bias, head_mix, out_proj_w):
            B, N, D = x.shape
            H = head_mix.shape[0]
            Dh = D // H
            K = conv_w.shape[-1]
            residual = x
            xf = x.astype(jnp.float32)
            rms = lax.rsqrt(jnp.mean(xf * xf, -1, keepdims=True) + 1e-06)
            xn = jnp.clip(norm_scale * xf * rms, -60000.0, 60000.0).astype(x.dtype)
            xc = lax.conv_general_dilated(xn.transpose(0, 2, 1), conv_w, (1,), [(K - 1, 0)], dimension_numbers=('NCH', 'OIH', 'NCH'), feature_group_count=D)
            xc = xc + conv_b[None, :, None]
            xc = jax.nn.silu(xc.transpose(0, 2, 1))
            fused = xc @ in_proj_w.T
            dt_raw, v, gate = jnp.split(fused, 3, axis=-1)
            dt = jnp.clip(jax.nn.softplus(dt_raw.astype(jnp.float32) + dt_bias), 0.001, 2.0)
            gate = jax.nn.sigmoid(gate)
            log_alpha = -dt
            inv_freq = 1.0 / ROPE_BASE ** (jnp.arange(0, Dh, 2, dtype=jnp.float32) / Dh)
            t = jnp.arange(N, dtype=jnp.float32)
            freqs = t[:, None] * inv_freq[None, :]
            cos = jnp.cos(freqs)[None, :, None, :]
            sin = jnp.sin(freqs)[None, :, None, :]
            v4 = v.reshape(B, N, H, Dh)
            v1, v2 = (v4[..., :Dh // 2], v4[..., Dh // 2:])
            v_rot = jnp.concatenate([v1 * cos - v2 * sin, v1 * sin + v2 * cos], -1).reshape(B, N, D)
            v_in = v_rot * dt
            pad = -N % CHUNK
            if pad:
                v_in = jnp.pad(v_in, ((0, 0), (0, pad), (0, 0)))
                log_alpha = jnp.pad(log_alpha, ((0, 0), (0, pad), (0, 0)))
            NC = v_in.shape[1] // CHUNK
            vc = v_in.reshape(B, NC, CHUNK, D)
            la = log_alpha.reshape(B, NC, CHUNK, D)
            L = jnp.clip(jnp.cumsum(la, axis=2), -20.0, 0.0)
            Lmax = jnp.max(L, axis=2, keepdims=True)
            Ls = L - Lmax
            cum = jnp.cumsum(jnp.exp(-Ls) * vc, axis=2)
            chunk_out = jnp.exp(Ls) * cum
            if NC > 1:
                bd = L[:, :, -1, :]
                bo = chunk_out[:, :, -1, :]
                cd = jnp.clip(jnp.cumsum(bd, axis=1), -80.0, 0.0)
                stab = jnp.max(cd, axis=1, keepdims=True)
                ncd = jnp.clip(cd - stab, -20.0, 0.0)
                seeds = bo * jnp.exp(-ncd)
                shifted = jnp.pad(seeds[:, :-1], ((0, 0), (1, 0), (0, 0)))
                carries = jnp.cumsum(shifted, axis=1) * jnp.exp(ncd)
                final = chunk_out + carries[:, :, None, :] * jnp.exp(L)
            else:
                final = chunk_out
            final = final.astype(x.dtype).reshape(B, -1, D)[:, :N, :]
            vm = jnp.einsum('bnhd,hm->bnmd', final.reshape(B, N, H, Dh), head_mix).reshape(B, N, D)
            out = vm * gate @ out_proj_w.T
            return residual + out
        D, H, K = (256, 16, 4)
        Dh = D // H
        key = jax.random.key(seed)
        ks = jax.random.split(key, 8)
        x = jax.random.normal(ks[0], (2, 512, D), dtype=jnp.float32)
        norm_scale = jnp.ones((D,), jnp.float32)
        conv_w = jax.random.normal(ks[1], (D, 1, K), jnp.float32) * 0.1
        conv_b = jnp.zeros((D,), jnp.float32)
        in_proj_w = jax.random.normal(ks[2], (3 * D, D), jnp.float32) * 0.02
        out_proj_w = jax.random.normal(ks[3], (D, D), jnp.float32) * 0.02
        u = jax.random.uniform(ks[4], (H, Dh), jnp.float32)
        dt = jnp.clip(jnp.exp(u * (np.log(0.1) - np.log(10.0)) + np.log(10.0)), 0.001, None)
        dt_bias = (dt + jnp.log(-jnp.expm1(-dt))).reshape(-1)
        head_mix = jnp.eye(H, dtype=jnp.float32)
        return {'x': x, 'norm_scale': norm_scale, 'conv_w': conv_w, 'conv_b': conv_b, 'in_proj_w': in_proj_w, 'dt_bias': dt_bias, 'head_mix': head_mix, 'out_proj_w': out_proj_w}
    _L0_attn_b_in = _L0_attn_b_setup()

    def _L0_ffn_setup():
        import jax, jax.numpy as jnp
        import numpy as np
        E, TOPK, H, I = (8, 2, 256, 512)
        SOFTCAP = 30.0
        key = jax.random.key(seed)
        ks = jax.random.split(key, 5)
        s = 1.0 / np.sqrt(H)
        si = 1.0 / np.sqrt(I)
        return {'hidden_states': jax.random.normal(ks[0], (4, 256, H), jnp.float32), 'w_gate': jax.random.normal(ks[1], (H, E), jnp.float32) * s, 'w1': jax.random.normal(ks[2], (E, H, I), jnp.float32) * s, 'w3': jax.random.normal(ks[3], (E, H, I), jnp.float32) * s, 'w2': jax.random.normal(ks[4], (E, I, H), jnp.float32) * si}
    _L0_ffn_in = _L0_ffn_setup()

    def _L1_attn_a_setup():
        import jax, jax.numpy as jnp
        import numpy as np
        HIDDEN = 256
        NUM_HEADS = 16
        HEAD_DIM = HIDDEN // NUM_HEADS
        key = jax.random.key(seed)
        ks = jax.random.split(key, 5)
        B, S, H = (2, 256, HIDDEN)
        qkv_bound = float(np.sqrt(6.0 / (H + 3 * H)))
        out_bound = float(np.sqrt(6.0 / (H + H)))
        return {'x': jax.random.normal(ks[0], (B, S, H), dtype=jnp.float32), 'W_qkv': jax.random.uniform(ks[1], (3 * H, H), minval=-qkv_bound, maxval=qkv_bound, dtype=jnp.float32), 'b_qkv': jnp.zeros((3 * H,), dtype=jnp.float32), 'W_out': jax.random.uniform(ks[2], (H, H), minval=-out_bound, maxval=out_bound, dtype=jnp.float32), 'b_out': jnp.zeros((H,), dtype=jnp.float32)}
    _L1_attn_a_in = _L1_attn_a_setup()

    def _L1_attn_b_setup():
        import jax, jax.numpy as jnp
        import numpy as np
        B, T, H, D, HID, K = (2, 64, 16, 128, 256, 4)
        SCALE = D ** (-0.5)
        LN_EPS = 1e-05

        def _dwconv_causal(x, w, b):
            xt = jnp.transpose(x, (0, 2, 1))
            out = jax.lax.conv_general_dilated(xt, w[:, None, :], window_strides=(1,), padding=[(K - 1, 0)], feature_group_count=w.shape[0])
            return jnp.transpose(out, (0, 2, 1)) + b

        def _delta_scan(q, k, v, a, beta):
            ks = k * SCALE
            xs = tuple((jnp.moveaxis(z, 1, 0) for z in (q, ks, v, a, beta)))

            def step(S, t):
                q_t, k_t, v_t, a_t, b_t = t
                y = jnp.einsum('bhvk,bhk->bhv', S, k_t)
                err = y - v_t
                S = a_t[..., None] * S - (b_t[..., None] * err)[..., None] * k_t[:, :, None, :]
                o = jnp.einsum('bhvk,bhk->bhv', S, q_t)
                return (S, o)
            S0 = jnp.zeros((q.shape[0], H, D, D), q.dtype)
            _, o = jax.lax.scan(step, S0, xs)
            return jnp.moveaxis(o, 0, 1)
        key = jax.random.key(seed)
        ks = jax.random.split(key, 16)
        p = lambda k, shape, s=0.02: jax.random.normal(k, shape, jnp.float32) * s
        return {'x': jax.random.normal(ks[0], (B, T, HID), jnp.float32), 'Wq': p(ks[1], (HID, H * D)), 'Wk': p(ks[2], (HID, H * D)), 'Wv': p(ks[3], (HID, H * D)), 'Wa': p(ks[4], (HID, H * D)), 'ba': jnp.zeros((H * D,), jnp.float32), 'Wb': p(ks[5], (HID, H)), 'bb': jnp.zeros((H,), jnp.float32), 'Wg': p(ks[6], (HID, H * D)), 'Wo': p(ks[7], (H * D, HID)), 'qconv_w': p(ks[8], (H * D, K), 0.2), 'qconv_b': jnp.zeros((H * D,), jnp.float32), 'kconv_w': p(ks[9], (H * D, K), 0.2), 'kconv_b': jnp.zeros((H * D,), jnp.float32), 'vconv_w': p(ks[10], (H * D, K), 0.2), 'vconv_b': jnp.zeros((H * D,), jnp.float32), 'ln_g': jnp.ones((D,), jnp.float32), 'ln_b': jnp.zeros((D,), jnp.float32)}
    _L1_attn_b_in = _L1_attn_b_setup()

    def _L1_ffn_setup():
        import jax, jax.numpy as jnp
        import numpy as np
        HID = 256
        N_HEADS = 16
        N_KV = 16
        HEAD_DIM = HID // N_HEADS
        N_EXP = 8
        TOP_K = 2
        MOE_I = 176
        SH_I = 704
        EPS = 1e-06
        ROPE_THETA = 1000000.0

        def _rms(x, w):
            v = jnp.mean(jnp.square(x), axis=-1, keepdims=True)
            return x * jax.lax.rsqrt(v + EPS) * w

        def _rope(q, k):
            S, D = (q.shape[1], q.shape[-1])
            inv = 1.0 / ROPE_THETA ** (jnp.arange(0, D, 2, dtype=jnp.float32) / D)
            freqs = jnp.arange(S, dtype=jnp.float32)[:, None] * inv[None, :]
            emb = jnp.concatenate([freqs, freqs], axis=-1)
            cos = jnp.cos(emb)[None, :, None, :]
            sin = jnp.sin(emb)[None, :, None, :]

            def rot(t):
                t1, t2 = (t[..., :D // 2], t[..., D // 2:])
                return jnp.concatenate([-t2, t1], axis=-1)
            return (q * cos + rot(q) * sin, k * cos + rot(k) * sin)
        key = jax.random.key(seed)
        ks = jax.random.split(key, 20)
        s = 0.02
        d = {'x': jax.random.normal(ks[0], (2, 128, HID), jnp.float32), 'w_ln1': jnp.ones((HID,), jnp.float32), 'wq': jax.random.normal(ks[1], (HID, N_HEADS * HEAD_DIM), jnp.float32) * s, 'bq': jnp.zeros((N_HEADS * HEAD_DIM,), jnp.float32), 'wk': jax.random.normal(ks[2], (HID, N_KV * HEAD_DIM), jnp.float32) * s, 'bk': jnp.zeros((N_KV * HEAD_DIM,), jnp.float32), 'wv': jax.random.normal(ks[3], (HID, N_KV * HEAD_DIM), jnp.float32) * s, 'bv': jnp.zeros((N_KV * HEAD_DIM,), jnp.float32), 'wo': jax.random.normal(ks[4], (N_HEADS * HEAD_DIM, HID), jnp.float32) * s, 'w_ln2': jnp.ones((HID,), jnp.float32), 'w_router': jax.random.normal(ks[5], (HID, N_EXP), jnp.float32) * s, 'w_gate_e': jax.random.normal(ks[6], (N_EXP, HID, MOE_I), jnp.float32) * s, 'w_up_e': jax.random.normal(ks[7], (N_EXP, HID, MOE_I), jnp.float32) * s, 'w_down_e': jax.random.normal(ks[8], (N_EXP, MOE_I, HID), jnp.float32) * s, 'w_sh_gate': jax.random.normal(ks[9], (HID, SH_I), jnp.float32) * s, 'w_sh_up': jax.random.normal(ks[10], (HID, SH_I), jnp.float32) * s, 'w_sh_down': jax.random.normal(ks[11], (SH_I, HID), jnp.float32) * s, 'w_sh_eg': jax.random.normal(ks[12], (HID, 1), jnp.float32) * s}
        return d
    _L1_ffn_in = _L1_ffn_setup()
    _d = {'L0_attn_a_x': _L0_attn_a_in['x'], 'L0_attn_a_Wq': _L0_attn_a_in['Wq'], 'L0_attn_a_Wk': _L0_attn_a_in['Wk'], 'L0_attn_a_Wv': _L0_attn_a_in['Wv'], 'L0_attn_a_Wg': _L0_attn_a_in['Wg'], 'L0_attn_a_Wp': _L0_attn_a_in['Wp'], 'L0_attn_b_norm_scale': _L0_attn_b_in['norm_scale'], 'L0_attn_b_conv_w': _L0_attn_b_in['conv_w'], 'L0_attn_b_conv_b': _L0_attn_b_in['conv_b'], 'L0_attn_b_in_proj_w': _L0_attn_b_in['in_proj_w'], 'L0_attn_b_dt_bias': _L0_attn_b_in['dt_bias'], 'L0_attn_b_head_mix': _L0_attn_b_in['head_mix'], 'L0_attn_b_out_proj_w': _L0_attn_b_in['out_proj_w'], 'L0_ffn_w_gate': _L0_ffn_in['w_gate'], 'L0_ffn_w1': _L0_ffn_in['w1'], 'L0_ffn_w3': _L0_ffn_in['w3'], 'L0_ffn_w2': _L0_ffn_in['w2'], 'L1_attn_a_W_qkv': _L1_attn_a_in['W_qkv'], 'L1_attn_a_b_qkv': _L1_attn_a_in['b_qkv'], 'L1_attn_a_W_out': _L1_attn_a_in['W_out'], 'L1_attn_a_b_out': _L1_attn_a_in['b_out'], 'L1_attn_b_Wq': _L1_attn_b_in['Wq'], 'L1_attn_b_Wk': _L1_attn_b_in['Wk'], 'L1_attn_b_Wv': _L1_attn_b_in['Wv'], 'L1_attn_b_Wa': _L1_attn_b_in['Wa'], 'L1_attn_b_ba': _L1_attn_b_in['ba'], 'L1_attn_b_Wb': _L1_attn_b_in['Wb'], 'L1_attn_b_bb': _L1_attn_b_in['bb'], 'L1_attn_b_Wg': _L1_attn_b_in['Wg'], 'L1_attn_b_Wo': _L1_attn_b_in['Wo'], 'L1_attn_b_qconv_w': _L1_attn_b_in['qconv_w'], 'L1_attn_b_qconv_b': _L1_attn_b_in['qconv_b'], 'L1_attn_b_kconv_w': _L1_attn_b_in['kconv_w'], 'L1_attn_b_kconv_b': _L1_attn_b_in['kconv_b'], 'L1_attn_b_vconv_w': _L1_attn_b_in['vconv_w'], 'L1_attn_b_vconv_b': _L1_attn_b_in['vconv_b'], 'L1_attn_b_ln_g': _L1_attn_b_in['ln_g'], 'L1_attn_b_ln_b': _L1_attn_b_in['ln_b'], 'L1_ffn_w_ln1': _L1_ffn_in['w_ln1'], 'L1_ffn_wq': _L1_ffn_in['wq'], 'L1_ffn_bq': _L1_ffn_in['bq'], 'L1_ffn_wk': _L1_ffn_in['wk'], 'L1_ffn_bk': _L1_ffn_in['bk'], 'L1_ffn_wv': _L1_ffn_in['wv'], 'L1_ffn_bv': _L1_ffn_in['bv'], 'L1_ffn_wo': _L1_ffn_in['wo'], 'L1_ffn_w_ln2': _L1_ffn_in['w_ln2'], 'L1_ffn_w_router': _L1_ffn_in['w_router'], 'L1_ffn_w_gate_e': _L1_ffn_in['w_gate_e'], 'L1_ffn_w_up_e': _L1_ffn_in['w_up_e'], 'L1_ffn_w_down_e': _L1_ffn_in['w_down_e'], 'L1_ffn_w_sh_gate': _L1_ffn_in['w_sh_gate'], 'L1_ffn_w_sh_up': _L1_ffn_in['w_sh_up'], 'L1_ffn_w_sh_down': _L1_ffn_in['w_sh_down'], 'L1_ffn_w_sh_eg': _L1_ffn_in['w_sh_eg']}
    _x0 = _d['L0_attn_a_x']
    _d['L0_attn_a_x'] = jax.random.normal(jax.random.fold_in(jax.random.key(seed), 1), (4, 256, 256), dtype=_x0.dtype)
    del _x0
    return _d

def reference(L0_attn_a_x, L0_attn_a_Wq, L0_attn_a_Wk, L0_attn_a_Wv, L0_attn_a_Wg, L0_attn_a_Wp, L0_attn_b_norm_scale, L0_attn_b_conv_w, L0_attn_b_conv_b, L0_attn_b_in_proj_w, L0_attn_b_dt_bias, L0_attn_b_head_mix, L0_attn_b_out_proj_w, L0_ffn_w_gate, L0_ffn_w1, L0_ffn_w3, L0_ffn_w2, L1_attn_a_W_qkv, L1_attn_a_b_qkv, L1_attn_a_W_out, L1_attn_a_b_out, L1_attn_b_Wq, L1_attn_b_Wk, L1_attn_b_Wv, L1_attn_b_Wa, L1_attn_b_ba, L1_attn_b_Wb, L1_attn_b_bb, L1_attn_b_Wg, L1_attn_b_Wo, L1_attn_b_qconv_w, L1_attn_b_qconv_b, L1_attn_b_kconv_w, L1_attn_b_kconv_b, L1_attn_b_vconv_w, L1_attn_b_vconv_b, L1_attn_b_ln_g, L1_attn_b_ln_b, L1_ffn_w_ln1, L1_ffn_wq, L1_ffn_bq, L1_ffn_wk, L1_ffn_bk, L1_ffn_wv, L1_ffn_bv, L1_ffn_wo, L1_ffn_w_ln2, L1_ffn_w_router, L1_ffn_w_gate_e, L1_ffn_w_up_e, L1_ffn_w_down_e, L1_ffn_w_sh_gate, L1_ffn_w_sh_up, L1_ffn_w_sh_down, L1_ffn_w_sh_eg):

    def _L0_attn_a_ref(x, Wq, Wk, Wv, Wg, Wp):
        import jax, jax.numpy as jnp
        import numpy as np
        B, N, D, BS = (2, 512, 256, 32)

        def rms_norm(x):
            eps = jnp.asarray(jnp.finfo(x.dtype).eps, x.dtype)
            return x * jax.lax.rsqrt(jnp.mean(x * x, axis=-1, keepdims=True) + eps)

        def la_kernel(q, k, v, bs):
            b, n, d = q.shape
            T = n // bs
            qc = q.reshape(b, T, bs, d).transpose(1, 0, 2, 3)
            kc = k.reshape(b, T, bs, d).transpose(1, 0, 2, 3)
            vc = v.reshape(b, T, bs, d).transpose(1, 0, 2, 3)
            mask = jnp.tril(jnp.ones((bs, bs), q.dtype))

            def step(kv, qkv):
                qt, kt, vt = qkv
                s = jnp.einsum('bid,bjd->bij', qt, kt) * mask
                ot = jnp.einsum('bij,bjd->bid', s, vt) + jnp.einsum('bid,bde->bie', qt, kv)
                kv = kv + jnp.einsum('bjd,bje->bde', kt, vt)
                return (kv, ot)
            kv0 = jnp.zeros((b, d, d), q.dtype)
            _, o = jax.lax.scan(step, kv0, (qc, kc, vc))
            return o.transpose(1, 0, 2, 3).reshape(b, n, d)
        xn = rms_norm(x)
        q = jax.nn.silu(jnp.einsum('bnd,od->bno', xn, Wq))
        k = jax.nn.silu(jnp.einsum('bnd,od->bno', xn, Wk))
        v = jax.nn.silu(jnp.einsum('bnd,od->bno', xn, Wv))
        g = jax.nn.sigmoid(jnp.einsum('bnd,od->bno', xn, Wg))
        o = la_kernel(q, k, v, BS) * g
        return jnp.einsum('bnd,od->bno', o, Wp)

    def _L0_attn_b_ref(x, norm_scale, conv_w, conv_b, in_proj_w, dt_bias, head_mix, out_proj_w):
        import jax, jax.numpy as jnp
        import numpy as np
        from jax import lax
        CHUNK = 32
        ROPE_BASE = 10000.0

        def _forward(x, norm_scale, conv_w, conv_b, in_proj_w, dt_bias, head_mix, out_proj_w):
            B, N, D = x.shape
            H = head_mix.shape[0]
            Dh = D // H
            K = conv_w.shape[-1]
            residual = x
            xf = x.astype(jnp.float32)
            rms = lax.rsqrt(jnp.mean(xf * xf, -1, keepdims=True) + 1e-06)
            xn = jnp.clip(norm_scale * xf * rms, -60000.0, 60000.0).astype(x.dtype)
            xc = lax.conv_general_dilated(xn.transpose(0, 2, 1), conv_w, (1,), [(K - 1, 0)], dimension_numbers=('NCH', 'OIH', 'NCH'), feature_group_count=D)
            xc = xc + conv_b[None, :, None]
            xc = jax.nn.silu(xc.transpose(0, 2, 1))
            fused = xc @ in_proj_w.T
            dt_raw, v, gate = jnp.split(fused, 3, axis=-1)
            dt = jnp.clip(jax.nn.softplus(dt_raw.astype(jnp.float32) + dt_bias), 0.001, 2.0)
            gate = jax.nn.sigmoid(gate)
            log_alpha = -dt
            inv_freq = 1.0 / ROPE_BASE ** (jnp.arange(0, Dh, 2, dtype=jnp.float32) / Dh)
            t = jnp.arange(N, dtype=jnp.float32)
            freqs = t[:, None] * inv_freq[None, :]
            cos = jnp.cos(freqs)[None, :, None, :]
            sin = jnp.sin(freqs)[None, :, None, :]
            v4 = v.reshape(B, N, H, Dh)
            v1, v2 = (v4[..., :Dh // 2], v4[..., Dh // 2:])
            v_rot = jnp.concatenate([v1 * cos - v2 * sin, v1 * sin + v2 * cos], -1).reshape(B, N, D)
            v_in = v_rot * dt
            pad = -N % CHUNK
            if pad:
                v_in = jnp.pad(v_in, ((0, 0), (0, pad), (0, 0)))
                log_alpha = jnp.pad(log_alpha, ((0, 0), (0, pad), (0, 0)))
            NC = v_in.shape[1] // CHUNK
            vc = v_in.reshape(B, NC, CHUNK, D)
            la = log_alpha.reshape(B, NC, CHUNK, D)
            L = jnp.clip(jnp.cumsum(la, axis=2), -20.0, 0.0)
            Lmax = jnp.max(L, axis=2, keepdims=True)
            Ls = L - Lmax
            cum = jnp.cumsum(jnp.exp(-Ls) * vc, axis=2)
            chunk_out = jnp.exp(Ls) * cum
            if NC > 1:
                bd = L[:, :, -1, :]
                bo = chunk_out[:, :, -1, :]
                cd = jnp.clip(jnp.cumsum(bd, axis=1), -80.0, 0.0)
                stab = jnp.max(cd, axis=1, keepdims=True)
                ncd = jnp.clip(cd - stab, -20.0, 0.0)
                seeds = bo * jnp.exp(-ncd)
                shifted = jnp.pad(seeds[:, :-1], ((0, 0), (1, 0), (0, 0)))
                carries = jnp.cumsum(shifted, axis=1) * jnp.exp(ncd)
                final = chunk_out + carries[:, :, None, :] * jnp.exp(L)
            else:
                final = chunk_out
            final = final.astype(x.dtype).reshape(B, -1, D)[:, :N, :]
            vm = jnp.einsum('bnhd,hm->bnmd', final.reshape(B, N, H, Dh), head_mix).reshape(B, N, D)
            out = vm * gate @ out_proj_w.T
            return residual + out
        return _forward(x, norm_scale, conv_w, conv_b, in_proj_w, dt_bias, head_mix, out_proj_w)

    def _L0_ffn_ref(hidden_states, w_gate, w1, w3, w2):
        import jax, jax.numpy as jnp
        import numpy as np
        E, TOPK, H, I = (8, 2, 256, 512)
        SOFTCAP = 30.0
        orig_shape = hidden_states.shape
        x = hidden_states.reshape(-1, H)
        logits = x @ w_gate
        logits = SOFTCAP * jnp.tanh(logits / SOFTCAP)
        probs = jax.nn.softmax(logits, axis=-1)
        _, idx = jax.lax.top_k(probs, TOPK)
        mask = jax.nn.one_hot(idx, E, dtype=probs.dtype).sum(-2)
        weights = probs * mask
        out = jnp.zeros_like(x)
        for e in range(E):
            h = jax.nn.silu(x @ w1[e]) * (x @ w3[e])
            out = out + h @ w2[e] * weights[:, e:e + 1]
        return out.reshape(orig_shape)

    def _L1_attn_a_ref(x, W_qkv, b_qkv, W_out, b_out):
        import jax, jax.numpy as jnp
        import numpy as np
        HIDDEN = 256
        NUM_HEADS = 16
        HEAD_DIM = HIDDEN // NUM_HEADS
        B, S, H = x.shape
        qkv = x @ W_qkv.T + b_qkv
        q, k, v = jnp.split(qkv, 3, axis=-1)

        def to_heads(t):
            return t.reshape(B, S, NUM_HEADS, HEAD_DIM).transpose(0, 2, 1, 3)
        q, k, v = (to_heads(q), to_heads(k), to_heads(v))
        scale = HEAD_DIM ** (-0.5)
        scores = jnp.einsum('bnqd,bnkd->bnqk', q, k) * scale
        causal = jnp.triu(jnp.ones((S, S), dtype=bool), k=1)
        scores = jnp.where(causal, -jnp.inf, scores)
        attn = jax.nn.softmax(scores, axis=-1)
        out = jnp.einsum('bnqk,bnkd->bnqd', attn, v)
        out = out.transpose(0, 2, 1, 3).reshape(B, S, H)
        return out @ W_out.T + b_out

    def _L1_attn_b_ref(x, Wq, Wk, Wv, Wa, ba, Wb, bb, Wg, Wo, qconv_w, qconv_b, kconv_w, kconv_b, vconv_w, vconv_b, ln_g, ln_b):
        import jax, jax.numpy as jnp
        import numpy as np
        B, T, H, D, HID, K = (2, 64, 16, 128, 256, 4)
        SCALE = D ** (-0.5)
        LN_EPS = 1e-05

        def _dwconv_causal(x, w, b):
            xt = jnp.transpose(x, (0, 2, 1))
            out = jax.lax.conv_general_dilated(xt, w[:, None, :], window_strides=(1,), padding=[(K - 1, 0)], feature_group_count=w.shape[0])
            return jnp.transpose(out, (0, 2, 1)) + b

        def _delta_scan(q, k, v, a, beta):
            ks = k * SCALE
            xs = tuple((jnp.moveaxis(z, 1, 0) for z in (q, ks, v, a, beta)))

            def step(S, t):
                q_t, k_t, v_t, a_t, b_t = t
                y = jnp.einsum('bhvk,bhk->bhv', S, k_t)
                err = y - v_t
                S = a_t[..., None] * S - (b_t[..., None] * err)[..., None] * k_t[:, :, None, :]
                o = jnp.einsum('bhvk,bhk->bhv', S, q_t)
                return (S, o)
            S0 = jnp.zeros((q.shape[0], H, D, D), q.dtype)
            _, o = jax.lax.scan(step, S0, xs)
            return jnp.moveaxis(o, 0, 1)
        b, t, _ = x.shape
        q = jax.nn.silu(_dwconv_causal(x @ Wq, qconv_w, qconv_b)).reshape(b, t, H, D)
        k = jax.nn.silu(_dwconv_causal(x @ Wk, kconv_w, kconv_b)).reshape(b, t, H, D)
        v = jax.nn.silu(_dwconv_causal(x @ Wv, vconv_w, vconv_b)).reshape(b, t, H, D)
        a = jax.nn.sigmoid(x @ Wa + ba).reshape(b, t, H, D)
        beta = jax.nn.sigmoid(x @ Wb + bb)
        o = _delta_scan(q, k, v, a, beta)
        mu = jnp.mean(o, axis=-1, keepdims=True)
        var = jnp.mean(jnp.square(o - mu), axis=-1, keepdims=True)
        o = (o - mu) * jax.lax.rsqrt(var + LN_EPS) * ln_g + ln_b
        g = jax.nn.sigmoid(x @ Wg).reshape(b, t, H, D)
        o = (o * g).reshape(b, t, H * D)
        return o @ Wo

    def _L1_ffn_ref(x, w_ln1, wq, bq, wk, bk, wv, bv, wo, w_ln2, w_router, w_gate_e, w_up_e, w_down_e, w_sh_gate, w_sh_up, w_sh_down, w_sh_eg):
        import jax, jax.numpy as jnp
        import numpy as np
        HID = 256
        N_HEADS = 16
        N_KV = 16
        HEAD_DIM = HID // N_HEADS
        N_EXP = 8
        TOP_K = 2
        MOE_I = 176
        SH_I = 704
        EPS = 1e-06
        ROPE_THETA = 1000000.0

        def _rms(x, w):
            v = jnp.mean(jnp.square(x), axis=-1, keepdims=True)
            return x * jax.lax.rsqrt(v + EPS) * w

        def _rope(q, k):
            S, D = (q.shape[1], q.shape[-1])
            inv = 1.0 / ROPE_THETA ** (jnp.arange(0, D, 2, dtype=jnp.float32) / D)
            freqs = jnp.arange(S, dtype=jnp.float32)[:, None] * inv[None, :]
            emb = jnp.concatenate([freqs, freqs], axis=-1)
            cos = jnp.cos(emb)[None, :, None, :]
            sin = jnp.sin(emb)[None, :, None, :]

            def rot(t):
                t1, t2 = (t[..., :D // 2], t[..., D // 2:])
                return jnp.concatenate([-t2, t1], axis=-1)
            return (q * cos + rot(q) * sin, k * cos + rot(k) * sin)
        B, S, H = x.shape
        h = _rms(x, w_ln1)
        q = (h @ wq + bq).reshape(B, S, N_HEADS, HEAD_DIM)
        k = (h @ wk + bk).reshape(B, S, N_KV, HEAD_DIM)
        v = (h @ wv + bv).reshape(B, S, N_KV, HEAD_DIM)
        q, k = _rope(q, k)
        rep = N_HEADS // N_KV
        if rep > 1:
            k = jnp.repeat(k, rep, axis=2)
            v = jnp.repeat(v, rep, axis=2)
        scores = jnp.einsum('bqhd,bkhd->bhqk', q, k) * HEAD_DIM ** (-0.5)
        causal = jnp.tril(jnp.ones((S, S), bool))
        scores = jnp.where(causal[None, None], scores, jnp.finfo(scores.dtype).min)
        attn = jax.nn.softmax(scores, axis=-1)
        ctx = jnp.einsum('bhqk,bkhd->bqhd', attn, v).reshape(B, S, N_HEADS * HEAD_DIM)
        x = x + ctx @ wo
        h = _rms(x, w_ln2).reshape(B * S, H)
        logits = h @ w_router
        probs = jax.nn.softmax(logits, axis=-1)
        top_w, top_i = jax.lax.top_k(probs, TOP_K)
        combine = jnp.sum(jax.nn.one_hot(top_i, N_EXP, dtype=h.dtype) * top_w[..., None], axis=1)
        g = jnp.einsum('th,ehi->eti', h, w_gate_e)
        u = jnp.einsum('th,ehi->eti', h, w_up_e)
        y = jnp.einsum('eti,eih->eth', jax.nn.silu(g) * u, w_down_e)
        routed = jnp.einsum('eth,te->th', y, combine)
        sh = jax.nn.silu(h @ w_sh_gate) * (h @ w_sh_up) @ w_sh_down
        sh = sh * jax.nn.sigmoid(h @ w_sh_eg)
        x = x + (routed + sh).reshape(B, S, H)
        return x
    x = L0_attn_a_x
    x = x + _L0_attn_a_ref(_layernorm(x, axis=-1), L0_attn_a_Wq, L0_attn_a_Wk, L0_attn_a_Wv, L0_attn_a_Wg, L0_attn_a_Wp)
    x = x + _L0_ffn_ref(_layernorm(x, axis=-1), L0_ffn_w_gate, L0_ffn_w1, L0_ffn_w3, L0_ffn_w2)
    x = x + _L0_attn_b_ref(_layernorm(x, axis=-1), L0_attn_b_norm_scale, L0_attn_b_conv_w, L0_attn_b_conv_b, L0_attn_b_in_proj_w, L0_attn_b_dt_bias, L0_attn_b_head_mix, L0_attn_b_out_proj_w)
    x = x + _L0_ffn_ref(_layernorm(x, axis=-1), L0_ffn_w_gate, L0_ffn_w1, L0_ffn_w3, L0_ffn_w2)
    x = x + _L1_attn_a_ref(_layernorm(x, axis=-1), L1_attn_a_W_qkv, L1_attn_a_b_qkv, L1_attn_a_W_out, L1_attn_a_b_out)
    x = x + _L1_ffn_ref(_layernorm(x, axis=-1), L1_ffn_w_ln1, L1_ffn_wq, L1_ffn_bq, L1_ffn_wk, L1_ffn_bk, L1_ffn_wv, L1_ffn_bv, L1_ffn_wo, L1_ffn_w_ln2, L1_ffn_w_router, L1_ffn_w_gate_e, L1_ffn_w_up_e, L1_ffn_w_down_e, L1_ffn_w_sh_gate, L1_ffn_w_sh_up, L1_ffn_w_sh_down, L1_ffn_w_sh_eg)
    x = x + _L1_attn_b_ref(_layernorm(x, axis=-1), L1_attn_b_Wq, L1_attn_b_Wk, L1_attn_b_Wv, L1_attn_b_Wa, L1_attn_b_ba, L1_attn_b_Wb, L1_attn_b_bb, L1_attn_b_Wg, L1_attn_b_Wo, L1_attn_b_qconv_w, L1_attn_b_qconv_b, L1_attn_b_kconv_w, L1_attn_b_kconv_b, L1_attn_b_vconv_w, L1_attn_b_vconv_b, L1_attn_b_ln_g, L1_attn_b_ln_b)
    x = x + _L1_ffn_ref(_layernorm(x, axis=-1), L1_ffn_w_ln1, L1_ffn_wq, L1_ffn_bq, L1_ffn_wk, L1_ffn_bk, L1_ffn_wv, L1_ffn_bv, L1_ffn_wo, L1_ffn_w_ln2, L1_ffn_w_router, L1_ffn_w_gate_e, L1_ffn_w_up_e, L1_ffn_w_down_e, L1_ffn_w_sh_gate, L1_ffn_w_sh_up, L1_ffn_w_sh_down, L1_ffn_w_sh_eg)
    return x

_drawn_inputs = setup_inputs


def setup_inputs(seed=0):
    import zlib

    import numpy as np

    out = dict(_drawn_inputs(seed))
    spreads = {'L0_attn_b_norm_scale': (1.0, 0.6),
     'L0_attn_b_conv_b': (0.0, 0.467),
     'L1_attn_a_b_qkv': (0.0, 0.1),
     'L1_attn_a_b_out': (0.0, 0.1),
     'L1_attn_b_ba': (0.0, 0.8),
     'L1_attn_b_bb': (0.0, 0.8),
     'L1_attn_b_qconv_b': (0.0, 2.0),
     'L1_attn_b_kconv_b': (0.0, 0.61),
     'L1_attn_b_vconv_b': (0.0, 0.619),
     'L1_attn_b_ln_g': (1.0, 0.6),
     'L1_attn_b_ln_b': (0.0, 0.529),
     'L1_ffn_w_ln1': (1.0, 0.6),
     'L1_ffn_bq': (0.0, 0.8),
     'L1_ffn_bk': (0.0, 0.8),
     'L1_ffn_bv': (0.0, 0.46),
     'L1_ffn_w_ln2': (1.0, 0.6)}
    factors = {'L0_attn_b_conv_w': 4.096,
     'L0_attn_b_dt_bias': 3.535,
     'L0_attn_b_head_mix': 3.64,
     'L1_attn_b_Wq': 4.24,
     'L1_attn_b_Wk': 4.867,
     'L1_attn_b_Wv': 4.6,
     'L1_attn_b_Wa': 8.0,
     'L1_attn_b_Wb': 8.0,
     'L1_attn_b_Wg': 8.0,
     'L1_attn_b_qconv_w': 4.145,
     'L1_attn_b_kconv_w': 4.867,
     'L1_attn_b_vconv_w': 4.523,
     'L1_ffn_wq': 8.0,
     'L1_ffn_wk': 8.0,
     'L1_ffn_wv': 5.069,
     'L1_ffn_w_router': 8.0,
     'L1_ffn_w_gate_e': 8.0,
     'L1_ffn_w_up_e': 8.0,
     'L1_ffn_w_down_e': 8.0,
     'L1_ffn_w_sh_gate': 6.766,
     'L1_ffn_w_sh_up': 6.66,
     'L1_ffn_w_sh_down': 6.675,
     'L1_ffn_w_sh_eg': 8.0}
    for name, (base, spread) in spreads.items():
        noise = np.random.default_rng([zlib.crc32(name.encode()), seed]).standard_normal(out[name].shape)
        drawn = base * np.exp(spread * noise) if base else spread * noise
        out[name] = jnp.asarray(drawn.astype(out[name].dtype))
    for name, factor in factors.items():
        out[name] = (out[name] * factor).astype(out[name].dtype)
    return out
```

```python
import numpy as np
import concourse.bass as bass
from concourse import mybir
from contextlib import ExitStack

FP32 = mybir.dt.float32
BF16 = mybir.dt.bfloat16
ALU = mybir.AluOpType
ACT = mybir.ActivationFunctionType
AX = mybir.AxisListType

P = 128
B, T, D = 4, 256, 256
N = B * T
NT = N // P
KD = D // P
NB = 512
NH = N // NB
E = 8
LN_EPS = 1e-5

START, STOP = 0, 8


class Chain:

    def __init__(self, engine, sem):
        self.engine, self.sem, self.count, self.base = engine, sem, 0, 0

    def then(self, instruction):
        self.count += 1
        instruction.then_inc(self.sem, 1)
        self.engine.wait_ge(self.sem, self.base + self.count)


class Core:

    def __init__(self, nc, ctx, args):
        self.nc, self.a = nc, args
        self.stages = 0

        def sb(name, shape, dt=FP32):
            return ctx.enter_context(nc.sbuf_tensor(name, shape, dt))

        self.X = sb("X", [P, NT, D])
        self.XN = sb("XN", [P, NT, D])
        self.XT = sb("XT", [P, KD, N])
        self.ident = sb("ident", [P, P])
        self.PS = ctx.enter_context(nc.psum_tensor("PS", [P, 8, NB], FP32))
        self.pool = [ctx.enter_context(nc.semaphore(f"stage_sem{i}")) for i in range(52)]


class Stage:

    def __init__(self, core, name):
        self.core, self.nc, self.name = core, core.nc, name
        self.ctx = ExitStack()
        self.sems = []
        core.stages += 1
        self.tag = f"{name}{core.stages}"

    def sb(self, name, shape, dt=FP32):
        return self.ctx.enter_context(self.nc.sbuf_tensor(f"{name}_{self.tag}", shape, dt))

    def sem(self, name):
        s = self.core.pool[len(self.sems)]
        self.sems.append(s)
        return s

    def end(self):
        for sem in self.sems:
            self.nc.gpsimd.sem_clear(sem)
        self.nc.all_engine_barrier()
        self.ctx.close()


def setup(core):
    nc, s = core.nc, Stage(core, "setup")
    x_in, filled = s.sem("x_in"), s.sem("filled")
    with nc.Block() as block:
        @block.sync
        def _(sp):
            sp.dma_start(core.X[:], core.a["L0_attn_a_x"].rearrange("b (i p) d -> p (b i) d", p=P)).then_inc(x_in, 16)
            sp.wait_ge(x_in, 16)

        @block.gpsimd
        def _(pool):
            nc.gpsimd.memset(core.ident[:], 0.0).then_inc(filled, 1)
            pool.wait_ge(filled, 1)
            nc.gpsimd.affine_select(out=core.ident[:], in_=core.ident[:], compare_op=ALU.not_equal,
                                    fill=1.0, base=0, pattern=[[-1, P]],
                                    channel_multiplier=1).then_inc(filled, 1)
            pool.wait_ge(filled, 2)
    s.end()


def finish(core, out):
    nc, s = core.nc, Stage(core, "finish")
    stored = s.sem("stored")
    with nc.Block() as block:
        @block.sync
        def _(sp):
            sp.dma_start(out.rearrange("b (i p) d -> p (b i) d", p=P), core.X[:]).then_inc(stored, 16)
            sp.wait_ge(stored, 16)
    s.end()


def norm(core, layer=True, rms_eps=None, weight=None):
    nc, X, XN, XT, PS = core.nc, core.X, core.XN, core.XT, core.PS
    s = Stage(core, "norm")
    stats = s.sb("stats", [P, NT, 6])
    mv = s.sb("mv", [P, NT, 2])
    root = s.sb("root", [P, NT])
    rstd = s.sb("rstd", [P, NT])
    rms = s.sb("rms", [P, NT])
    eps = s.sb("eps", [P, 2])
    w = s.sb("w", [P, KD])
    H = s.sb("H", [P, NT, D]) if rms_eps is not None else XN
    w_in, sumsq, rooted, scaled, turned, moved, chain_v = (s.sem(n) for n in (
        "w_in", "sumsq", "rooted", "scaled", "turned", "moved", "chain_v"))
    src = X if layer else XN
    with nc.Block() as block:
        @block.sync
        def _(sp):
            if weight is not None:
                sp.dma_start(w[:], weight.rearrange("(k p) -> p k", p=P),
                             allow_slow_non_contiguous=True).then_inc(w_in, 16)
                sp.wait_ge(w_in, 16)

        @block.vector
        def _(dve):
            c = Chain(dve, chain_v)
            nc.vector.memset(eps[:, 0:1], LN_EPS)
            c.then(nc.vector.memset(eps[:, 1:2], rms_eps or 0.0))
            for i in range(NT):
                last = nc.vector.bn_stats(stats[:, i, :], src[:, i, :])
            c.then(last)
            for i in range(NT):
                last = nc.vector.bn_aggr(mv[:, i, :], stats[:, i, :])
            if layer:
                last.then_inc(sumsq, 1)
                dve.wait_ge(rooted, 1)
                c.then(nc.vector.reciprocal(rstd[:], root[:]))
                for i in range(NT):
                    last = nc.vector.tensor_scalar(XN[:, i, :], X[:, i, :], mv[:, i, 0:1], rstd[:, i:i + 1],
                                                   ALU.subtract, ALU.mult)
                if rms_eps is None:
                    last.then_inc(scaled, 1)
                else:
                    c.then(last)
                    c.then(nc.vector.tensor_tensor(rms[:], mv[:, :, 1], rstd[:], ALU.mult))
                    nc.vector.tensor_tensor(rms[:], rms[:], rstd[:], ALU.mult).then_inc(sumsq, 1)
            else:
                c.then(last)
                c.then(nc.vector.tensor_tensor(rms[:], mv[:, :, 0], mv[:, :, 0], ALU.mult))
                nc.vector.tensor_tensor(rms[:], rms[:], mv[:, :, 1], ALU.add).then_inc(sumsq, 1)
            if rms_eps is not None:
                dve.wait_ge(rooted, 1 + layer)
                c.then(nc.vector.reciprocal(rms[:], root[:]))
                for i in range(NT):
                    last = nc.vector.tensor_scalar(H[:, i, :], XN[:, i, :], rms[:, i:i + 1], None, ALU.mult)
                last.then_inc(scaled, 1)
            for q in range(2):
                dve.wait_ge(turned, q + 1)
                if weight is not None:
                    if q == 0:
                        dve.wait_ge(w_in, 16)
                    nc.vector.tensor_scalar(XT[:, 0, q * NB:(q + 1) * NB], PS[:, q, :], w[:, 0:1], None,
                                            ALU.mult)
                else:
                    nc.vector.tensor_copy(XT[:, 0, q * NB:(q + 1) * NB], PS[:, q, :])

        @block.scalar
        def _(act):
            if layer:
                act.wait_ge(sumsq, 1)
                nc.scalar.activation(root[:], mv[:, :, 1], ACT.Sqrt, bias=eps[:, 0:1]).then_inc(rooted, 1)
            if rms_eps is not None:
                act.wait_ge(sumsq, 1 + layer)
                nc.scalar.activation(root[:], rms[:], ACT.Sqrt, bias=eps[:, 1:2]).then_inc(rooted, 1)
            for q in range(2):
                act.wait_ge(turned, q + 3)
                if weight is not None:
                    act.wait_ge(w_in, 16)
                    nc.scalar.activation(XT[:, 1, q * NB:(q + 1) * NB], PS[:, 2 + q, :], ACT.Copy,
                                         scale=w[:, 1:2])
                else:
                    nc.scalar.copy(XT[:, 1, q * NB:(q + 1) * NB], PS[:, 2 + q, :])

        @block.tensor
        def _(pe):
            pe.wait_ge(scaled, 1)
            for k in range(KD):
                for q in range(2):
                    for i in range(4):
                        last = nc.tensor.transpose(PS[:, 2 * k + q, i * P:(i + 1) * P],
                                                   H[:, 4 * q + i, k * P:(k + 1) * P], core.ident[:])
                    last.then_inc(turned, 1)
    s.end()


def linear_attention(core):
    nc, a, X, XT, PS = core.nc, core.a, core.X, core.XT, core.PS
    s = Stage(core, "linattn")
    names = ["Wq", "Wk", "Wg", "Wv", "Wp"]
    W = s.sb("W", [P, 5, KD, D])
    FT = s.sb("FT", [P, 3, KD, N])
    V = s.sb("V", [P, NT, D])
    ST = s.sb("ST", [P, 2, 2, T])
    OT = s.sb("OT", [P, KD, N])
    w_in, mm, ev, v_mm, v_ev, s_mm, s_ev, o_mm, o_ev, y_mm, masked, y_ev = (s.sem(n) for n in (
        "w_in", "mm", "ev", "v_mm", "v_ev", "s_mm", "s_ev", "o_mm", "o_ev", "y_mm", "masked", "y_ev"))
    JOBS = [(i, m, n) for i in range(3) for m in range(KD) for n in range(NH)]
    NJ = len(JOBS)

    with nc.Block() as block:
        @block.sync
        def _(sp):
            for i, name in enumerate(names):
                sp.dma_start(W[:, i], a["L0_attn_a_" + name].rearrange("(k p) n -> p k n", p=P)).then_inc(w_in, 16)
            sp.wait_ge(w_in, 80)

        @block.tensor
        def _(pe):
            pe.wait_ge(w_in, 80)
            for g, (i, m, n) in enumerate(JOBS):
                if g >= 4:
                    pe.wait_ge(ev, g - 3)
                for k in range(KD):
                    last = nc.tensor.matmul(PS[:, g % 4, :], W[:, i, k, m * P:(m + 1) * P],
                                            XT[:, k, n * NB:(n + 1) * NB], start=(k == 0), stop=(k == KD - 1))
                last.then_inc(mm, 1)
            for i in range(NT):
                if i >= 4:
                    pe.wait_ge(v_ev, i - 3)
                for k in range(KD):
                    last = nc.tensor.matmul(PS[:, 4 + i % 4, 0:D], XT[:, k, i * P:(i + 1) * P],
                                            W[:, 3, k, :], start=(k == 0), stop=(k == KD - 1))
                last.then_inc(v_mm, 1)
            pe.wait_ge(ev, NJ)
            pe.wait_ge(v_ev, NT)

            def scores(b):
                if b >= 2:
                    pe.wait_ge(s_ev, b - 1)
                for j in range(2):
                    for k in range(KD):
                        last = nc.tensor.matmul(PS[:, b % 2, j * T + j * P:(j + 1) * T],
                                                FT[:, 1, k, b * T + j * P:b * T + (j + 1) * P],
                                                FT[:, 0, k, b * T + j * P:(b + 1) * T],
                                                start=(k == 0), stop=(k == KD - 1))
                last.then_inc(s_mm, 1)

            scores(0)
            for b in range(B):
                if b + 1 < B:
                    scores(b + 1)
                pe.wait_ge(masked, b + 1)
                if b >= 2:
                    pe.wait_ge(o_ev, b - 1)
                for m in range(KD):
                    nc.tensor.matmul(PS[:, 2 + b % 2, m * T:(m + 1) * T], V[:, 2 * b, m * P:(m + 1) * P],
                                     ST[:, b % 2, 0, :], start=True, stop=False)
                    last = nc.tensor.matmul(PS[:, 2 + b % 2, m * T + P:(m + 1) * T],
                                            V[:, 2 * b + 1, m * P:(m + 1) * P],
                                            ST[:, b % 2, 1, P:T], start=False, stop=True)
                last.then_inc(o_mm, 1)
            for i in range(NT):
                pe.wait_ge(o_ev, i // 2 + 1)
                if i >= 4:
                    pe.wait_ge(y_ev, i - 3)
                for k in range(KD):
                    last = nc.tensor.matmul(PS[:, 4 + i % 4, 0:D], OT[:, k, i * P:(i + 1) * P],
                                            W[:, 4, k, :], start=(k == 0), stop=(k == KD - 1))
                last.then_inc(y_mm, 1)

        @block.scalar
        def _(act):
            for g, (i, m, n) in enumerate(JOBS):
                act.wait_ge(mm, g + 1)
                nc.scalar.activation(FT[:, i, m, n * NB:(n + 1) * NB], PS[:, g % 4, :],
                                     ACT.Sigmoid if i == 2 else ACT.Silu).then_inc(ev, 1)
            for i in range(NT):
                act.wait_ge(v_mm, i + 1)
                nc.scalar.activation(V[:, i, :], PS[:, 4 + i % 4, 0:D], ACT.Silu).then_inc(v_ev, 1)
            for b in range(B):
                act.wait_ge(s_mm, b + 1)
                if b >= 2:
                    act.wait_ge(o_mm, b - 1)
                nc.scalar.copy(ST[:, b % 2, 0, :], PS[:, b % 2, 0:T])
                nc.scalar.copy(ST[:, b % 2, 1, P:T], PS[:, b % 2, T + P:2 * T]).then_inc(s_ev, 1)

        @block.gpsimd
        def _(pool):
            for b in range(B):
                pool.wait_ge(s_ev, b + 1)
                for j in range(2):
                    v = ST[:, b % 2, j, j * P:(j + 1) * P]
                    last = nc.gpsimd.affine_select(out=v, in_=v, compare_op=ALU.is_ge, fill=0.0, base=0,
                                                   pattern=[[1, P]], channel_multiplier=-1)
                last.then_inc(masked, 1)

        @block.vector
        def _(dve):
            for b in range(B):
                dve.wait_ge(o_mm, b + 1)
                if b == 0:
                    dve.wait_ge(ev, NJ)
                for m in range(KD):
                    last = nc.vector.tensor_tensor(OT[:, m, b * T:(b + 1) * T], PS[:, 2 + b % 2, m * T:(m + 1) * T],
                                                   FT[:, 2, m, b * T:(b + 1) * T], ALU.mult)
                last.then_inc(o_ev, 1)
            for i in range(NT):
                dve.wait_ge(y_mm, i + 1)
                nc.vector.tensor_tensor(X[:, i, :], PS[:, 4 + i % 4, 0:D], X[:, i, :],
                                        ALU.add).then_inc(y_ev, 1)
    s.end()


def top2(core, s, dve, c, p, weights, rank):
    nc = core.nc
    bc = lambda t: t[:].unsqueeze(2).broadcast_to([P, NT, E])
    m = s.top_m
    eq = s.top_eq
    oh = s.top_oh
    rest = s.top_rest
    src = p
    for r in range(2):
        c.then(nc.vector.tensor_reduce(m[:], src[:], AX.X, ALU.max))
        c.then(nc.vector.tensor_tensor(eq[:], src[:], bc(m), ALU.is_equal))
        c.then(nc.vector.tensor_tensor(eq[:], eq[:], rank[:].unsqueeze(1).broadcast_to([P, NT, E]), ALU.mult))
        c.then(nc.vector.tensor_reduce(m[:], eq[:], AX.X, ALU.max))
        c.then(nc.vector.tensor_tensor(oh[:, r], eq[:], bc(m), ALU.is_equal))
        if r == 0:
            c.then(nc.vector.scalar_tensor_tensor(rest[:], oh[:, 0], -2.0, src[:], ALU.mult, ALU.add))
            src = rest
    c.then(nc.vector.tensor_tensor(oh[:, 0], oh[:, 0], oh[:, 1], ALU.add))
    return nc.vector.tensor_tensor(weights, oh[:, 0], p[:], ALU.mult)


def moe(core, a="L0_ffn_"):
    nc, args, X, XT, PS = core.nc, core.a, core.X, core.XT, core.PS
    I = 512
    MI = I // P
    SOFTCAP = 30.0
    s = Stage(core, "moe")
    WG = s.sb("WG", [P, KD, E])
    logit = s.sb("logit", [P, NT, E])
    prob = s.sb("prob", [P, NT, E])
    weight = s.sb("weight", [P, E, NT])
    rank = s.sb("rank", [P, E])
    s.top_m = s.sb("top_m", [P, NT])
    s.top_eq = s.sb("top_eq", [P, NT, E])
    s.top_oh = s.sb("top_oh", [P, 2, NT, E])
    s.top_rest = s.sb("top_rest", [P, NT, E])
    mx = s.sb("mx", [P, NT])
    W1 = s.sb("W1", [P, 2, KD, I])
    W3 = s.sb("W3", [P, 2, KD, I])
    W2 = s.sb("W2", [P, 2, MI, D])
    SG = s.sb("SG", [P, 4, NB])
    HT = s.sb("HT", [P, 2, MI, N])
    g_in, r_mm, tanh_d, sub_d, exp_d, chain_v, route_d = (s.sem(n) for n in (
        "g_in", "r_mm", "tanh_d", "sub_d", "exp_d", "chain_v", "route_d"))
    w_in = [s.sem("w_in0"), s.sem("w_in1")]
    up_mm, silu_d, h_d, dn_mm, dn_d = (s.sem(n) for n in ("up_mm", "silu_d", "h_d", "dn_mm", "dn_d"))
    G = NH * MI

    with nc.Block() as block:
        @block.sync
        def _(sp):
            sp.dma_start(WG[:], args[a + "w_gate"].rearrange("(k p) e -> p k e", p=P)).then_inc(g_in, 16)

            def load(e, r):
                one = lambda w: args[a + w][bass.ds(e, 1)]
                sp.dma_start(W1[:, r], one("w1").rearrange("o (k p) n -> p (o k) n", p=P)).then_inc(w_in[r], 16)
                sp.dma_start(W3[:, r], one("w3").rearrange("o (k p) n -> p (o k) n", p=P)).then_inc(w_in[r], 16)
                sp.dma_start(W2[:, r], one("w2").rearrange("o (k p) n -> p (o k) n", p=P)).then_inc(w_in[r], 16)

            load(0, 0)
            load(1, 1)
            with sp.Fori(1, E // 2) as j:
                for r in range(2):
                    sp.wait_ge(dn_mm, NT * (2 * j + r) - NT)
                    load(2 * j + r, r)
            sp.wait_ge(g_in, 16)
            for r in range(2):
                sp.wait_ge(w_in[r], 48 * (E // 2))

        @block.tensor
        def _(pe):
            pe.wait_ge(g_in, 16)
            for i in range(NT):
                for k in range(KD):
                    last = nc.tensor.matmul(PS[:, 7, i * E:(i + 1) * E], XT[:, k, i * P:(i + 1) * P],
                                            WG[:, k, :], start=(k == 0), stop=(k == KD - 1))
            last.then_inc(r_mm, 1)
            pe.wait_ge(tanh_d, 1)

            def expert(j, r, first):
                pe.wait_ge(w_in[r], 48 * j + 48)
                for n in range(NH):
                    for m in range(MI):
                        g = n * MI + m
                        if not (first and g < 2):
                            pe.wait_ge(h_d, (2 * j + r) * G + g - 1)
                        for q, w in enumerate((W1, W3)):
                            for k in range(KD):
                                last = nc.tensor.matmul(PS[:, 2 * (g % 2) + q, :], w[:, r, k, m * P:(m + 1) * P],
                                                        XT[:, k, n * NB:(n + 1) * NB],
                                                        start=(k == 0), stop=(k == KD - 1))
                        last.then_inc(up_mm, 1)
                for i in range(NT):
                    if i % 4 == 0:
                        pe.wait_ge(h_d, (2 * j + r) * G + MI * (i // 4 + 1))
                    if not (first and i < 4):
                        pe.wait_ge(dn_d, (2 * j + r) * NT + i - 3)
                    for k in range(MI):
                        last = nc.tensor.matmul(PS[:, 4 + i % 4, 0:D], HT[:, r, k, i * P:(i + 1) * P],
                                                W2[:, r, k, :], start=(k == 0), stop=(k == MI - 1))
                    last.then_inc(dn_mm, 1)

            expert(0, 0, True)
            expert(0, 1, False)
            with pe.Fori(1, E // 2) as j:
                expert(j, 0, False)
                expert(j, 1, False)

        @block.scalar
        def _(act):
            act.wait_ge(r_mm, 1)
            nc.scalar.activation(logit[:], PS[:, 7, 0:NT * E].rearrange("p (i e) -> p i e", e=E), ACT.Tanh,
                                 scale=1.0 / SOFTCAP).then_inc(tanh_d, 1)
            act.wait_ge(sub_d, 1)
            nc.scalar.activation(prob[:], logit[:], ACT.Exp, scale=SOFTCAP).then_inc(exp_d, 1)

            def expert(j, r, first):
                for g in range(G):
                    act.wait_ge(up_mm, (2 * j + r) * G + g + 1)
                    if not (first and g < 4):
                        act.wait_ge(h_d, (2 * j + r) * G + g - 3)
                    nc.scalar.activation(SG[:, g % 4, :], PS[:, 2 * (g % 2), :], ACT.Silu).then_inc(silu_d, 1)

            expert(0, 0, True)
            expert(0, 1, False)
            with act.Fori(1, E // 2) as j:
                expert(j, 0, False)
                expert(j, 1, False)

        @block.vector
        def _(dve):
            c = Chain(dve, chain_v)
            for e in range(E):
                last = nc.vector.memset(rank[:, e:e + 1], float(E - e))
            c.then(last)
            dve.wait_ge(tanh_d, 1)
            c.then(nc.vector.tensor_reduce(mx[:], logit[:], AX.X, ALU.max))
            nc.vector.tensor_tensor(logit[:], logit[:], mx[:].unsqueeze(2).broadcast_to([P, NT, E]),
                                    ALU.subtract).then_inc(sub_d, 1)
            dve.wait_ge(exp_d, 1)
            c.then(nc.vector.tensor_reduce(mx[:], prob[:], AX.X, ALU.add))
            c.then(nc.vector.reciprocal(mx[:], mx[:]))
            c.then(nc.vector.tensor_tensor(prob[:], prob[:], mx[:].unsqueeze(2).broadcast_to([P, NT, E]), ALU.mult))
            c.then(top2(core, s, dve, c, prob, weight[:].rearrange("p e i -> p i e"), rank))

            def expert(j, r, first):
                for g in range(G):
                    n, m = g // MI, g % MI
                    dve.wait_ge(silu_d, (2 * j + r) * G + g + 1)
                    nc.vector.tensor_tensor(HT[:, r, m, n * NB:(n + 1) * NB], SG[:, g % 4, :],
                                            PS[:, 2 * (g % 2) + 1, :], ALU.mult).then_inc(h_d, 1)
                for i in range(NT):
                    dve.wait_ge(dn_mm, (2 * j + r) * NT + i + 1)
                    nc.vector.scalar_tensor_tensor(X[:, i, :], PS[:, 4 + i % 4, 0:D],
                                                   weight[:, bass.ds(2 * j + r, 1), i], X[:, i, :],
                                                   ALU.mult, ALU.add).then_inc(dn_d, 1)

            expert(0, 0, True)
            expert(0, 1, False)
            with dve.Fori(1, E // 2) as j:
                expert(j, 0, False)
                expert(j, 1, False)
    s.end()


def conv_scan(core):
    nc, a, X, XN, XT, PS = core.nc, core.a, core.X, core.XN, core.XT, core.PS
    TAPS = 4
    CH = 32
    HD = 16
    HEADS = D // HD
    C = T // CH
    ROWS = KD * B
    s = Stage(core, "cscan")
    flat = lambda t: t[:].rearrange("p k n -> p (k n)")
    chunks = lambda t: t[:].rearrange("p k (b c j) -> p (k b c) j", b=B, j=CH)
    XP = s.sb("XP", [P, KD, B, T + TAPS - 1])
    XC = s.sb("XC", [P, KD, N])
    CW = s.sb("CW", [P, KD, TAPS])
    CB = s.sb("CB", [P, KD])
    DB = s.sb("DB", [P, KD])
    IP = s.sb("IP", [P, KD, 4 * D])
    OP = s.sb("OP", [P, KD, D])
    HM = s.sb("HM", [P, KD, HEADS])
    IM = s.sb("IM", [P, HD])
    KM = s.sb("KM", [P, KD, D])
    TRIG = s.sb("TRIG", [P, 2, T])
    ONE = s.sb("ONE", [P, 1])
    KEEP = s.sb("KEEP", [P, KD * N])
    KEEPC = s.sb("KEEPC", [P, ROWS * C])
    A1 = s.sb("A1", [P, KD, N])
    A2 = s.sb("A2", [P, KD, N])
    DT = s.sb("DT", [P, KD, N])
    VR = s.sb("VR", [P, KD, N])
    GT = s.sb("GT", [P, KD, N])
    VS = s.sb("VS", [P, 2, NB])
    CK = s.sb("CK", [P, 8, ROWS, C])
    w_in, c_in, ready, conv_d, xc_d, mm, dt_ev, rot_v, rot_s, g_ev, sp1, dt_d, clip_d, exp_d, cexp, fin, mix_mm, mix_d, y_mm, y_ev, chain_v, chain_p, swap_d, res_d = (
        s.sem(n) for n in (
            "w_in", "c_in", "ready", "conv_d", "xc_d", "mm", "dt_ev", "rot_v", "rot_s", "g_ev", "sp1", "dt_d", "clip_d",
            "exp_d", "cexp", "fin", "mix_mm", "mix_d", "y_mm", "y_ev", "chain_v", "chain_p", "swap_d", "res_d"))
    JOBS = [(0, m, n) for m in range(KD) for n in range(NH)] + \
           [(i, m, n) for m in range(KD) for n in range(NH) for i in (1, 3)] + \
           [(2, m, n) for m in range(KD) for n in range(NH)]
    TILES = KD * NH
    GBANK = lambda g: 4 + g % 4 if g >= 3 * TILES else g % 4
    CUM = s.sb("CUM", [P, KD, N])

    with nc.Block() as block:
        @block.sync
        def _(sp):
            col = lambda t: t.rearrange("(k p) -> p k", p=P)
            pre = "L0_attn_b_"
            sp.dma_start(CW[:], a[pre + "conv_w"].rearrange("(k p) o t -> p k (o t)", p=P)).then_inc(c_in, 16)
            sp.dma_start(CB[:], col(a[pre + "conv_b"]), allow_slow_non_contiguous=True).then_inc(c_in, 16)
            sp.dma_start(DB[:], col(a[pre + "dt_bias"]), allow_slow_non_contiguous=True).then_inc(c_in, 16)
            sp.dma_start(IP[:, :, 0:3 * D], a[pre + "in_proj_w"].rearrange("(k p) n -> p k n", p=P)).then_inc(w_in, 16)
            sp.dma_start(OP[:], a[pre + "out_proj_w"].rearrange("(k p) n -> p k n", p=P)).then_inc(w_in, 16)
            sp.dma_start(HM[:], a["L0_attn_b_head_rows"].rearrange("(k p) n -> p k n", p=P)).then_inc(w_in, 16)
            sp.dma_start(TRIG[:], a["trig0"].rearrange("c p t -> p c t")).then_inc(w_in, 16)
            sp.wait_ge(w_in, 64)
            sp.wait_ge(c_in, 48)

        @block.gpsimd
        def _(pool):
            c = Chain(pool, chain_p)
            nc.gpsimd.memset(XP[:, :, :, 0:TAPS - 1], 0.0).then_inc(ready, 1)
            c.then(nc.gpsimd.memset(KEEP[:], 1.0))
            c.then(nc.gpsimd.memset(KEEPC[:], 1.0))
            nc.gpsimd.memset(KEEP[:].rearrange("p (c j) -> p c j", j=CH)[:, :, 0:1], 0.0)
            nc.gpsimd.memset(KEEPC[:].rearrange("p (c j) -> p c j", j=C)[:, :, 0:1], 0.0)
            c.then(nc.gpsimd.memset(ONE[:], 1.0))
            pool.wait_ge(w_in, 64)
            for k in range(KD):
                v = IP[:, k, D:2 * D].rearrange("p (h a d) -> p h a d", a=2, d=HD // 2)
                w = IP[:, k, 3 * D:4 * D].rearrange("p (h a d) -> p h a d", a=2, d=HD // 2)
                nc.gpsimd.tensor_copy(w[:, :, 0], v[:, :, 1])
                last = nc.gpsimd.tensor_copy(w[:, :, 1], v[:, :, 0])
            last.then_inc(swap_d, 1)
            nc.gpsimd.tensor_tensor(X[:], X[:], XN[:], ALU.add).then_inc(res_d, 1)

        @block.vector
        def _(dve):
            c = Chain(dve, chain_v)
            c.then(nc.vector.tensor_scalar(XP[:, :, :, TAPS - 1:].rearrange("p k b t -> p (k b) t"),
                                           XT[:].rearrange("p k (b t) -> p (k b) t", b=B), 60000.0, -60000.0,
                                           ALU.min, ALU.max))
            dve.wait_ge(ready, 1)
            dve.wait_ge(c_in, 48)
            acc = A1
            for tau in range(TAPS):
                for k in range(KD):
                    x = XP[:, k, :, tau:tau + T]
                    o = acc[:, k, :].rearrange("p (b t) -> p b t", b=B)
                    if tau == 0:
                        last = nc.vector.tensor_scalar(o, x, CW[:, k, 0:1], None, ALU.mult)
                    else:
                        last = nc.vector.scalar_tensor_tensor(o, x, CW[:, k, tau:tau + 1], o, ALU.mult, ALU.add)
                    if tau == TAPS - 1:
                        last.then_inc(conv_d, 1)
                if tau < TAPS - 1:
                    c.then(last)
            c.then(nc.vector.tensor_reduce(IM[:], core.ident[:].rearrange("p (h d) -> p d h", d=HD), AX.X, ALU.add))
            dve.wait_ge(w_in, 64)
            for k in range(KD):
                c.then(nc.vector.tensor_tensor(KM[:, k].rearrange("p (m d) -> p m d", d=HD),
                                               HM[:, k].unsqueeze(2).broadcast_to([P, HEADS, HD]),
                                               IM[:].unsqueeze(1).broadcast_to([P, HEADS, HD]), ALU.mult))
            trig = lambda q: TRIG[:, q].unsqueeze(1).broadcast_to([P, NB // T, T])
            two = lambda t: t.rearrange("p (b t) -> p b t", t=T)
            for g, (i, m, n) in enumerate(JOBS):
                if i == 1:
                    dve.wait_ge(mm, g + 1)
                    nc.vector.tensor_tensor(two(VR[:, m, n * NB:(n + 1) * NB]), two(PS[:, g % 4, :]), trig(0),
                                            ALU.mult).then_inc(rot_v, 1)
                if i == 3:
                    dve.wait_ge(mm, g + 1)
                    r = (g - TILES) // 2 % 2
                    c.then(nc.vector.tensor_tensor(two(VS[:, r]), two(PS[:, g % 4, :]), trig(1), ALU.mult))
                    o = VR[:, m, n * NB:(n + 1) * NB]
                    nc.vector.tensor_tensor(o, o, VS[:, r], ALU.add).then_inc(rot_s, 1)
            dve.wait_ge(sp1, 2)
            c.then(nc.vector.tensor_tensor(flat(DT), flat(A1), flat(A2), ALU.add))
            c.then(nc.vector.tensor_scalar(flat(DT), flat(DT), 1e-3, 2.0, ALU.max, ALU.min))
            c.then(nc.vector.tensor_tensor_scan(flat(A1), KEEP[:], flat(DT), 0.0, ALU.mult, ALU.add))
            c.then(nc.vector.tensor_scalar(flat(A1), flat(A1), 20.0, 0.0, ALU.min, ALU.max))
            nc.vector.tensor_tensor(chunks(A2), chunks(A1), chunks(A1)[:, :, 0:1].broadcast_to([P, ROWS * C, CH]),
                                    ALU.subtract).then_inc(clip_d, 1)
            nc.vector.tensor_tensor(flat(VR), flat(VR), flat(DT), ALU.mult).then_inc(dt_d, 1)
            dve.wait_ge(dt_d, 1)
            ck = lambda q: CK[:, q].rearrange("p r c -> p (r c)")
            c.then(nc.vector.tensor_copy(ck(2), chunks(A1)[:, :, CH - 1]))
            c.then(nc.vector.tensor_tensor_scan(ck(0), KEEPC[:], ck(2), 0.0, ALU.mult, ALU.add))
            c.then(nc.vector.tensor_scalar(ck(0), ck(0), 80.0, 0.0, ALU.min, ALU.max))
            c.then(nc.vector.tensor_tensor(CK[:, 1], CK[:, 0], CK[:, 0, :, 0:1].broadcast_to([P, ROWS, C]), ALU.subtract))
            nc.vector.tensor_scalar(ck(1), ck(1), 0.0, 20.0, ALU.max, ALU.min).then_inc(clip_d, 1)
            dve.wait_ge(exp_d, 1)
            c.then(nc.vector.tensor_tensor(flat(VR), flat(VR), flat(DT), ALU.mult))
            c.then(nc.vector.tensor_tensor_scan(flat(CUM), KEEP[:], flat(VR), 0.0, ALU.mult, ALU.add))
            dve.wait_ge(exp_d, 2)
            c.then(nc.vector.tensor_tensor(flat(VR), flat(CUM), flat(A2), ALU.mult))
            dve.wait_ge(cexp, 2)
            c.then(nc.vector.tensor_tensor(ck(5), chunks(VR)[:, :, CH - 1], ck(3), ALU.mult))
            c.then(nc.vector.memset(CK[:, 6, :, 0:1], 0.0))
            c.then(nc.vector.tensor_copy(CK[:, 6, :, 1:C], CK[:, 5, :, 0:C - 1]))
            c.then(nc.vector.tensor_tensor_scan(ck(7), KEEPC[:], ck(6), 0.0, ALU.mult, ALU.add))
            c.then(nc.vector.tensor_tensor(ck(7), ck(7), ck(4), ALU.mult))
            dve.wait_ge(exp_d, 3)
            c.then(nc.vector.tensor_tensor(chunks(A1), chunks(A1), ck(7).unsqueeze(2).broadcast_to([P, ROWS * C, CH]),
                                           ALU.mult))
            nc.vector.tensor_tensor(flat(VR), flat(VR), flat(A1), ALU.add).then_inc(fin, 1)
            dve.wait_ge(g_ev, TILES)
            for g in range(TILES):
                m, n = g // NH, g % NH
                dve.wait_ge(mix_mm, g + 1)
                o = GT[:, m, n * NB:(n + 1) * NB]
                nc.vector.tensor_tensor(o, PS[:, g % 4, :], o, ALU.mult).then_inc(mix_d, 1)
            dve.wait_ge(res_d, 1)
            for i in range(NT):
                dve.wait_ge(y_mm, i + 1)
                nc.vector.tensor_tensor(X[:, i, :], PS[:, 4 + i % 4, 0:D], X[:, i, :],
                                        ALU.add).then_inc(y_ev, 1)

        @block.scalar
        def _(act):
            act.wait_ge(c_in, 48)
            for k in range(KD):
                act.wait_ge(conv_d, k + 1)
                nc.scalar.activation(XC[:, k, :], A1[:, k, :], ACT.Silu, bias=CB[:, k:k + 1]).then_inc(xc_d, 1)
            act.wait_ge(xc_d, KD)
            for g, (i, m, n) in enumerate(JOBS[:TILES]):
                act.wait_ge(mm, g + 1)
                cols = slice(n * NB, (n + 1) * NB)
                nc.scalar.activation(A2[:, m, cols], PS[:, g % 4, :], ACT.Abs, bias=DB[:, m:m + 1])
                nc.scalar.activation(A1[:, m, cols], PS[:, g % 4, :], ACT.Relu, bias=DB[:, m:m + 1]).then_inc(dt_ev, 1)
            act.wait_ge(dt_ev, TILES)
            nc.scalar.activation(flat(A2), flat(A2), ACT.Exp, scale=-1.0).then_inc(sp1, 1)
            act.wait_ge(chain_p, 3)
            act.wait_ge(sp1, 1)
            nc.scalar.activation(flat(A2), flat(A2), ACT.Ln, bias=ONE[:]).then_inc(sp1, 1)
            act.wait_ge(clip_d, 1)
            act.wait_ge(dt_d, 1)
            nc.scalar.activation(flat(DT), flat(A2), ACT.Exp).then_inc(exp_d, 1)
            act.wait_ge(exp_d, 1)
            nc.scalar.activation(flat(A2), flat(A2), ACT.Exp, scale=-1.0).then_inc(exp_d, 1)
            act.wait_ge(clip_d, 2)
            nc.scalar.activation(CK[:, 3], CK[:, 1], ACT.Exp).then_inc(cexp, 1)
            nc.scalar.activation(CK[:, 4], CK[:, 1], ACT.Exp, scale=-1.0).then_inc(cexp, 1)
            nc.scalar.activation(flat(A1), flat(A1), ACT.Exp, scale=-1.0).then_inc(exp_d, 1)
            for g, (i, m, n) in list(enumerate(JOBS))[3 * TILES:]:
                act.wait_ge(mm, g + 1)
                nc.scalar.activation(GT[:, m, n * NB:(n + 1) * NB], PS[:, GBANK(g), :], ACT.Sigmoid).then_inc(g_ev, 1)

        @block.tensor
        def _(pe):
            pe.wait_ge(w_in, 64)
            pe.wait_ge(xc_d, KD)
            for g, (i, m, n) in enumerate(JOBS):
                if 4 <= g < 3 * TILES:
                    old = g - 4
                    if old < TILES:
                        pe.wait_ge(dt_ev, old + 1)
                    elif JOBS[old][0] == 1:
                        pe.wait_ge(rot_v, (old - TILES) // 2 + 1)
                    else:
                        pe.wait_ge(rot_s, (old - TILES) // 2 + 1)
                if i == 3:
                    pe.wait_ge(swap_d, 1)
                for k in range(KD):
                    last = nc.tensor.matmul(PS[:, GBANK(g), :], IP[:, k, i * D + m * P:i * D + (m + 1) * P],
                                            XC[:, k, n * NB:(n + 1) * NB], start=(k == 0), stop=(k == KD - 1))
                last.then_inc(mm, 1)
            pe.wait_ge(fin, 1)
            for g in range(TILES):
                m, n = g // NH, g % NH
                for k in range(KD):
                    last = nc.tensor.matmul(PS[:, g % 4, :], KM[:, k, m * P:(m + 1) * P],
                                            VR[:, k, n * NB:(n + 1) * NB], start=(k == 0), stop=(k == KD - 1))
                last.then_inc(mix_mm, 1)
            pe.wait_ge(mix_d, TILES)
            pe.wait_ge(g_ev, TILES)
            for i in range(NT):
                if i >= 4:
                    pe.wait_ge(y_ev, i - 3)
                for k in range(KD):
                    last = nc.tensor.matmul(PS[:, 4 + i % 4, 0:D], GT[:, k, i * P:(i + 1) * P],
                                            OP[:, k, :], start=(k == 0), stop=(k == KD - 1))
                last.then_inc(y_mm, 1)
    s.end()


def softmax_attention(core, q, k, v, bq, bk, bv, wo, bo, rope, swapped, dst):
    nc, XT, PS = core.nc, core.XT, core.PS
    HD = 16
    HEADS = D // HD
    HK = HEADS // KD
    s = Stage(core, "attn")
    W = s.sb("W", [P, 4, KD, D])
    WS = s.sb("WS", [P, 2, KD, D])
    BC = s.sb("BC", [P, 2, KD])
    BS = s.sb("BS", [P, 2, KD])
    BV = s.sb("BV", [P, 2, D])
    TRIG = s.sb("TRIG", [P, 2, T])
    QK = s.sb("QK", [P, 2, KD, N])
    RS = s.sb("RS", [P, 2, NB])
    HMASK = s.sb("HMASK", [P, HK])
    KM = s.sb("KM", [P, KD, HK, N])
    V = s.sb("V", [P, NT, HEADS, HD + 1])
    LOW = s.sb("LOW", [P, 4, P], BF16)
    IB = s.sb("IB", [P, P], BF16)
    NM = s.sb("NM", [P, 4, 4])
    PR = s.sb("PR", [P, 4, NB])
    PT = s.sb("PT", [P, 4, NB])
    REC = s.sb("REC", [P, 2, HEADS])
    ON = s.sb("ON", [P, NT, HEADS, HD])
    OT = s.sb("OT", [P, KD, N])
    w_in, b_in, consts, mm, ev, rot, km_d, v_mm, v_ev, s_mm, max_d, exp_d, t_mm, t_ev, o_mm, o_ev, ot_mm, ot_ev, y_mm, y_ev, chain_v, chain_p, swap_d, bo_d, rs_d = (
        s.sem(n) for n in (
            "w_in", "b_in", "consts", "mm", "ev", "rot", "km_d", "v_mm", "v_ev", "s_mm", "max_d", "exp_d", "t_mm", "t_ev",
            "o_mm", "o_ev", "ot_mm", "ot_ev", "y_mm", "y_ev", "chain_v", "chain_p", "swap_d", "bo_d", "rs_d"))
    COPIES = 2 if rope is not None else 1
    JOBS = [(i, m, n, c) for i in range(2) for m in range(KD) for n in range(NH) for c in range(COPIES)]
    NJ = len(JOBS)
    UNITS = []
    for b in range(B):
        for qt in range(2):
            per = 4 if qt == 0 else 2
            for kt in range(KD):
                for h in range(0, HK, per):
                    UNITS.append((b, qt, kt, h, per))
    NU = len(UNITS)
    W_IN = 16 * (4 + (rope is not None))
    B_IN = 16 * (3 + (bo is not None) + 2 * (rope is not None))
    k_ready = rot if rope is not None else ev
    k_count = lambda kk: NH * KD + NH * (kk + 1)
    km_pool = s.sem("km_pool")
    last_unit = {2 * b + qt: u for u, (b, qt, kt, h, per) in enumerate(UNITS)}
    first_unit = {}
    for u, (b, qt, kt, h, per) in enumerate(UNITS):
        first_unit.setdefault(2 * b + qt, u)

    with nc.Block() as block:
        @block.sync
        def _(sp):
            for i, w in enumerate((q, k, v, wo)):
                sp.dma_start(W[:, i], w.rearrange("(k p) n -> p k n", p=P)).then_inc(w_in, 16)
            if rope is not None:
                sp.dma_start(TRIG[:], rope.rearrange("c p t -> p c t")).then_inc(w_in, 16)
                for i, t in enumerate(swapped):
                    sp.dma_start(BS[:, i], t.rearrange("(k p) -> p k", p=P),
                                 allow_slow_non_contiguous=True).then_inc(b_in, 16)
            for i, t in enumerate((bq, bk)):
                sp.dma_start(BC[:, i], t.rearrange("(k p) -> p k", p=P),
                             allow_slow_non_contiguous=True).then_inc(b_in, 16)
            row = lambda t: t.rearrange("(o n) -> o n", o=1).broadcast_to([P, D])
            sp.dma_start(BV[:, 0], row(bv)).then_inc(b_in, 16)
            if bo is not None:
                sp.dma_start(BV[:, 1], row(bo)).then_inc(b_in, 16)
            sp.wait_ge(w_in, W_IN)
            sp.wait_ge(b_in, B_IN)

        @block.gpsimd
        def _(pool):
            c = Chain(pool, chain_p)
            c.then(nc.gpsimd.memset(LOW[:], 0.0))
            nc.gpsimd.memset(V[:, :, :, HD:], 1.0).then_inc(consts, 1)
            c.then(nc.gpsimd.tensor_copy(IB[:], core.ident[:]))
            c.then(nc.gpsimd.affine_select(out=LOW[:], in_=LOW[:], compare_op=ALU.is_ge, fill=-1e30, base=0,
                                           pattern=[[0, 4], [-1, P]], channel_multiplier=1))
            nc.gpsimd.memset(NM[:], 0.0).then_inc(consts, 1)
            if rope is not None:
                pool.wait_ge(w_in, W_IN)
                for i in range(2):
                    for kk in range(KD):
                        x = W[:, i, kk].rearrange("p (h a d) -> p h a d", a=2, d=HD // 2)
                        y = WS[:, i, kk].rearrange("p (h a d) -> p h a d", a=2, d=HD // 2)
                        nc.gpsimd.tensor_copy(y[:, :, 0], x[:, :, 1])
                        last = nc.gpsimd.tensor_copy(y[:, :, 1], x[:, :, 0])
                last.then_inc(swap_d, 1)
            if bo is not None:
                pool.wait_ge(b_in, B_IN)
                nc.gpsimd.tensor_tensor(dst[:], dst[:], BV[:, 1].unsqueeze(1).broadcast_to([P, NT, D]),
                                        ALU.add).then_inc(bo_d, 1)
            pool.wait_ge(km_d, 1)
            for kk in range(KD):
                pool.wait_ge(k_ready, k_count(kk))
                for h in range(0, 2):
                    last = nc.gpsimd.tensor_scalar(KM[:, kk, h], QK[:, 1, kk], HMASK[:, h:h + 1], None, ALU.mult)
                last.then_inc(km_pool, 1)

        @block.tensor
        def _(pe):
            pe.wait_ge(w_in, W_IN)
            for g, (i, m, n, cp) in enumerate(JOBS):
                if cp == 1 and g == 1:
                    pe.wait_ge(swap_d, 1)
                if g >= 4:
                    pe.wait_ge(ev, g - 3)
                w = WS if cp else W
                for kk in range(KD):
                    last = nc.tensor.matmul(PS[:, g % 4, :], w[:, i, kk, m * P:(m + 1) * P],
                                            XT[:, kk, n * NB:(n + 1) * NB], start=(kk == 0), stop=(kk == KD - 1))
                last.then_inc(mm, 1)
            for i in range(NT):
                if i >= 4:
                    pe.wait_ge(v_ev, i - 3)
                for kk in range(KD):
                    last = nc.tensor.matmul(PS[:, 4 + i % 4, 0:D], XT[:, kk, i * P:(i + 1) * P],
                                            W[:, 2, kk, :], start=(kk == 0), stop=(kk == KD - 1))
                last.then_inc(v_mm, 1)
            pe.wait_ge(ev, NJ)
            pe.wait_ge(v_ev, NT)
            pe.wait_ge(km_d, 3)
            pe.wait_ge(km_pool, KD)
            pe.wait_ge(chain_p, 3)

            def scores(u):
                b, qt, kt, h, per = UNITS[u]
                bank = PS[:, u % 3, :]
                if u >= 3:
                    pe.wait_ge(exp_d, u - 2)
                keys = (qt + 1) * P
                nc.tensor.matmul(bank, QK[:, 0, kt, b * T + qt * P:b * T + (qt + 1) * P],
                                 KM[:, kt, h:h + per, b * T:b * T + keys], start=True, stop=False)
                last = nc.tensor.matmul(bank.rearrange("p (h j) -> p h j", h=per)[:, :, qt * P:keys],
                                        IB[:], LOW[:, 0:per, :], start=False, stop=True)
                last.then_inc(s_mm, 1)

            def turn(u):
                pe.wait_ge(exp_d, u + 1)
                if u >= 2:
                    pe.wait_ge(t_ev, u - 1)
                for i in range(4):
                    last = nc.tensor.transpose(PS[:, 3 + u % 2, i * P:(i + 1) * P],
                                               PR[:, u % 4, i * P:(i + 1) * P], core.ident[:])
                last.then_inc(t_mm, 1)

            def values(u):
                b, qt, kt, h, per = UNITS[u]
                i = 2 * b + qt
                pe.wait_ge(t_ev, u + 1)
                if i >= 2 and u == first_unit[i]:
                    pe.wait_ge(o_ev, i - 1)
                for j in range(per):
                    o = PS[:, 5 + i % 2, (kt * HK + h + j) * (HD + 1):(kt * HK + h + j + 1) * (HD + 1)]
                    for t in range(qt + 1):
                        last = nc.tensor.matmul(o, PT[:, u % 4, (j * (qt + 1) + t) * P:(j * (qt + 1) + t + 1) * P],
                                                V[:, 2 * b + t, kt * HK + h + j, :], start=(t == 0), stop=(t == qt))
                last.then_inc(o_mm, 1)

            scores(0)
            scores(1)
            for u in range(NU):
                if u + 2 < NU:
                    scores(u + 2)
                turn(u)
                if u >= 1:
                    values(u - 1)
            values(NU - 1)
            pe.wait_ge(o_ev, NT)
            for kk in range(KD):
                for n in range(NH):
                    for i in range(4):
                        last = nc.tensor.transpose(PS[:, 2 * kk + n, i * P:(i + 1) * P],
                                                   ON[:, 4 * n + i].rearrange("p h d -> p (h d)")[:, kk * P:(kk + 1) * P],
                                                   core.ident[:])
                    last.then_inc(ot_mm, 1)
            pe.wait_ge(ot_ev, KD * NH)
            for i in range(NT):
                if i >= 4:
                    pe.wait_ge(y_ev, i - 3)
                for kk in range(KD):
                    last = nc.tensor.matmul(PS[:, 4 + i % 4, 0:D], OT[:, kk, i * P:(i + 1) * P],
                                            W[:, 3, kk, :], start=(kk == 0), stop=(kk == KD - 1))
                last.then_inc(y_mm, 1)

        @block.scalar
        def _(act):
            if rope is None:
                act.wait_ge(b_in, B_IN)
                for g, (i, m, n, cp) in enumerate(JOBS):
                    act.wait_ge(mm, g + 1)
                    nc.scalar.activation(QK[:, i, m, n * NB:(n + 1) * NB], PS[:, g % 4, :], ACT.Identity,
                                         bias=BC[:, i, m:m + 1]).then_inc(ev, 1)
            act.wait_ge(km_d, 1)
            for kk in range(KD):
                act.wait_ge(k_ready, k_count(kk))
                for h in range(2, 4):
                    last = nc.scalar.activation(KM[:, kk, h], QK[:, 1, kk], ACT.Copy, scale=HMASK[:, h:h + 1])
            last.then_inc(km_d, 1)
            for u, (b, qt, kt, h, per) in enumerate(UNITS):
                act.wait_ge(max_d, u + 1)
                if u >= 4:
                    act.wait_ge(t_mm, u - 3)
                w = NB // per
                for j in range(per):
                    last = nc.scalar.activation(PR[:, u % 4, j * w:(j + 1) * w], PS[:, u % 3, j * w:(j + 1) * w],
                                                ACT.Exp, bias=NM[:, u % 4, j:j + 1])
                last.then_inc(exp_d, 1)

        @block.vector
        def _(dve):
            c = Chain(dve, chain_v)
            c.then(nc.vector.tensor_reduce(HMASK[:], core.ident[:].rearrange("p (h d) -> p h d", d=HD), AX.X, ALU.add))
            nc.vector.tensor_scalar(HMASK[:], HMASK[:], float(HD) ** -0.5, None, ALU.mult).then_inc(km_d, 1)
            if rope is not None:
                dve.wait_ge(w_in, W_IN)
                dve.wait_ge(b_in, B_IN)
                two = lambda t: t.rearrange("p (b t) -> p b t", t=T)
                trig = lambda x: TRIG[:, x].unsqueeze(1).broadcast_to([P, NB // T, T])
                for g, (i, m, n, cp) in enumerate(JOBS):
                    dve.wait_ge(mm, g + 1)
                    o = QK[:, i, m, n * NB:(n + 1) * NB]
                    if cp == 0:
                        nc.vector.scalar_tensor_tensor(two(o), two(PS[:, g % 4, :]), BC[:, i, m:m + 1], trig(0),
                                                       ALU.add, ALU.mult).then_inc(ev, 1)
                    else:
                        r = g // 2 % 2
                        nc.vector.scalar_tensor_tensor(two(RS[:, r]), two(PS[:, g % 4, :]), BS[:, i, m:m + 1], trig(1),
                                                       ALU.add, ALU.mult).then_inc(ev, 1)
                        dve.wait_ge(ev, g + 1)
                        nc.vector.tensor_tensor(o, o, RS[:, r], ALU.add).then_inc(rot, 1)
            else:
                dve.wait_ge(b_in, B_IN)
            for i in range(NT):
                dve.wait_ge(v_mm, i + 1)
                nc.vector.tensor_tensor(V[:, i, :, 0:HD], PS[:, 4 + i % 4, 0:D].rearrange("p (h d) -> p h d", d=HD),
                                        BV[:, 0].rearrange("p (h d) -> p h d", d=HD), ALU.add).then_inc(v_ev, 1)
            dve.wait_ge(k_ready, k_count(KD - 1))
            dve.wait_ge(km_d, 1)
            for kk in range(KD):
                for h in range(4, HK):
                    last = nc.vector.tensor_scalar(KM[:, kk, h], QK[:, 1, kk], HMASK[:, h:h + 1], None, ALU.mult)
            last.then_inc(km_d, 1)
            dve.wait_ge(consts, 2)

            def evacuate(u):
                b, qt, kt, h, per = UNITS[u]
                dve.wait_ge(t_mm, u + 1)
                if u >= 4:
                    dve.wait_ge(o_mm, u - 3)
                nc.vector.tensor_copy(PT[:, u % 4, :], PS[:, 3 + u % 2, :]).then_inc(t_ev, 1)

            def normalise(i):
                dve.wait_ge(o_mm, last_unit[i] + 1)
                o = PS[:, 5 + i % 2, 0:HEADS * (HD + 1)].rearrange("p (h d) -> p h d", d=HD + 1)
                c.then(nc.vector.reciprocal(REC[:, i % 2], o[:, :, HD]))
                nc.vector.tensor_tensor(ON[:, i], o[:, :, 0:HD],
                                        REC[:, i % 2].unsqueeze(2).broadcast_to([P, HEADS, HD]),
                                        ALU.mult).then_inc(o_ev, 1)

            done = 0
            for u, (b, qt, kt, h, per) in enumerate(UNITS):
                dve.wait_ge(s_mm, u + 1)
                if u >= 4:
                    dve.wait_ge(exp_d, u - 3)
                nc.vector.tensor_reduce(NM[:, u % 4, 0:per], PS[:, u % 3, :].rearrange("p (h j) -> p h j", h=per),
                                        AX.X, ALU.max, negate=True).then_inc(max_d, 1)
                if u >= 1:
                    evacuate(u - 1)
                if done < NT and u >= last_unit[done] + 3:
                    normalise(done)
                    done += 1
            evacuate(NU - 1)
            for i in range(done, NT):
                normalise(i)
            for g in range(KD * NH):
                kk, n = g // NH, g % NH
                dve.wait_ge(ot_mm, g + 1)
                nc.vector.tensor_copy(OT[:, kk, n * NB:(n + 1) * NB], PS[:, g, :]).then_inc(ot_ev, 1)
            if bo is not None:
                dve.wait_ge(bo_d, 1)
            for i in range(NT):
                dve.wait_ge(y_mm, i + 1)
                nc.vector.tensor_tensor(dst[:, i, :], PS[:, 4 + i % 4, 0:D], dst[:, i, :],
                                        ALU.add).then_inc(y_ev, 1)
    s.end()


def routed_ffn(core):
    nc, a, X, XN, XT, PS = core.nc, core.a, core.X, core.XN, core.XT, core.PS
    I, SH = 176, 704
    HID = E * I + SH
    TILES = -(-HID // P)
    R = E + 1
    s = Stage(core, "rffn")
    WG = s.sb("WG", [P, KD, R])
    logit = s.sb("logit", [P, NT, E])
    prob = s.sb("prob", [P, NT, E])
    weight = s.sb("weight", [P, NT, R])
    rank = s.sb("rank", [P, E])
    s.top_m = s.sb("top_m", [P, NT])
    s.top_eq = s.sb("top_eq", [P, NT, E])
    s.top_oh = s.sb("top_oh", [P, 2, NT, E])
    s.top_rest = s.sb("top_rest", [P, NT, E])
    mx = s.sb("mx", [P, NT])
    WT = s.sb("WT", [NT * R, P])
    CB = s.sb("CB", [P, TILES, N])
    WU = s.sb("WU", [P, 2, 2, KD, P])
    WD = s.sb("WD", [P, 2, D])
    SG = s.sb("SG", [P, 2, NB])
    SU = s.sb("SU", [P, 2, NB])
    HT = s.sb("HT", [P, 2, N])
    YT = s.sb("YT", [P, KD, N])
    scratch = nc.dram_tensor(f"routes_{s.tag}", (R, NT, P), FP32, kind="Internal").ap()
    g_in, r_mm, log_d, sub_d, exp_d, chain_v, route_d, wt_mm, wt_d, wt_out, cb_in, res_d = (s.sem(n) for n in (
        "g_in", "r_mm", "log_d", "sub_d", "exp_d", "chain_v", "route_d", "wt_mm", "wt_d", "wt_out", "cb_in", "res_d"))
    w_in = [s.sem("w_in0"), s.sem("w_in1")]
    up_mm, silu_d, su_d, h_d, dn_mm, yt_ev, y_mm = (s.sem(n) for n in (
        "up_mm", "silu_d", "su_d", "h_d", "dn_mm", "yt_ev", "y_mm"))
    PIECES = []
    for m in range(TILES):
        u = m * P
        while u < (m + 1) * P:
            r = min(u // I, E)
            end = (m + 1) * P if r == E else min((r + 1) * I, (m + 1) * P)
            PIECES.append((m, u - m * P, end - m * P, r))
            u = end

    with nc.Block() as block:
        @block.sync
        def _(sp):
            sp.dma_start(WG[:, :, 0:E], a["L1_ffn_w_router"].rearrange("(k p) e -> p k e", p=P)).then_inc(g_in, 16)
            sp.dma_start(WG[:, :, E:R], a["L1_ffn_w_sh_eg"].rearrange("(k p) e -> p k e", p=P),
                         allow_slow_non_contiguous=True).then_inc(g_in, 16)

            def load(m, r):
                up = a["L1_ffn_up"][bass.ds(m, 1)]
                for q in range(2):
                    sp.dma_start(WU[:, r, q], up[:, q].rearrange("o (k p) n -> p (o k) n", p=P)).then_inc(w_in[r], 16)
                sp.dma_start(WD[:, r], a["L1_ffn_down"][bass.ds(m, 1)].rearrange("o p n -> p (o n)")).then_inc(w_in[r], 16)

            load(0, 0)
            load(1, 1)
            sp.wait_ge(g_in, 32)
            sp.wait_ge(wt_d, 1)
            for i in range(NT):
                sp.dma_start(scratch[:, i, :], WT[i * R:(i + 1) * R, :]).then_inc(wt_out, 16)
            sp.wait_ge(wt_out, 16 * NT)
            for m, lo, hi, r in PIECES:
                if hi > lo:
                    sp.dma_start(CB[lo:hi, m, :], scratch[r:r + 1].rearrange("o i p -> o (i p)")
                                 .broadcast_to([hi - lo, N])).then_inc(cb_in, 16)
            with sp.Fori(1, TILES // 2) as j:
                sp.wait_ge(dn_mm, 2 * j - 1)
                load(2 * j, 0)
                sp.wait_ge(dn_mm, 2 * j)
                load(2 * j + 1, 1)
            sp.wait_ge(dn_mm, TILES - 2)
            load(TILES - 1, 0)
            sp.wait_ge(w_in[0], 48 * (TILES // 2 + 1))
            sp.wait_ge(w_in[1], 48 * (TILES // 2))
            sp.wait_ge(cb_in, 16 * len(PIECES))

        @block.gpsimd
        def _(pool):
            nc.gpsimd.tensor_tensor(X[:], X[:], XN[:], ALU.add).then_inc(res_d, 1)

        @block.tensor
        def _(pe):
            pe.wait_ge(g_in, 32)
            for i in range(NT):
                for k in range(KD):
                    last = nc.tensor.matmul(PS[:, 7, i * R:(i + 1) * R], XT[:, k, i * P:(i + 1) * P],
                                            WG[:, k, :], start=(k == 0), stop=(k == KD - 1))
            last.then_inc(r_mm, 1)
            pe.wait_ge(route_d, 1)
            nc.tensor.transpose(PS[0:NT * R, 6, 0:P], weight[:].rearrange("p i r -> p (i r)"),
                                core.ident[:]).then_inc(wt_mm, 1)
            pe.wait_ge(wt_d, 1)

            def up(m, r, first):
                pe.wait_ge(w_in[r], 24 * m + (48 if r == 0 else 24))
                for n in range(NH):
                    if not first:
                        pe.wait_ge(h_d, NH * m - NH + n + 1)
                    for q in range(2):
                        for k in range(KD):
                            last = nc.tensor.matmul(PS[:, 4 + 2 * n + q, :], WU[:, r, q, k, :],
                                                    XT[:, k, n * NB:(n + 1) * NB], start=(k == 0), stop=(k == KD - 1))
                    last.then_inc(up_mm, 1)

            def down(m, r, start, stop):
                for n in range(NH):
                    pe.wait_ge(h_d, NH * m + n + 1)
                    for q in range(KD):
                        last = nc.tensor.matmul(PS[:, n * KD + q, :], WD[:, r, q * P:(q + 1) * P],
                                                HT[:, r, n * NB:(n + 1) * NB], start=start, stop=stop)
                last.then_inc(dn_mm, 1)

            up(0, 0, True)
            up(1, 1, False)
            down(0, 0, True, False)
            with pe.Fori(1, TILES // 2) as j:
                up(2 * j, 0, False)
                down(2 * j - 1, 1, False, False)
                up(2 * j + 1, 1, False)
                down(2 * j, 0, False, False)
            up(TILES - 1, 0, False)
            down(TILES - 2, 1, False, False)
            down(TILES - 1, 0, False, True)
            for i in range(NT):
                pe.wait_ge(yt_ev, KD * (i // 4 + 1))
                for k in range(KD):
                    last = nc.tensor.transpose(PS[:, 4 + i // 2, (i % 2) * D + k * P:(i % 2) * D + (k + 1) * P],
                                               YT[:, k, i * P:(i + 1) * P], core.ident[:])
                if i % 2:
                    last.then_inc(y_mm, 1)

        @block.scalar
        def _(act):
            act.wait_ge(r_mm, 1)
            l = PS[:, 7, 0:NT * R].rearrange("p (i e) -> p i e", e=R)
            nc.scalar.activation(weight[:, :, E:R], l[:, :, E:R], ACT.Sigmoid)
            nc.scalar.activation(logit[:], l[:, :, 0:E], ACT.Copy).then_inc(log_d, 1)
            act.wait_ge(sub_d, 1)
            nc.scalar.activation(prob[:], logit[:], ACT.Exp).then_inc(exp_d, 1)
            act.wait_ge(wt_mm, 1)
            nc.scalar.copy(WT[:], PS[0:NT * R, 6, 0:P]).then_inc(wt_d, 1)

            def gate(m, first):
                for n in range(NH):
                    act.wait_ge(up_mm, NH * m + n + 1)
                    if not first:
                        act.wait_ge(h_d, NH * m + n - 1)
                    nc.scalar.activation(SG[:, n, :], PS[:, 4 + 2 * n, :], ACT.Silu).then_inc(silu_d, 1)

            gate(0, True)
            with act.Fori(1, TILES) as m:
                gate(m, False)
            for n in range(NH):
                act.wait_ge(dn_mm, TILES)
                for q in range(KD):
                    nc.scalar.copy(YT[:, q, n * NB:(n + 1) * NB], PS[:, n * KD + q, :]).then_inc(yt_ev, 1)

        @block.vector
        def _(dve):
            c = Chain(dve, chain_v)
            for e in range(E):
                last = nc.vector.memset(rank[:, e:e + 1], float(E - e))
            c.then(last)
            dve.wait_ge(log_d, 1)
            c.then(nc.vector.tensor_reduce(mx[:], logit[:], AX.X, ALU.max))
            nc.vector.tensor_tensor(logit[:], logit[:], mx[:].unsqueeze(2).broadcast_to([P, NT, E]),
                                    ALU.subtract).then_inc(sub_d, 1)
            dve.wait_ge(exp_d, 1)
            c.then(nc.vector.tensor_reduce(mx[:], prob[:], AX.X, ALU.add))
            c.then(nc.vector.reciprocal(mx[:], mx[:]))
            c.then(nc.vector.tensor_tensor(prob[:], prob[:], mx[:].unsqueeze(2).broadcast_to([P, NT, E]), ALU.mult))
            top2(core, s, dve, c, prob, weight[:, :, 0:E], rank).then_inc(route_d, 1)
            dve.wait_ge(cb_in, 16 * len(PIECES))

            def hidden(m, r, first):
                for n in range(NH):
                    cols = slice(n * NB, (n + 1) * NB)
                    dve.wait_ge(up_mm, NH * m + n + 1)
                    nc.vector.tensor_tensor(SU[:, n, :], PS[:, 5 + 2 * n, :], CB[:, bass.ds(m, 1), cols]
                                            .rearrange("p o n -> p (o n)"), ALU.mult).then_inc(su_d, 1)
                    dve.wait_ge(silu_d, NH * m + n + 1)
                    dve.wait_ge(su_d, NH * m + n + 1)
                    if not first:
                        dve.wait_ge(dn_mm, m - 1)
                    nc.vector.tensor_tensor(HT[:, r, cols], SG[:, n, :], SU[:, n, :], ALU.mult).then_inc(h_d, 1)

            hidden(0, 0, True)
            hidden(1, 1, True)
            with dve.Fori(1, TILES // 2) as j:
                hidden(2 * j, 0, False)
                hidden(2 * j + 1, 1, False)
            hidden(TILES - 1, 0, False)
            dve.wait_ge(res_d, 1)
            for i in range(NT):
                dve.wait_ge(y_mm, i // 2 + 1)
                nc.vector.tensor_tensor(X[:, i, :], PS[:, 4 + i // 2, (i % 2) * D:(i % 2 + 1) * D], X[:, i, :], ALU.add)
    s.end()


def delta_attention(core):
    nc, a, X, XT, PS = core.nc, core.a, core.X, core.XT, core.PS
    YT = core.XN[:].rearrange("p i d -> p (i d)").rearrange("p (k n) -> p k n", k=KD)
    H, HD, TAPS = 16, 128, 4
    BT = 64
    C = 8
    NBLK, NC = T // BT, BT // C
    BH = H * B
    W2 = 2 * C
    WIN = BT + TAPS - 1
    s = Stage(core, "delta")
    XP = s.sb("XP", [P, KD, B, T + TAPS - 1])
    KQV = s.sb("KQV", [P, 3, H, B, BT])
    AA = s.sb("AA", [P, H, B, BT])
    S = s.sb("S", [P, BH, HD])
    STT = s.sb("STT", [P, BH, HD])
    WH = s.sb("WH", [P, 2, 4, KD, P])
    WO = s.sb("WO", [P, 2, KD + 2, P])
    CW = s.sb("CW", [P, 3, H, TAPS])
    CB = s.sb("CB", [P, 4, H])
    WB = s.sb("WB", [P, KD, H])
    BB = s.sb("BB", [H, 1])
    BETA = s.sb("BETA", [H, B, T])
    LN = s.sb("LN", [P, 3])
    MEAN = s.sb("MEAN", [P, P])
    ONES = s.sb("ONES", [P, P])
    RSEL = s.sb("RSEL", [P, 4])
    KQ = s.sb("KQ", [P, BH, W2])
    VC = s.sb("VC", [P, BH, C])
    AC = s.sb("AC", [P, BH, C])
    DS = s.sb("DS", [P, BH, C])
    AP_ = s.sb("AP", [P, BH])
    BE = s.sb("BE", [P, BH, C])
    PR = s.sb("PR", [P, 2, BH * (W2 - 1)])
    TMP = PR[:].rearrange("p a n -> p (a n)")[:, 0:6 * B * BT].rearrange("p (r i b t) -> p r i b t", r=2, i=3, b=B)
    KD_ = WH[:].rearrange("p r i k n -> p (r i k n)").rearrange("p (g q k) -> p g q k", g=4, q=4)
    room = XT[:].rearrange("p k n -> p (k n)")
    T1 = room[:, 0:BH * (W2 - 1)]
    U, WC = (room[:, 960 + i * BH * C:960 + (i + 1) * BH * C].rearrange("p (n t) -> p n t", t=C) for i in range(2))
    F = s.sb("F", [P, BH, W2])
    E1 = s.sb("E1", [P, BH])
    WT = s.sb("WT", [P, 4, P])

    names = ["c_in", "consts", "xp_d", "z_mm", "beta_d", "p_mm", "tap0", "conv_d", "act_d", "a_d", "blk_in", "stage_d",
             "pr_d", "g_mm", "f_mm", "f_d", "be_mm", "be_d", "kt_mm", "kd_d", "step", "w_d", "wt_mm", "wt_d", "up_mm", "dec_d",
             "add_d", "st_mm", "st_d", "o_d", "gate_mm", "gate_d", "mean_mm", "cen_d", "sq_d", "var_mm", "root_d",
             "out_d", "yo_mm", "yo_d", "t_mm", "chain_v", "chain_p", "pd", "step_c"]
    (c_in, consts, xp_d, z_mm, beta_d, p_mm, tap0, conv_d, act_d, a_d, blk_in, stage_d, pr_d, g_mm, f_mm, f_d, be_mm,
     be_d, kt_mm, kd_d, step, w_d, wt_mm, wt_d, up_mm, dec_d, add_d, st_mm, st_d, o_d, gate_mm, gate_d, mean_mm,
     cen_d, sq_d, var_mm, root_d, out_d, yo_mm, yo_d, t_mm, chain_v, chain_p, pd, step_c) = (s.sem(n) for n in names)
    wh_in = [s.sem("wh_in0"), s.sem("wh_in1")]
    wo_in = [s.sem("wo_in0"), s.sem("wo_in1")]
    CIN = 16 * (3 + 3 + 1 + 1 + 1 + 2)
    flat = lambda t: t.rearrange("p h b t -> p (h b) t")
    Kb, Qb, Vb = (KQV[:, i] for i in range(3))
    width = lambda t: W2 - 1 - 2 * t

    with nc.Block() as block:
        @block.sync
        def _(sp):
            pre = "L1_attn_b_"
            for i, n in enumerate("qkv"):
                sp.dma_start(CW[:, i], a[pre + n + "conv_w"].rearrange("(h p) t -> p h t", p=P)).then_inc(c_in, 16)
                sp.dma_start(CB[:, i], a[pre + n + "conv_b"].rearrange("(h p) -> p h", p=P),
                             allow_slow_non_contiguous=True).then_inc(c_in, 16)
            sp.dma_start(CB[:, 3], a[pre + "ba"].rearrange("(h p) -> p h", p=P),
                         allow_slow_non_contiguous=True).then_inc(c_in, 16)
            sp.dma_start(WB[:], a[pre + "Wb"].rearrange("(k p) h -> p k h", p=P)).then_inc(c_in, 16)
            sp.dma_start(BB[:], a[pre + "bb"].rearrange("(h o) -> h o", o=1)).then_inc(c_in, 16)
            for i, n in enumerate(("ln_g", "ln_b")):
                sp.dma_start(LN[:, i:i + 1], a[pre + n].rearrange("(p o) -> p o", o=1)).then_inc(c_in, 16)

            def load(h, r):
                sp.dma_start(WH[:, r].rearrange("p i k n -> p (i k n)"),
                             a["L1_attn_b_heads"][bass.ds(h, 1)].rearrange("o p n -> p (o n)")).then_inc(wh_in[r], 16)

            def load_out(h, r):
                sp.dma_start(WO[:, r].rearrange("p i n -> p (i n)"),
                             a["L1_attn_b_outs"][bass.ds(h, 1)].rearrange("o p n -> p (o n)")).then_inc(wo_in[r], 16)

            def block_loads(n, first, heads_done=None):
                if not first:
                    sp.wait_ge(yo_mm, heads_done)
                for r in range(2):
                    load(r, r)
                with sp.Fori(1, H // 2) as j:
                    for r in range(2):
                        sp.wait_ge(p_mm, 4 * H * n + 4 * (2 * j + r) - 4)
                        load(2 * j + r, r)
                for r in range(2):
                    load_out(r, r)
                with sp.Fori(1, H // 2) as j:
                    for r in range(2):
                        sp.wait_ge(gate_mm, H * n + 2 * j + r - 1)
                        load_out(2 * j + r, r)
                for r in range(2):
                    sp.wait_ge(gate_mm, H * n + H - 1 + r)
                    load_out(r, r)
                with sp.Fori(1, H // 2) as j:
                    for r in range(2):
                        sp.wait_ge(yo_mm, H * n + 2 * j + r - 1)
                        load_out(2 * j + r, r)

            block_loads(0, True)
            with sp.Fori(1, NBLK) as n:
                block_loads(n, False, sp.snap(H * n))
            sp.wait_ge(c_in, CIN)
            for r in range(2):
                sp.wait_ge(wh_in[r], 16 * NBLK * H // 2)
                sp.wait_ge(wo_in[r], 16 * NBLK * H)

        @block.gpsimd
        def _(pool):
            c = Chain(pool, chain_p)
            nc.gpsimd.memset(XP[:, :, :, 0:TAPS - 1], 0.0)
            nc.gpsimd.memset(MEAN[:], 1.0 / HD)
            nc.gpsimd.memset(ONES[:], 1.0)
            nc.gpsimd.memset(LN[:, 2:3], LN_EPS)
            nc.gpsimd.memset(DS[:, :, C - 1:C], 1.0)
            nc.gpsimd.memset(S[:], 0.0)
            nc.gpsimd.memset(STT[:], 0.0).then_inc(consts, 1)

            def chunk(n, ch, ci, first):
                if not first:
                    pool.wait_ge(step, C * ci)
                    pool.wait_ge(kt_mm, ci)
                    pool.wait_ge(w_d, ci)
                pool.wait_ge(act_d, 3 * H * n + 3 * H)
                pool.wait_ge(a_d, n + 1)
                t0 = ch * C
                tok = lambda arr: flat(arr)[:, :, bass.ds(t0, C)]
                kq = KQ[:].rearrange("p n (t q) -> p n t q", q=2)
                c.then(nc.gpsimd.tensor_copy(kq[:, :, :, 0], tok(Kb)))
                nc.gpsimd.tensor_copy(kq[:, :, :, 1], tok(Qb))
                c.then(nc.gpsimd.tensor_scalar(kq[:, :, :, 0], kq[:, :, :, 0], float(HD) ** -0.5, None, ALU.mult))
                nc.gpsimd.tensor_copy(VC[:], tok(Vb))
                nc.gpsimd.tensor_copy(AC[:], tok(AA)).then_inc(stage_d, 1)
                for t in range(C):
                    w = width(t)
                    if not (first and t < 2):
                        pool.wait_ge(g_mm, C * ci + t - 1)
                    nc.gpsimd.tensor_tensor(PR[:, t % 2, 0:BH * w].rearrange("p (n w) -> p n w", w=w),
                                            KQ[:, :, 2 * t:2 * t + 1].broadcast_to([P, BH, w]), KQ[:, :, 2 * t + 1:W2],
                                            ALU.mult).then_inc(pr_d, 1)
                pool.wait_ge(stage_d, ci + 1)
                for t in reversed(range(C - 1)):
                    c.then(nc.gpsimd.tensor_tensor(DS[:, :, t], DS[:, :, t + 1], AC[:, :, t + 1], ALU.mult))
                c.then(nc.gpsimd.tensor_tensor(AP_[:], DS[:, :, 0], AC[:, :, 0], ALU.mult))
                if not first:
                    pool.wait_ge(st_mm, 16 * ci)
                    pool.wait_ge(add_d, 16 * ci)
                nc.gpsimd.tensor_tensor(S[:], S[:], AP_[:].unsqueeze(2).broadcast_to([P, BH, HD]),
                                        ALU.mult).then_inc(dec_d, 1)

            def blk(n, first):
                if first:
                    chunk(n, 0, 0, True)
                    k = c.count
                    with pool.Fori(1, NC) as ch:
                        c.base = k * ch
                        c.count = 0
                        chunk(n, ch, ch, False)
                else:
                    with pool.Fori(0, NC) as ch:
                        c.base = K_P * (n * NC + ch)
                        c.count = 0
                        chunk(n, ch, n * NC + ch, False)

            K_P = 2 + (C - 1) + 1
            blk(0, True)
            with pool.Fori(1, NBLK) as n:
                blk(n, False)

        @block.tensor
        def _(pe):
            pe.wait_ge(c_in, CIN)
            pe.wait_ge(xp_d, 2)
            for n in range(NH):
                for k in range(KD):
                    last = nc.tensor.matmul(PS[0:H, n, :], WB[:, k, :], XT[:, k, n * NB:(n + 1) * NB],
                                            start=(k == 0), stop=(k == KD - 1))
                last.then_inc(z_mm, 1)
            pe.wait_ge(beta_d, 2)
            pe.wait_ge(consts, 1)

            def head(n, hi, j, r, first, blk_n=None):
                pe.wait_ge(wh_in[r], 16 * j + 16)
                if not first:
                    pe.wait_ge(tap0, 3 * hi - 3)
                    pe.wait_ge(conv_d, 3 * hi - 3)
                    pe.wait_ge(pd, hi - 1)
                    if blk_n is not None:
                        pe.wait_ge(yo_d, blk_n)
                for i in range(3):
                    for k in range(KD):
                        last = nc.tensor.matmul(PS[:, 4 * r + i, 0:B * WIN], WH[:, r, i, k, :],
                                                XP[:, k, :, bass.ds(n * BT, WIN)], start=(k == 0), stop=(k == KD - 1))
                    last.then_inc(p_mm, 1)
                for k in range(KD):
                    last = nc.tensor.matmul(PS[:, 4 * r + 3, 0:B * BT], WH[:, r, 3, k, :],
                                            XP[:, k, :, bass.ds(n * BT + TAPS - 1, BT)],
                                            start=(k == 0), stop=(k == KD - 1))
                last.then_inc(p_mm, 1)

            def chunk(n, ch, ci, first):
                pe.wait_ge(act_d, 3 * H * n + 3 * H)
                pe.wait_ge(a_d, n + 1)
                pe.wait_ge(stage_d, ci + 1)
                if not first:
                    pe.wait_ge(st_d, 16 * ci)
                for i in range(BH):
                    last = nc.tensor.matmul(PS[:, 4 + i // 32, (i % 32) * W2:(i % 32 + 1) * W2], STT[:, i, :],
                                            KQ[:, i, :], start=True, stop=True)
                    if i % 32 == 31:
                        last.then_inc(f_mm, 1)
                for h in range(H):
                    last = nc.tensor.matmul(PS[:, 6, h * B * C:(h + 1) * B * C],
                                            core.ident[0:H, h:h + 1].broadcast_to([H, P]),
                                            BETA[:, :, bass.ds(n * BT + ch * C, C)], start=True, stop=True)
                last.then_inc(be_mm, 1)
                for g in range(4):
                    last = nc.tensor.transpose(PS[:, 7, g * P:(g + 1) * P],
                                               KQ[:, 16 * g:16 * g + 16, 0:W2:2], core.ident[:])
                last.then_inc(kt_mm, 1)
                for t in range(C):
                    w = width(t)
                    pe.wait_ge(pr_d, C * ci + t + 1)
                    if not (first and t < 2):
                        pe.wait_ge(step, C * ci + t - 1)
                    for i in range(2):
                        last = nc.tensor.matmul(PS[:, 2 * (t % 2) + i, 0:32 * w], ONES[:],
                                                PR[:, t % 2, 32 * w * i:32 * w * (i + 1)], start=True, stop=True)
                    last.then_inc(g_mm, 1)
                pe.wait_ge(w_d, ci + 1)
                pe.wait_ge(kd_d, ci + 1)
                for g in range(4):
                    last = nc.tensor.transpose(PS[:, 7, g * P:(g + 1) * P], WC[:, 16 * g:16 * g + 16, :], core.ident[:])
                last.then_inc(wt_mm, 1)
                pe.wait_ge(wt_d, ci + 1)
                pe.wait_ge(be_d, ci + 1)
                pe.wait_ge(f_d, 2 * ci + 2)
                for q in range(16):
                    if q >= 4:
                        pe.wait_ge(add_d, 16 * ci + q - 3)
                    g, rr = q // 4, q % 4
                    nc.tensor.matmul(PS[:, 4 + q % 4, :], WT[32 * rr:32 * rr + 32, g, :],
                                     KD_[32 * rr:32 * rr + 32, g].rearrange("p a k -> p (a k)"),
                                     start=True, stop=True, tile_position=(32 * rr, 0)).then_inc(up_mm, 1)
                for q in range(16):
                    pe.wait_ge(add_d, 16 * ci + q + 1)
                    if q >= 4:
                        pe.wait_ge(st_d, 16 * ci + q - 3)
                    for i in range(4):
                        last = nc.tensor.transpose(PS[:, q % 4, i * P:(i + 1) * P], S[:, 4 * q + i, :], core.ident[:])
                    last.then_inc(st_mm, 1)

            def gate_head(n, j, r, first):
                pe.wait_ge(st_d, 16 * NC * n + 16 * NC)
                pe.wait_ge(wo_in[r], 16 * (H * n + j) + 16)
                if not first:
                    pe.wait_ge(gate_d, H * n + 2 * j + r - 1)
                for k in range(KD):
                    last = nc.tensor.matmul(PS[:, 4 + r, 0:B * BT], WO[:, r, k, :],
                                            XP[:, k, :, bass.ds(n * BT + TAPS - 1, BT)],
                                            start=(k == 0), stop=(k == KD - 1))
                last.then_inc(gate_mm, 1)

            def blk(n, first):
                if first:
                    head(n, 0, 0, 0, True)
                    head(n, 1, 0, 1, True)
                    with pe.Fori(1, H // 2) as j:
                        head(n, 2 * j, j, 0, False)
                        head(n, 2 * j + 1, j, 1, False)
                else:
                    with pe.Fori(0, H // 2) as j:
                        head(n, H * n + 2 * j, H // 2 * n + j, 0, False, n)
                        head(n, H * n + 2 * j + 1, H // 2 * n + j, 1, False, n)
                if first:
                    chunk(n, 0, 0, True)
                    with pe.Fori(1, NC) as ch:
                        chunk(n, ch, ch, False)
                else:
                    with pe.Fori(0, NC) as ch:
                        chunk(n, ch, n * NC + ch, False)
                if first:
                    for r in range(2):
                        gate_head(n, 0, r, True)
                with pe.Fori(1 if first else 0, H // 2) as j:
                    for r in range(2):
                        gate_head(n, j, r, False)
                pe.wait_ge(o_d, NC * n + NC)
                for g in range(8):
                    if g >= 4:
                        pe.wait_ge(cen_d, 8 * n + g - 3)
                    nc.tensor.matmul(PS[:, g % 4, :], MEAN[:], flat(Vb)[:, 8 * g:8 * g + 8, :], start=True,
                                     stop=True).then_inc(mean_mm, 1)
                pe.wait_ge(cen_d, 8 * n + 8)
                for g in range(8):
                    pe.wait_ge(sq_d, 8 * n + g + 1)
                    if g >= 4:
                        pe.wait_ge(root_d, 8 * n + g - 3)
                    nc.tensor.matmul(PS[:, g % 4, :], MEAN[:], flat(Kb)[:, 8 * g:8 * g + 8, :], start=True,
                                     stop=True).then_inc(var_mm, 1)
                pe.wait_ge(out_d, n + 1)
                pe.wait_ge(root_d, 8 * n + 8)

                def out_head(j, r, start, stop):
                    pe.wait_ge(wo_in[r], 16 * (H * n + H // 2 + j) + 16)
                    for k in range(KD):
                        last = nc.tensor.matmul(PS[:, k, 0:B * BT], WO[:, r, KD + k, :],
                                                KQV[:, 2, bass.ds(2 * j + r, 1)].rearrange("p o b t -> p (o b) t"),
                                                start=start, stop=stop)
                    last.then_inc(yo_mm, 1)

                out_head(0, 0, True, False)
                out_head(0, 1, False, False)
                with pe.Fori(1, H // 2 - 1) as j:
                    out_head(j, 0, False, False)
                    out_head(j, 1, False, False)
                out_head(H // 2 - 1, 0, False, False)
                out_head(H // 2 - 1, 1, False, True)

            blk(0, True)
            with pe.Fori(1, NBLK) as n:
                blk(n, False)
            pe.wait_ge(yo_d, NBLK)
            for i in range(NT):
                for k in range(KD):
                    last = nc.tensor.transpose(PS[:, i // 2, (i % 2) * D + k * P:(i % 2) * D + (k + 1) * P],
                                               YT[:, k, i * P:(i + 1) * P], core.ident[:])
                if i % 2:
                    last.then_inc(t_mm, 1)

        @block.scalar
        def _(act):
            act.wait_ge(c_in, CIN)
            for n in range(NH):
                act.wait_ge(z_mm, n + 1)
                nc.scalar.activation(BETA[:].rearrange("h b t -> h (b t)")[:, n * NB:(n + 1) * NB], PS[0:H, n, :],
                                     ACT.Sigmoid, bias=BB[:]).then_inc(beta_d, 1)

            def taps(n, h, hi, r, first):
                win = lambda bank: PS[:, bank, 0:B * WIN].rearrange("p (b t) -> p b t", b=B)
                for i in range(3):
                    act.wait_ge(p_mm, 4 * hi + i + 1)
                    if not first:
                        act.wait_ge(act_d, 3 * hi - 5 + i)
                    nc.scalar.activation(TMP[:, r, i], win(4 * r + i)[:, :, TAPS - 1:], ACT.Identity,
                                         bias=CB[:, i, bass.ds(h, 1)],
                                         scale=CW[:, i, bass.ds(h, 1), TAPS - 1]).then_inc(tap0, 1)
                act.wait_ge(p_mm, 4 * hi + 4)
                nc.scalar.activation(AA[:, bass.ds(h, 1)].rearrange("p o b t -> p (o b t)"), PS[:, 4 * r + 3, 0:B * BT],
                                     ACT.Identity, bias=CB[:, 3, bass.ds(h, 1)]).then_inc(pd, 1)

            def silus(n, h, hi, r):
                for i in range(3):
                    act.wait_ge(conv_d, 3 * hi + i + 1)
                    nc.scalar.activation(KQV[:, (1, 0, 2)[i], bass.ds(h, 1)].rearrange("p o b t -> p (o b) t"),
                                         TMP[:, r, i], ACT.Silu).then_inc(act_d, 1)

            def chunk(n, ch, ci, first):
                for i in range(2):
                    act.wait_ge(f_mm, 2 * ci + i + 1)
                    nc.scalar.copy(F[:, 32 * i:32 * i + 32, :].rearrange("p n w -> p (n w)"),
                                   PS[:, 4 + i, :]).then_inc(f_d, 1)
                act.wait_ge(be_mm, ci + 1)
                nc.scalar.copy(BE[:].rearrange("p n t -> p (n t)"), PS[:, 6, :]).then_inc(be_d, 1)
                act.wait_ge(kt_mm, ci + 1)
                for q in range(4):
                    last = nc.scalar.activation(KD_[:, :, q, :], PS[:, 7, :].rearrange("p (g k) -> p g k", g=4),
                                                ACT.Copy, scale=RSEL[:, q:q + 1])
                last.then_inc(kd_d, 1)
                act.wait_ge(wt_mm, ci + 1)
                nc.scalar.copy(WT[:].rearrange("p g v -> p (g v)"), PS[:, 7, :]).then_inc(wt_d, 1)
                for q in range(16):
                    act.wait_ge(st_mm, 16 * ci + q + 1)
                    nc.scalar.copy(STT[:, 4 * q:4 * q + 4, :].rearrange("p n v -> p (n v)"),
                                   PS[:, q % 4, :]).then_inc(st_d, 1)

            def blk(n, first):
                if first:
                    taps(n, 0, 0, 0, True)
                    taps(n, 1, 1, 1, True)
                    silus(n, 0, 0, 0)
                else:
                    act.wait_ge(out_d, n)
                    act.wait_ge(yo_mm, H * n)
                    taps(n, 0, H * n, 0, False)
                    taps(n, 1, H * n + 1, 1, False)
                    silus(n, 0, H * n, 0)
                with act.Fori(1, H // 2) as j:
                    hi = 2 * j if first else H * n + 2 * j
                    taps(n, 2 * j, hi, 0, False)
                    silus(n, 2 * j - 1, hi - 1, 1)
                    taps(n, 2 * j + 1, hi + 1, 1, False)
                    silus(n, 2 * j, hi, 0)
                silus(n, H - 1, H - 1 if first else H * n + H - 1, 1)
                act.wait_ge(pd, H if first else H * n + H)
                nc.scalar.activation(flat(AA), flat(AA), ACT.Sigmoid).then_inc(a_d, 1)
                if first:
                    act.wait_ge(consts, 2)
                    chunk(n, 0, 0, True)
                    with act.Fori(1, NC) as ch:
                        chunk(n, ch, ch, False)
                else:
                    with act.Fori(0, NC) as ch:
                        chunk(n, ch, n * NC + ch, False)
                act.wait_ge(stage_d, NC * n + NC)
                with act.Fori(0, H // 2) as j:
                    for r in range(2):
                        h = 2 * j + r
                        act.wait_ge(gate_mm, H * n + h + 1)
                        nc.scalar.activation(AA[:, bass.ds(h, 1)].rearrange("p o b t -> p (o b t)"),
                                             PS[:, 4 + r, 0:B * BT], ACT.Sigmoid).then_inc(gate_d, 1)
                for g in range(8):
                    act.wait_ge(cen_d, 8 * n + g + 1)
                    nc.scalar.activation(flat(Kb)[:, 8 * g:8 * g + 8, :], flat(Vb)[:, 8 * g:8 * g + 8, :],
                                         ACT.Square).then_inc(sq_d, 1)
                for g in range(8):
                    act.wait_ge(var_mm, 8 * n + g + 1)
                    nc.scalar.activation(flat(Qb)[:, 8 * g:8 * g + 8, :].rearrange("p n t -> p (n t)"), PS[:, g % 4, :],
                                         ACT.Sqrt, bias=LN[:, 2:3]).then_inc(root_d, 1)
                act.wait_ge(yo_mm, H * n + H)
                for k in range(KD):
                    last = nc.scalar.copy(YT[:, k].rearrange("p (b t) -> p b t", b=B)[:, :, bass.ds(n * BT, BT)],
                                          PS[:, k, 0:B * BT].rearrange("p (b t) -> p b t", b=B))
                last.then_inc(yo_d, 1)

            blk(0, True)
            with act.Fori(1, NBLK) as n:
                blk(n, False)

        @block.vector
        def _(dve):
            c = Chain(dve, chain_v)
            for k in range(KD):
                nc.vector.tensor_copy(XP[:, k, :, TAPS - 1:], XT[:, k].rearrange("p (b t) -> p b t", b=B)).then_inc(xp_d, 1)
            c.then(nc.vector.tensor_reduce(RSEL[:], core.ident[:].rearrange("p (g q t) -> p q g t", g=4, q=4), AX.XY, ALU.add))
            dve.wait_ge(c_in, CIN)
            dve.wait_ge(consts, 1)
            nc.vector.tensor_copy(LN[:, 2:3], LN[:, 2:3]).then_inc(consts, 1)
            C0 = 1

            def head(h, hi, r):
                win = lambda bank: PS[:, bank, 0:B * WIN].rearrange("p (b t) -> p b t", b=B)
                for i in range(3):
                    dve.wait_ge(tap0, 3 * hi + i + 1)
                for tau in range(TAPS - 1):
                    for i in range(3):
                        if tau:
                            dve.wait_ge(step_c, 6 * hi + 3 * (tau - 1) + i + 1)
                        nc.vector.scalar_tensor_tensor(TMP[:, r, i], win(4 * r + i)[:, :, tau:tau + BT],
                                                       CW[:, i, bass.ds(h, 1), tau], TMP[:, r, i], ALU.mult,
                                                       ALU.add).then_inc(conv_d if tau == TAPS - 2 else step_c, 1)

            def chunk(n, ch, ci, first):
                dve.wait_ge(stage_d, ci + 1)
                dve.wait_ge(f_d, 2 * ci + 2)
                dve.wait_ge(be_d, ci + 1)
                for t in range(C):
                    w = width(t)
                    rest = F[:, :, 2 * t + 1:W2]
                    nc.vector.tensor_tensor(E1[:], F[:, :, 2 * t], VC[:, :, t], ALU.subtract)
                    c.then(nc.vector.tensor_tensor(rest, rest, AC[:, :, t:t + 1].broadcast_to([P, BH, w]), ALU.mult))
                    c.then(nc.vector.tensor_tensor(U[:, :, t], E1[:], BE[:, :, t], ALU.mult))
                    dve.wait_ge(g_mm, C * ci + t + 1)
                    halves = lambda x: x.rearrange("p (i n) w -> p i n w", i=2)
                    t1 = T1[:, 0:BH * w].rearrange("p (n w) -> p n w", w=w)
                    g = PS[:, 2 * (t % 2):2 * (t % 2) + 2, 0:32 * w].rearrange("p i (n w) -> p i n w", w=w)
                    nc.vector.tensor_tensor(halves(t1), g, halves(U[:, :, t:t + 1]).broadcast_to([P, 2, 32, w]),
                                            ALU.mult).then_inc(step, 1)
                    dve.wait_ge(step, C * ci + t + 1)
                    c.then(nc.vector.tensor_tensor(rest, rest, t1, ALU.subtract))
                dve.wait_ge(dec_d, ci + 1)
                nc.vector.scalar_tensor_tensor(WC, U, -1.0, DS[:], ALU.mult, ALU.mult).then_inc(w_d, 1)
                nc.vector.tensor_copy(flat(Vb)[:, :, bass.ds(ch * C, C)], F[:, :, 1:W2:2]).then_inc(o_d, 1)
                for q in range(16):
                    dve.wait_ge(up_mm, 16 * ci + q + 1)
                    o = S[:, 4 * q:4 * q + 4, :].rearrange("p n k -> p (n k)")
                    nc.vector.tensor_tensor(o, o, PS[:, 4 + q % 4, :], ALU.add).then_inc(add_d, 1)

            def blk(n, first):
                if first:
                    with dve.Fori(0, H // 2) as j:
                        head(2 * j, 2 * j, 0)
                        head(2 * j + 1, 2 * j + 1, 1)
                    c.base, c.count = C0, 0
                    with dve.Fori(0, NC) as ch:
                        c.base, c.count = C0 + K_V * ch, 0
                        chunk(n, ch, ch, False)
                else:
                    with dve.Fori(0, H // 2) as j:
                        head(2 * j, H * n + 2 * j, 0)
                        head(2 * j + 1, H * n + 2 * j + 1, 1)
                    with dve.Fori(0, NC) as ch:
                        c.base, c.count = C0 + K_V * (n * NC + ch) + K_T * n, 0
                        chunk(n, ch, n * NC + ch, False)
                c.base, c.count = C0 + K_V * NC * (n + 1) + K_T * n, 0
                for g in range(8):
                    dve.wait_ge(mean_mm, 8 * n + g + 1)
                    o = flat(Vb)[:, 8 * g:8 * g + 8, :].rearrange("p n t -> p (n t)")
                    nc.vector.tensor_tensor(o, o, PS[:, g % 4, :], ALU.subtract).then_inc(cen_d, 1)
                dve.wait_ge(root_d, 8 * n + 8)
                fl = lambda t: t.rearrange("p h b t -> p (h b t)")
                c.then(nc.vector.reciprocal(fl(Qb), fl(Qb)))
                dve.wait_ge(cen_d, 8 * n + 8)
                c.then(nc.vector.tensor_tensor(fl(Vb), fl(Vb), fl(Qb), ALU.mult))
                c.then(nc.vector.tensor_scalar(fl(Vb), fl(Vb), LN[:, 0:1], LN[:, 1:2], ALU.mult, ALU.add))
                dve.wait_ge(gate_d, H * n + H)
                nc.vector.tensor_tensor(fl(Vb), fl(Vb), AA[:].rearrange("p h b t -> p (h b t)"), ALU.mult).then_inc(out_d, 1)

            K_V = 3 * C
            K_T = 3
            blk(0, True)
            with dve.Fori(1, NBLK) as n:
                blk(n, False)
            for i in range(NT):
                dve.wait_ge(t_mm, i // 2 + 1)
                nc.vector.tensor_tensor(X[:, i, :], PS[:, i // 2, (i % 2) * D:(i % 2 + 1) * D], X[:, i, :], ALU.add)
    s.end()


def program(nc, args, out):
    with ExitStack() as ctx:
        core = Core(nc, ctx, args)
        setup(core)

        def sub1():
            norm(core, rms_eps=float(np.finfo(np.float32).eps))
            linear_attention(core)

        def sub2():
            norm(core)
            moe(core)

        def sub3():
            norm(core, rms_eps=1e-6, weight=args["L0_attn_b_norm_scale"])
            conv_scan(core)

        def sub5():
            norm(core)
            qkv, b = args["L1_attn_a_W_qkv"], args["L1_attn_a_b_qkv"]
            softmax_attention(core, qkv[:, 0:D], qkv[:, D:2 * D], qkv[:, 2 * D:3 * D], b[0:D], b[D:2 * D], b[2 * D:3 * D],
                              args["L1_attn_a_W_out"], args["L1_attn_a_b_out"], None, None, core.X)

        def sub6():
            w = lambda n: args["L1_ffn_" + n]
            norm(core, rms_eps=1e-6, weight=w("w_ln1"))
            softmax_attention(core, w("wq"), w("wk"), w("wv"), w("bq"), w("bk"), w("bv"), w("wo"), None,
                              args["trig1"], (w("bq_swapped"), w("bk_swapped")), core.XN)
            norm(core, layer=False, rms_eps=1e-6, weight=w("w_ln2"))
            routed_ffn(core)

        def sub7():
            norm(core)
            delta_attention(core)

        subs = [sub1, sub2, sub3, sub2, sub5, sub6, sub7, sub6]
        for f in subs[START:STOP]:
            f()
        finish(core, out)


TURNED = ("L0_attn_a_Wq", "L0_attn_a_Wk", "L0_attn_a_Wv", "L0_attn_a_Wg", "L0_attn_a_Wp",
          "L0_attn_b_in_proj_w", "L0_attn_b_out_proj_w", "L1_attn_a_W_qkv", "L1_attn_a_W_out")


def trig_table(base, head=16):
    inv = (np.float32(1.0) / np.float32(base) ** (np.arange(0, head, 2, dtype=np.float32) / np.float32(head)))
    angle = np.arange(T, dtype=np.float32)[:, None] * inv.astype(np.float32)[None, :]
    cos, sin = np.cos(angle).T, np.sin(angle).T
    return np.ascontiguousarray(np.stack([np.tile(np.concatenate([cos, cos]), (P // head, 1)),
                                          np.tile(np.concatenate([-sin, sin]), (P // head, 1))]).astype(np.float32))


def kernel(**inputs):
    import concourse.bacc as bacc
    from concourse.bass_utils import run_bass_kernel_spmd

    nc = bacc.Bacc("TRN2", target_bir_lowering=False, num_devices=1)
    arrays, args = {}, {}
    for name, a in inputs.items():
        a = np.asarray(a)
        if name in TURNED:
            a = a.T
        a = np.ascontiguousarray(a)
        arrays[f"in_{name}"] = a
        args[name] = nc.dram_tensor(f"in_{name}", a.shape, mybir.dt.from_np(a.dtype), kind="ExternalInput").ap()
    rows = np.ascontiguousarray(np.repeat(np.asarray(inputs["L0_attn_b_head_mix"]), 16, axis=0))
    swap = lambda n: np.ascontiguousarray(np.asarray(inputs[n]).reshape(-1, 2, 8)[:, ::-1].reshape(-1))
    hidden = 17 * P
    f = lambda n: np.asarray(inputs["L1_ffn_" + n])
    up = np.zeros((2, D, hidden), np.float32)
    for i, (routed, shared) in enumerate((("w_gate_e", "w_sh_gate"), ("w_up_e", "w_sh_up"))):
        up[i, :, :E * 176] = f(routed).transpose(1, 0, 2).reshape(D, -1)
        up[i, :, E * 176:E * 176 + 704] = f(shared)
    down = np.zeros((hidden, D), np.float32)
    down[:E * 176] = f("w_down_e").reshape(-1, D)
    down[E * 176:E * 176 + 704] = f("w_sh_down")
    g = lambda n: np.asarray(inputs["L1_attn_b_" + n]).reshape(KD, P, 16, P).transpose(2, 1, 0, 3)
    heads = np.ascontiguousarray(np.stack([g("Wq"), g("Wk"), g("Wv"), g("Wa")], axis=2).reshape(16, P, -1))
    wo = np.asarray(inputs["L1_attn_b_Wo"]).reshape(16, P, KD, P)
    outs = np.ascontiguousarray(np.concatenate([g("Wg"), wo], axis=2).reshape(16, P, -1))
    for name, a in (("L1_attn_b_heads", heads), ("L1_attn_b_outs", outs), ("L1_ffn_up", np.ascontiguousarray(up.reshape(2, D, 17, P).transpose(2, 0, 1, 3))),
                    ("L1_ffn_down", down.reshape(17, P, D)),
                    ("L1_ffn_bq_swapped", swap("L1_ffn_bq")), ("L1_ffn_bk_swapped", swap("L1_ffn_bk")),
                    ("L0_attn_b_head_rows", rows), ("trig0", trig_table(10000.0)), ("trig1", trig_table(1e6))):
        arrays[f"in_{name}"] = a
        args[name] = nc.dram_tensor(f"in_{name}", a.shape, FP32, kind="ExternalInput").ap()
    out = nc.dram_tensor("out_0_dram", (B, T, D), FP32, kind="ExternalOutput").ap()
    program(nc, args, out)
    r = run_bass_kernel_spmd(nc, [arrays], core_ids=[0])
    return r.results[0]["out_0_dram"]
```

```python
import numpy as np
import concourse.bass as bass
from concourse import mybir
from contextlib import ExitStack

FP32 = mybir.dt.float32
PART = mybir.dt.float32r
BF16 = mybir.dt.bfloat16
ALU = mybir.AluOpType
ACT = mybir.ActivationFunctionType
AX = mybir.AxisListType

P = 128
B, T, D = 4, 256, 256
N = B * T
NT = N // P
KD = D // P
NB = 512
NH = N // NB
E = 8
LN_EPS = 1e-5

START, STOP = 0, 8


class Chain:

    def __init__(self, engine, sem):
        self.engine, self.sem, self.count, self.base = engine, sem, 0, 0

    def then(self, instruction):
        self.count += 1
        instruction.then_inc(self.sem, 1)
        self.engine.wait_ge(self.sem, self.base + self.count)


class Core:

    def __init__(self, nc, ctx, args):
        self.nc, self.a = nc, args
        self.stages = 0

        def sb(name, shape, dt=FP32):
            return ctx.enter_context(nc.sbuf_tensor(name, shape, dt))

        self.X = sb("X", [P, NT, D])
        self.XN = sb("XN", [P, NT, D])
        self.XT = sb("XT", [P, KD, N])
        self.ident = sb("ident", [P, P])
        self.PS = ctx.enter_context(nc.psum_tensor("PS", [P, 8, NB], FP32))
        self.pool = [ctx.enter_context(nc.semaphore(f"stage_sem{i}")) for i in range(60)]


class Stage:

    def __init__(self, core, name):
        self.core, self.nc, self.name = core, core.nc, name
        self.ctx = ExitStack()
        self.sems = []
        core.stages += 1
        self.tag = f"{name}{core.stages}"

    def sb(self, name, shape, dt=FP32):
        return self.ctx.enter_context(self.nc.sbuf_tensor(f"{name}_{self.tag}", shape, dt))

    def sem(self, name):
        s = self.core.pool[len(self.sems)]
        self.sems.append(s)
        return s

    def end(self):
        for sem in self.sems:
            self.nc.gpsimd.sem_clear(sem)
        self.nc.all_engine_barrier()
        self.ctx.close()


def setup(core):
    nc, s = core.nc, Stage(core, "setup")
    x_in, filled = s.sem("x_in"), s.sem("filled")
    with nc.Block() as block:
        @block.sync
        def _(sp):
            sp.dma_start(core.X[:], core.a["L0_attn_a_x"].rearrange("b (i p) d -> p (b i) d", p=P)).then_inc(x_in, 16)
            sp.wait_ge(x_in, 16)

        @block.gpsimd
        def _(pool):
            nc.gpsimd.memset(core.ident[:], 0.0).then_inc(filled, 1)
            pool.wait_ge(filled, 1)
            nc.gpsimd.affine_select(out=core.ident[:], in_=core.ident[:], compare_op=ALU.not_equal,
                                    fill=1.0, base=0, pattern=[[-1, P]],
                                    channel_multiplier=1).then_inc(filled, 1)
            pool.wait_ge(filled, 2)
    s.end()


def finish(core, out):
    nc, s = core.nc, Stage(core, "finish")
    stored = s.sem("stored")
    with nc.Block() as block:
        @block.sync
        def _(sp):
            sp.dma_start(out.rearrange("b (i p) d -> p (b i) d", p=P), core.X[:]).then_inc(stored, 16)
            sp.wait_ge(stored, 16)
    s.end()


def norm(core, layer=True, rms_eps=None, weight=None):
    nc, X, XN, XT, PS = core.nc, core.X, core.XN, core.XT, core.PS
    s = Stage(core, "norm")
    stats = s.sb("stats", [P, NT, 6])
    mv = s.sb("mv", [P, NT, 2])
    root = s.sb("root", [P, NT])
    rstd = s.sb("rstd", [P, NT])
    rms = s.sb("rms", [P, NT])
    eps = s.sb("eps", [P, 2])
    w = s.sb("w", [P, KD])
    H = s.sb("H", [P, NT, D]) if rms_eps is not None else XN
    w_in, sumsq, rooted, scaled, turned, moved, chain_v = (s.sem(n) for n in (
        "w_in", "sumsq", "rooted", "scaled", "turned", "moved", "chain_v"))
    src = X if layer else XN
    with nc.Block() as block:
        @block.sync
        def _(sp):
            if weight is not None:
                sp.dma_start(w[:], weight.rearrange("(k p) -> p k", p=P),
                             allow_slow_non_contiguous=True).then_inc(w_in, 16)
                sp.wait_ge(w_in, 16)

        @block.vector
        def _(dve):
            c = Chain(dve, chain_v)
            nc.vector.memset(eps[:, 0:1], LN_EPS)
            c.then(nc.vector.memset(eps[:, 1:2], rms_eps or 0.0))
            for i in range(NT):
                last = nc.vector.bn_stats(stats[:, i, :], src[:, i, :])
            c.then(last)
            for i in range(NT):
                last = nc.vector.bn_aggr(mv[:, i, :], stats[:, i, :])
            if layer:
                last.then_inc(sumsq, 1)
                dve.wait_ge(rooted, 1)
                c.then(nc.vector.reciprocal(rstd[:], root[:]))
                for i in range(NT):
                    last = nc.vector.tensor_scalar(XN[:, i, :], X[:, i, :], mv[:, i, 0:1], rstd[:, i:i + 1],
                                                   ALU.subtract, ALU.mult)
                if rms_eps is None:
                    last.then_inc(scaled, 1)
                else:
                    c.then(last)
                    c.then(nc.vector.tensor_tensor(rms[:], mv[:, :, 1], rstd[:], ALU.mult))
                    nc.vector.tensor_tensor(rms[:], rms[:], rstd[:], ALU.mult).then_inc(sumsq, 1)
            else:
                c.then(last)
                c.then(nc.vector.tensor_tensor(rms[:], mv[:, :, 0], mv[:, :, 0], ALU.mult))
                nc.vector.tensor_tensor(rms[:], rms[:], mv[:, :, 1], ALU.add).then_inc(sumsq, 1)
            if rms_eps is not None:
                dve.wait_ge(rooted, 1 + layer)
                c.then(nc.vector.reciprocal(rms[:], root[:]))
                for i in range(NT):
                    last = nc.vector.tensor_scalar(H[:, i, :], XN[:, i, :], rms[:, i:i + 1], None, ALU.mult)
                last.then_inc(scaled, 1)
            for q in range(2):
                dve.wait_ge(turned, q + 1)
                if weight is not None:
                    if q == 0:
                        dve.wait_ge(w_in, 16)
                    nc.vector.tensor_scalar(XT[:, 0, q * NB:(q + 1) * NB], PS[:, q, :], w[:, 0:1], None,
                                            ALU.mult)
                else:
                    nc.vector.tensor_copy(XT[:, 0, q * NB:(q + 1) * NB], PS[:, q, :])

        @block.scalar
        def _(act):
            if layer:
                act.wait_ge(sumsq, 1)
                nc.scalar.activation(root[:], mv[:, :, 1], ACT.Sqrt, bias=eps[:, 0:1]).then_inc(rooted, 1)
            if rms_eps is not None:
                act.wait_ge(sumsq, 1 + layer)
                nc.scalar.activation(root[:], rms[:], ACT.Sqrt, bias=eps[:, 1:2]).then_inc(rooted, 1)
            for q in range(2):
                act.wait_ge(turned, q + 3)
                if weight is not None:
                    act.wait_ge(w_in, 16)
                    nc.scalar.activation(XT[:, 1, q * NB:(q + 1) * NB], PS[:, 2 + q, :], ACT.Copy,
                                         scale=w[:, 1:2])
                else:
                    nc.scalar.copy(XT[:, 1, q * NB:(q + 1) * NB], PS[:, 2 + q, :])

        @block.tensor
        def _(pe):
            pe.wait_ge(scaled, 1)
            for k in range(KD):
                for q in range(2):
                    for i in range(4):
                        last = nc.tensor.transpose(PS[:, 2 * k + q, i * P:(i + 1) * P],
                                                   H[:, 4 * q + i, k * P:(k + 1) * P], core.ident[:])
                    last.then_inc(turned, 1)
    s.end()


def linear_attention(core):
    nc, a, X, XT, PS = core.nc, core.a, core.X, core.XT, core.PS
    s = Stage(core, "linattn")
    names = ["Wq", "Wk", "Wg", "Wv", "Wp"]
    W = s.sb("W", [P, 5, KD, D])
    FT = s.sb("FT", [P, 3, KD, N])
    V = s.sb("V", [P, NT, D])
    ST = s.sb("ST", [P, 2, 2, T])
    OT = s.sb("OT", [P, KD, N])
    w_in, mm, ev, v_mm, v_ev, s_mm, s_ev, o_mm, o_ev, y_mm, masked, y_ev = (s.sem(n) for n in (
        "w_in", "mm", "ev", "v_mm", "v_ev", "s_mm", "s_ev", "o_mm", "o_ev", "y_mm", "masked", "y_ev"))
    JOBS = [(i, m, n) for i in range(3) for m in range(KD) for n in range(NH)]
    NJ = len(JOBS)

    with nc.Block() as block:
        @block.sync
        def _(sp):
            for i, name in enumerate(names):
                sp.dma_start(W[:, i], a["L0_attn_a_" + name].rearrange("(k p) n -> p k n", p=P)).then_inc(w_in, 16)
            sp.wait_ge(w_in, 80)

        @block.tensor
        def _(pe):
            pe.wait_ge(w_in, 80)
            for g, (i, m, n) in enumerate(JOBS):
                if g >= 4:
                    pe.wait_ge(ev, g - 3)
                for k in range(KD):
                    last = nc.tensor.matmul(PS[:, g % 4, :], W[:, i, k, m * P:(m + 1) * P],
                                            XT[:, k, n * NB:(n + 1) * NB], start=(k == 0), stop=(k == KD - 1))
                last.then_inc(mm, 1)
            for i in range(NT):
                if i >= 4:
                    pe.wait_ge(v_ev, i - 3)
                for k in range(KD):
                    last = nc.tensor.matmul(PS[:, 4 + i % 4, 0:D], XT[:, k, i * P:(i + 1) * P],
                                            W[:, 3, k, :], start=(k == 0), stop=(k == KD - 1))
                last.then_inc(v_mm, 1)
            pe.wait_ge(ev, NJ)
            pe.wait_ge(v_ev, NT)

            def scores(b):
                if b >= 2:
                    pe.wait_ge(s_ev, b - 1)
                for j in range(2):
                    for k in range(KD):
                        last = nc.tensor.matmul(PS[:, b % 2, j * T + j * P:(j + 1) * T],
                                                FT[:, 1, k, b * T + j * P:b * T + (j + 1) * P],
                                                FT[:, 0, k, b * T + j * P:(b + 1) * T],
                                                start=(k == 0), stop=(k == KD - 1))
                last.then_inc(s_mm, 1)

            scores(0)
            for b in range(B):
                if b + 1 < B:
                    scores(b + 1)
                pe.wait_ge(masked, b + 1)
                if b >= 2:
                    pe.wait_ge(o_ev, b - 1)
                for m in range(KD):
                    nc.tensor.matmul(PS[:, 2 + b % 2, m * T:(m + 1) * T], V[:, 2 * b, m * P:(m + 1) * P],
                                     ST[:, b % 2, 0, :], start=True, stop=False)
                    last = nc.tensor.matmul(PS[:, 2 + b % 2, m * T + P:(m + 1) * T],
                                            V[:, 2 * b + 1, m * P:(m + 1) * P],
                                            ST[:, b % 2, 1, P:T], start=False, stop=True)
                last.then_inc(o_mm, 1)
            for i in range(NT):
                pe.wait_ge(o_ev, i // 2 + 1)
                if i >= 4:
                    pe.wait_ge(y_ev, i - 3)
                for k in range(KD):
                    last = nc.tensor.matmul(PS[:, 4 + i % 4, 0:D], OT[:, k, i * P:(i + 1) * P],
                                            W[:, 4, k, :], start=(k == 0), stop=(k == KD - 1))
                last.then_inc(y_mm, 1)

        @block.scalar
        def _(act):
            for g, (i, m, n) in enumerate(JOBS):
                act.wait_ge(mm, g + 1)
                nc.scalar.activation(FT[:, i, m, n * NB:(n + 1) * NB], PS[:, g % 4, :],
                                     ACT.Sigmoid if i == 2 else ACT.Silu).then_inc(ev, 1)
            for i in range(NT):
                act.wait_ge(v_mm, i + 1)
                nc.scalar.activation(V[:, i, :], PS[:, 4 + i % 4, 0:D], ACT.Silu).then_inc(v_ev, 1)
            for b in range(B):
                act.wait_ge(s_mm, b + 1)
                if b >= 2:
                    act.wait_ge(o_mm, b - 1)
                nc.scalar.copy(ST[:, b % 2, 0, :], PS[:, b % 2, 0:T])
                nc.scalar.copy(ST[:, b % 2, 1, P:T], PS[:, b % 2, T + P:2 * T]).then_inc(s_ev, 1)

        @block.gpsimd
        def _(pool):
            for b in range(B):
                pool.wait_ge(s_ev, b + 1)
                for j in range(2):
                    v = ST[:, b % 2, j, j * P:(j + 1) * P]
                    last = nc.gpsimd.affine_select(out=v, in_=v, compare_op=ALU.is_ge, fill=0.0, base=0,
                                                   pattern=[[1, P]], channel_multiplier=-1)
                last.then_inc(masked, 1)

        @block.vector
        def _(dve):
            for b in range(B):
                dve.wait_ge(o_mm, b + 1)
                if b == 0:
                    dve.wait_ge(ev, NJ)
                for m in range(KD):
                    last = nc.vector.tensor_tensor(OT[:, m, b * T:(b + 1) * T], PS[:, 2 + b % 2, m * T:(m + 1) * T],
                                                   FT[:, 2, m, b * T:(b + 1) * T], ALU.mult)
                last.then_inc(o_ev, 1)
            for i in range(NT):
                dve.wait_ge(y_mm, i + 1)
                nc.vector.tensor_tensor(X[:, i, :], PS[:, 4 + i % 4, 0:D], X[:, i, :],
                                        ALU.add).then_inc(y_ev, 1)
    s.end()


def top2(core, s, dve, c, p, weights, rank):
    nc = core.nc
    bc = lambda t: t[:].unsqueeze(2).broadcast_to([P, NT, E])
    m = s.top_m
    eq = s.top_eq
    oh = s.top_oh
    rest = s.top_rest
    src = p
    for r in range(2):
        c.then(nc.vector.tensor_reduce(m[:], src[:], AX.X, ALU.max))
        c.then(nc.vector.tensor_tensor(eq[:], src[:], bc(m), ALU.is_equal))
        c.then(nc.vector.tensor_tensor(eq[:], eq[:], rank[:].unsqueeze(1).broadcast_to([P, NT, E]), ALU.mult))
        c.then(nc.vector.tensor_reduce(m[:], eq[:], AX.X, ALU.max))
        c.then(nc.vector.tensor_tensor(oh[:, r], eq[:], bc(m), ALU.is_equal))
        if r == 0:
            c.then(nc.vector.scalar_tensor_tensor(rest[:], oh[:, 0], -2.0, src[:], ALU.mult, ALU.add))
            src = rest
    c.then(nc.vector.tensor_tensor(oh[:, 0], oh[:, 0], oh[:, 1], ALU.add))
    return nc.vector.tensor_tensor(weights, oh[:, 0], p[:], ALU.mult)


def moe(core, a="L0_ffn_"):
    nc, args, X, XT, PS = core.nc, core.a, core.X, core.XT, core.PS
    I = 512
    MI = I // P
    SOFTCAP = 30.0
    s = Stage(core, "moe")
    WG = s.sb("WG", [P, KD, E])
    logit = s.sb("logit", [P, NT, E])
    prob = s.sb("prob", [P, NT, E])
    weight = s.sb("weight", [P, E, NT])
    rank = s.sb("rank", [P, E])
    s.top_m = s.sb("top_m", [P, NT])
    s.top_eq = s.sb("top_eq", [P, NT, E])
    s.top_oh = s.sb("top_oh", [P, 2, NT, E])
    s.top_rest = s.sb("top_rest", [P, NT, E])
    mx = s.sb("mx", [P, NT])
    WW = 2 * KD * I + MI * D
    W = s.sb("W", [P, 2, WW])
    WP = [s.sb(f"WP{q}", [P, 2, WW], PART) for q in range(2)]
    XP = [s.sb(f"XP{q}", [P, KD, N], PART) for q in range(2)]
    HP = [s.sb(f"HP{q}", [P, MI, N], PART) for q in range(2)]
    SG = s.sb("SG", [P, 4, NB])
    HF = s.sb("HF", [P, 4, NB])
    up_w = lambda q, r, i, k, m: WP[q][:, r, (i * KD + k) * I + m * P:(i * KD + k) * I + (m + 1) * P]
    down_w = lambda q, r, k: WP[q][:, r, 2 * KD * I + k * D:2 * KD * I + (k + 1) * D]
    PASSES = ((0, 0), (0, 1), (1, 0))
    g_in, r_mm, tanh_d, sub_d, exp_d, chain_v, route_d = (s.sem(n) for n in (
        "g_in", "r_mm", "tanh_d", "sub_d", "exp_d", "chain_v", "route_d"))
    w_in = [s.sem("w_in0"), s.sem("w_in1")]
    up_mm, silu_d, h_d, dn_mm, dn_d = (s.sem(n) for n in ("up_mm", "silu_d", "h_d", "dn_mm", "dn_d"))
    xh_d, xl_d, wh_d, wl_d, hh_d, hl_d = (s.sem(n) for n in ("xh_d", "xl_d", "wh_d", "wl_d", "hh_d", "hl_d"))
    G = NH * MI

    with nc.Block() as block:
        @block.sync
        def _(sp):
            sp.dma_start(WG[:], args[a + "w_gate"].rearrange("(k p) e -> p k e", p=P)).then_inc(g_in, 16)

            def load(e, r):
                for i, (w, k, n) in enumerate((("w1", KD, I), ("w3", KD, I), ("w2", MI, D))):
                    sp.dma_start(W[:, r, i * KD * I:(i + 1) * KD * I].rearrange("p (k n) -> p k n", k=k),
                                 args[a + w][bass.ds(e, 1)].rearrange("o (k p) n -> p (o k) n", p=P)).then_inc(w_in[r], 16)

            load(0, 0)
            load(1, 1)
            with sp.Fori(1, E // 2) as j:
                for r in range(2):
                    sp.wait_ge(wl_d, 2 * j + r - 1)
                    load(2 * j + r, r)
            sp.wait_ge(g_in, 16)
            for r in range(2):
                sp.wait_ge(w_in[r], 48 * (E // 2))

        @block.tensor
        def _(pe):
            pe.wait_ge(g_in, 16)
            for i in range(NT):
                for k in range(KD):
                    last = nc.tensor.matmul(PS[:, 7, i * E:(i + 1) * E], XT[:, k, i * P:(i + 1) * P],
                                            WG[:, k, :], start=(k == 0), stop=(k == KD - 1))
            last.then_inc(r_mm, 1)
            pe.wait_ge(tanh_d, 1)

            pe.wait_ge(xh_d, 1)
            pe.wait_ge(xl_d, 1)

            def expert(j, r, first):
                pe.wait_ge(wh_d, 2 * j + r + 1)
                pe.wait_ge(wl_d, 2 * j + r + 1)
                for n in range(NH):
                    for m in range(MI):
                        g = n * MI + m
                        if not (first and g < 2):
                            pe.wait_ge(h_d, (2 * j + r) * G + g - 1)
                        for i in range(2):
                            for k in range(KD):
                                for step, (qw, qx) in enumerate(PASSES):
                                    last = nc.tensor.matmul(PS[:, 2 * (g % 2) + i, :], up_w(qw, r, i, k, m),
                                                            XP[qx][:, k, n * NB:(n + 1) * NB], start=(k + step == 0),
                                                            stop=(k == KD - 1 and step == 2))
                        last.then_inc(up_mm, 1)
                for i in range(NT):
                    if i % 4 == 0:
                        pe.wait_ge(hh_d, (2 * j + r) * G + MI * (i // 4 + 1))
                        pe.wait_ge(hl_d, (2 * j + r) * G + MI * (i // 4 + 1))
                    if not (first and i < 4):
                        pe.wait_ge(dn_d, (2 * j + r) * NT + i - 3)
                    for k in range(MI):
                        for step, (qw, qx) in enumerate(PASSES):
                            last = nc.tensor.matmul(PS[:, 4 + i % 4, 0:D], HP[qx][:, k, i * P:(i + 1) * P],
                                                    down_w(qw, r, k), start=(k + step == 0),
                                                    stop=(k == MI - 1 and step == 2))
                    last.then_inc(dn_mm, 1)

            expert(0, 0, True)
            expert(0, 1, False)
            with pe.Fori(1, E // 2) as j:
                expert(j, 0, False)
                expert(j, 1, False)

        @block.scalar
        def _(act):
            act.wait_ge(r_mm, 1)
            nc.scalar.activation(logit[:], PS[:, 7, 0:NT * E].rearrange("p (i e) -> p i e", e=E), ACT.Tanh,
                                 scale=1.0 / SOFTCAP).then_inc(tanh_d, 1)
            act.wait_ge(sub_d, 1)
            nc.scalar.activation(prob[:], logit[:], ACT.Exp, scale=SOFTCAP).then_inc(exp_d, 1)

            nc.scalar.copy(XP[0][:], XT[:]).then_inc(xh_d, 1)

            def split(j, r, first):
                act.wait_ge(w_in[r], 48 * j + 48)
                if not first:
                    act.wait_ge(dn_mm, NT * (2 * j + r) - NT)
                nc.scalar.copy(WP[0][:, r], W[:, r]).then_inc(wh_d, 1)

            def hidden(j, r, g):
                n, m = g // MI, g % MI
                act.wait_ge(h_d, (2 * j + r) * G + g + 1)
                nc.scalar.copy(HP[0][:, m, n * NB:(n + 1) * NB], HF[:, g % 4, :]).then_inc(hh_d, 1)

            def expert(j, r, first):
                for g in range(G):
                    act.wait_ge(up_mm, (2 * j + r) * G + g + 1)
                    if not (first and g < 4):
                        act.wait_ge(h_d, (2 * j + r) * G + g - 3)
                    nc.scalar.activation(SG[:, g % 4, :], PS[:, 2 * (g % 2), :], ACT.Silu).then_inc(silu_d, 1)
                    if g:
                        hidden(j, r, g - 1)
                hidden(j, r, G - 1)

            split(0, 0, True)
            split(0, 1, True)
            expert(0, 0, True)
            with act.Fori(1, E // 2) as j:
                split(j, 0, False)
                expert(j - 1, 1, False)
                split(j, 1, False)
                expert(j, 0, False)
            expert(E // 2 - 1, 1, False)

        @block.gpsimd
        def _(pool):
            pool.wait_ge(xh_d, 1)
            nc.gpsimd.tensor_tensor(XP[1][:], XT[:], XP[0][:], ALU.subtract).then_inc(xl_d, 1)

            def split(j, r, first):
                pool.wait_ge(wh_d, 2 * j + r + 1)
                nc.gpsimd.tensor_tensor(WP[1][:, r], W[:, r], WP[0][:, r], ALU.subtract).then_inc(wl_d, 1)

            def expert(j, r):
                for g in range(G):
                    n, m = g // MI, g % MI
                    pool.wait_ge(hh_d, (2 * j + r) * G + g + 1)
                    nc.gpsimd.tensor_tensor(HP[1][:, m, n * NB:(n + 1) * NB], HF[:, g % 4, :],
                                            HP[0][:, m, n * NB:(n + 1) * NB], ALU.subtract).then_inc(hl_d, 1)

            split(0, 0, True)
            split(0, 1, True)
            expert(0, 0)
            with pool.Fori(1, E // 2) as j:
                split(j, 0, False)
                expert(j - 1, 1)
                split(j, 1, False)
                expert(j, 0)
            expert(E // 2 - 1, 1)

        @block.vector
        def _(dve):
            c = Chain(dve, chain_v)
            for e in range(E):
                last = nc.vector.memset(rank[:, e:e + 1], float(E - e))
            c.then(last)
            dve.wait_ge(tanh_d, 1)
            c.then(nc.vector.tensor_reduce(mx[:], logit[:], AX.X, ALU.max))
            nc.vector.tensor_tensor(logit[:], logit[:], mx[:].unsqueeze(2).broadcast_to([P, NT, E]),
                                    ALU.subtract).then_inc(sub_d, 1)
            dve.wait_ge(exp_d, 1)
            c.then(nc.vector.tensor_reduce(mx[:], prob[:], AX.X, ALU.add))
            c.then(nc.vector.reciprocal(mx[:], mx[:]))
            c.then(nc.vector.tensor_tensor(prob[:], prob[:], mx[:].unsqueeze(2).broadcast_to([P, NT, E]), ALU.mult))
            c.then(top2(core, s, dve, c, prob, weight[:].rearrange("p e i -> p i e"), rank))

            def expert(j, r, first):
                for g in range(G):
                    dve.wait_ge(silu_d, (2 * j + r) * G + g + 1)
                    if not (first and g < 4):
                        dve.wait_ge(hl_d, (2 * j + r) * G + g - 3)
                    nc.vector.tensor_tensor(HF[:, g % 4, :], SG[:, g % 4, :],
                                            PS[:, 2 * (g % 2) + 1, :], ALU.mult).then_inc(h_d, 1)
                for i in range(NT):
                    dve.wait_ge(dn_mm, (2 * j + r) * NT + i + 1)
                    nc.vector.scalar_tensor_tensor(X[:, i, :], PS[:, 4 + i % 4, 0:D],
                                                   weight[:, bass.ds(2 * j + r, 1), i], X[:, i, :],
                                                   ALU.mult, ALU.add).then_inc(dn_d, 1)

            expert(0, 0, True)
            expert(0, 1, False)
            with dve.Fori(1, E // 2) as j:
                expert(j, 0, False)
                expert(j, 1, False)
    s.end()


def conv_scan(core):
    nc, a, X, XN, XT, PS = core.nc, core.a, core.X, core.XN, core.XT, core.PS
    TAPS = 4
    CH = 32
    HD = 16
    HEADS = D // HD
    C = T // CH
    ROWS = KD * B
    s = Stage(core, "cscan")
    flat = lambda t: t[:].rearrange("p k n -> p (k n)")
    chunks = lambda t: t[:].rearrange("p k (b c j) -> p (k b c) j", b=B, j=CH)
    XP = s.sb("XP", [P, KD, B, T + TAPS - 1])
    XC = s.sb("XC", [P, KD, N])
    CW = s.sb("CW", [P, KD, TAPS])
    CB = s.sb("CB", [P, KD])
    DB = s.sb("DB", [P, KD])
    IP = s.sb("IP", [P, KD, 4 * D])
    OP = s.sb("OP", [P, KD, D])
    HM = s.sb("HM", [P, KD, HEADS])
    IM = s.sb("IM", [P, HD])
    KM = s.sb("KM", [P, KD, D])
    TRIG = s.sb("TRIG", [P, 2, T])
    ONE = s.sb("ONE", [P, 1])
    KEEP = s.sb("KEEP", [P, KD * N])
    KEEPC = s.sb("KEEPC", [P, ROWS * C])
    A1 = s.sb("A1", [P, KD, N])
    A2 = s.sb("A2", [P, KD, N])
    DT = s.sb("DT", [P, KD, N])
    VR = s.sb("VR", [P, KD, N])
    GT = s.sb("GT", [P, KD, N])
    VS = s.sb("VS", [P, 2, NB])
    CK = s.sb("CK", [P, 8, ROWS, C])
    w_in, c_in, ready, conv_d, xc_d, mm, dt_ev, rot_v, rot_s, g_ev, sp1, dt_d, clip_d, exp_d, cexp, fin, mix_mm, mix_d, y_mm, y_ev, chain_v, chain_p, swap_d, res_d = (
        s.sem(n) for n in (
            "w_in", "c_in", "ready", "conv_d", "xc_d", "mm", "dt_ev", "rot_v", "rot_s", "g_ev", "sp1", "dt_d", "clip_d",
            "exp_d", "cexp", "fin", "mix_mm", "mix_d", "y_mm", "y_ev", "chain_v", "chain_p", "swap_d", "res_d"))
    JOBS = [(0, m, n) for m in range(KD) for n in range(NH)] + \
           [(i, m, n) for m in range(KD) for n in range(NH) for i in (1, 3)] + \
           [(2, m, n) for m in range(KD) for n in range(NH)]
    TILES = KD * NH
    GBANK = lambda g: 4 + g % 4 if g >= 3 * TILES else g % 4
    CUM = s.sb("CUM", [P, KD, N])

    with nc.Block() as block:
        @block.sync
        def _(sp):
            col = lambda t: t.rearrange("(k p) -> p k", p=P)
            pre = "L0_attn_b_"
            sp.dma_start(CW[:], a[pre + "conv_w"].rearrange("(k p) o t -> p k (o t)", p=P)).then_inc(c_in, 16)
            sp.dma_start(CB[:], col(a[pre + "conv_b"]), allow_slow_non_contiguous=True).then_inc(c_in, 16)
            sp.dma_start(DB[:], col(a[pre + "dt_bias"]), allow_slow_non_contiguous=True).then_inc(c_in, 16)
            sp.dma_start(IP[:, :, 0:3 * D], a[pre + "in_proj_w"].rearrange("(k p) n -> p k n", p=P)).then_inc(w_in, 16)
            sp.dma_start(OP[:], a[pre + "out_proj_w"].rearrange("(k p) n -> p k n", p=P)).then_inc(w_in, 16)
            sp.dma_start(HM[:], a["L0_attn_b_head_rows"].rearrange("(k p) n -> p k n", p=P)).then_inc(w_in, 16)
            sp.dma_start(TRIG[:], a["trig0"].rearrange("c p t -> p c t")).then_inc(w_in, 16)
            sp.wait_ge(w_in, 64)
            sp.wait_ge(c_in, 48)

        @block.gpsimd
        def _(pool):
            c = Chain(pool, chain_p)
            nc.gpsimd.memset(XP[:, :, :, 0:TAPS - 1], 0.0).then_inc(ready, 1)
            c.then(nc.gpsimd.memset(KEEP[:], 1.0))
            c.then(nc.gpsimd.memset(KEEPC[:], 1.0))
            nc.gpsimd.memset(KEEP[:].rearrange("p (c j) -> p c j", j=CH)[:, :, 0:1], 0.0)
            nc.gpsimd.memset(KEEPC[:].rearrange("p (c j) -> p c j", j=C)[:, :, 0:1], 0.0)
            c.then(nc.gpsimd.memset(ONE[:], 1.0))
            pool.wait_ge(w_in, 64)
            for k in range(KD):
                v = IP[:, k, D:2 * D].rearrange("p (h a d) -> p h a d", a=2, d=HD // 2)
                w = IP[:, k, 3 * D:4 * D].rearrange("p (h a d) -> p h a d", a=2, d=HD // 2)
                nc.gpsimd.tensor_copy(w[:, :, 0], v[:, :, 1])
                last = nc.gpsimd.tensor_copy(w[:, :, 1], v[:, :, 0])
            last.then_inc(swap_d, 1)
            nc.gpsimd.tensor_tensor(X[:], X[:], XN[:], ALU.add).then_inc(res_d, 1)

        @block.vector
        def _(dve):
            c = Chain(dve, chain_v)
            c.then(nc.vector.tensor_scalar(XP[:, :, :, TAPS - 1:].rearrange("p k b t -> p (k b) t"),
                                           XT[:].rearrange("p k (b t) -> p (k b) t", b=B), 60000.0, -60000.0,
                                           ALU.min, ALU.max))
            dve.wait_ge(ready, 1)
            dve.wait_ge(c_in, 48)
            acc = A1
            for tau in range(TAPS):
                for k in range(KD):
                    x = XP[:, k, :, tau:tau + T]
                    o = acc[:, k, :].rearrange("p (b t) -> p b t", b=B)
                    if tau == 0:
                        last = nc.vector.tensor_scalar(o, x, CW[:, k, 0:1], None, ALU.mult)
                    else:
                        last = nc.vector.scalar_tensor_tensor(o, x, CW[:, k, tau:tau + 1], o, ALU.mult, ALU.add)
                    if tau == TAPS - 1:
                        last.then_inc(conv_d, 1)
                if tau < TAPS - 1:
                    c.then(last)
            c.then(nc.vector.tensor_reduce(IM[:], core.ident[:].rearrange("p (h d) -> p d h", d=HD), AX.X, ALU.add))
            dve.wait_ge(w_in, 64)
            for k in range(KD):
                c.then(nc.vector.tensor_tensor(KM[:, k].rearrange("p (m d) -> p m d", d=HD),
                                               HM[:, k].unsqueeze(2).broadcast_to([P, HEADS, HD]),
                                               IM[:].unsqueeze(1).broadcast_to([P, HEADS, HD]), ALU.mult))
            trig = lambda q: TRIG[:, q].unsqueeze(1).broadcast_to([P, NB // T, T])
            two = lambda t: t.rearrange("p (b t) -> p b t", t=T)
            for g, (i, m, n) in enumerate(JOBS):
                if i == 1:
                    dve.wait_ge(mm, g + 1)
                    nc.vector.tensor_tensor(two(VR[:, m, n * NB:(n + 1) * NB]), two(PS[:, g % 4, :]), trig(0),
                                            ALU.mult).then_inc(rot_v, 1)
                if i == 3:
                    dve.wait_ge(mm, g + 1)
                    r = (g - TILES) // 2 % 2
                    c.then(nc.vector.tensor_tensor(two(VS[:, r]), two(PS[:, g % 4, :]), trig(1), ALU.mult))
                    o = VR[:, m, n * NB:(n + 1) * NB]
                    nc.vector.tensor_tensor(o, o, VS[:, r], ALU.add).then_inc(rot_s, 1)
            dve.wait_ge(sp1, 2)
            c.then(nc.vector.tensor_tensor(flat(DT), flat(A1), flat(A2), ALU.add))
            c.then(nc.vector.tensor_scalar(flat(DT), flat(DT), 1e-3, 2.0, ALU.max, ALU.min))
            c.then(nc.vector.tensor_tensor_scan(flat(A1), KEEP[:], flat(DT), 0.0, ALU.mult, ALU.add))
            c.then(nc.vector.tensor_scalar(flat(A1), flat(A1), 20.0, 0.0, ALU.min, ALU.max))
            nc.vector.tensor_tensor(chunks(A2), chunks(A1), chunks(A1)[:, :, 0:1].broadcast_to([P, ROWS * C, CH]),
                                    ALU.subtract).then_inc(clip_d, 1)
            nc.vector.tensor_tensor(flat(VR), flat(VR), flat(DT), ALU.mult).then_inc(dt_d, 1)
            dve.wait_ge(dt_d, 1)
            ck = lambda q: CK[:, q].rearrange("p r c -> p (r c)")
            c.then(nc.vector.tensor_copy(ck(2), chunks(A1)[:, :, CH - 1]))
            c.then(nc.vector.tensor_tensor_scan(ck(0), KEEPC[:], ck(2), 0.0, ALU.mult, ALU.add))
            c.then(nc.vector.tensor_scalar(ck(0), ck(0), 80.0, 0.0, ALU.min, ALU.max))
            c.then(nc.vector.tensor_tensor(CK[:, 1], CK[:, 0], CK[:, 0, :, 0:1].broadcast_to([P, ROWS, C]), ALU.subtract))
            nc.vector.tensor_scalar(ck(1), ck(1), 0.0, 20.0, ALU.max, ALU.min).then_inc(clip_d, 1)
            dve.wait_ge(exp_d, 1)
            c.then(nc.vector.tensor_tensor(flat(VR), flat(VR), flat(DT), ALU.mult))
            c.then(nc.vector.tensor_tensor_scan(flat(CUM), KEEP[:], flat(VR), 0.0, ALU.mult, ALU.add))
            dve.wait_ge(exp_d, 2)
            c.then(nc.vector.tensor_tensor(flat(VR), flat(CUM), flat(A2), ALU.mult))
            dve.wait_ge(cexp, 2)
            c.then(nc.vector.tensor_tensor(ck(5), chunks(VR)[:, :, CH - 1], ck(3), ALU.mult))
            c.then(nc.vector.memset(CK[:, 6, :, 0:1], 0.0))
            c.then(nc.vector.tensor_copy(CK[:, 6, :, 1:C], CK[:, 5, :, 0:C - 1]))
            c.then(nc.vector.tensor_tensor_scan(ck(7), KEEPC[:], ck(6), 0.0, ALU.mult, ALU.add))
            c.then(nc.vector.tensor_tensor(ck(7), ck(7), ck(4), ALU.mult))
            dve.wait_ge(exp_d, 3)
            c.then(nc.vector.tensor_tensor(chunks(A1), chunks(A1), ck(7).unsqueeze(2).broadcast_to([P, ROWS * C, CH]),
                                           ALU.mult))
            nc.vector.tensor_tensor(flat(VR), flat(VR), flat(A1), ALU.add).then_inc(fin, 1)
            dve.wait_ge(g_ev, TILES)
            for g in range(TILES):
                m, n = g // NH, g % NH
                dve.wait_ge(mix_mm, g + 1)
                o = GT[:, m, n * NB:(n + 1) * NB]
                nc.vector.tensor_tensor(o, PS[:, g % 4, :], o, ALU.mult).then_inc(mix_d, 1)
            dve.wait_ge(res_d, 1)
            for i in range(NT):
                dve.wait_ge(y_mm, i + 1)
                nc.vector.tensor_tensor(X[:, i, :], PS[:, 4 + i % 4, 0:D], X[:, i, :],
                                        ALU.add).then_inc(y_ev, 1)

        @block.scalar
        def _(act):
            act.wait_ge(c_in, 48)
            for k in range(KD):
                act.wait_ge(conv_d, k + 1)
                nc.scalar.activation(XC[:, k, :], A1[:, k, :], ACT.Silu, bias=CB[:, k:k + 1]).then_inc(xc_d, 1)
            act.wait_ge(xc_d, KD)
            for g, (i, m, n) in enumerate(JOBS[:TILES]):
                act.wait_ge(mm, g + 1)
                cols = slice(n * NB, (n + 1) * NB)
                nc.scalar.activation(A2[:, m, cols], PS[:, g % 4, :], ACT.Abs, bias=DB[:, m:m + 1])
                nc.scalar.activation(A1[:, m, cols], PS[:, g % 4, :], ACT.Relu, bias=DB[:, m:m + 1]).then_inc(dt_ev, 1)
            act.wait_ge(dt_ev, TILES)
            nc.scalar.activation(flat(A2), flat(A2), ACT.Exp, scale=-1.0).then_inc(sp1, 1)
            act.wait_ge(chain_p, 3)
            act.wait_ge(sp1, 1)
            nc.scalar.activation(flat(A2), flat(A2), ACT.Ln, bias=ONE[:]).then_inc(sp1, 1)
            act.wait_ge(clip_d, 1)
            act.wait_ge(dt_d, 1)
            nc.scalar.activation(flat(DT), flat(A2), ACT.Exp).then_inc(exp_d, 1)
            act.wait_ge(exp_d, 1)
            nc.scalar.activation(flat(A2), flat(A2), ACT.Exp, scale=-1.0).then_inc(exp_d, 1)
            act.wait_ge(clip_d, 2)
            nc.scalar.activation(CK[:, 3], CK[:, 1], ACT.Exp).then_inc(cexp, 1)
            nc.scalar.activation(CK[:, 4], CK[:, 1], ACT.Exp, scale=-1.0).then_inc(cexp, 1)
            nc.scalar.activation(flat(A1), flat(A1), ACT.Exp, scale=-1.0).then_inc(exp_d, 1)
            for g, (i, m, n) in list(enumerate(JOBS))[3 * TILES:]:
                act.wait_ge(mm, g + 1)
                nc.scalar.activation(GT[:, m, n * NB:(n + 1) * NB], PS[:, GBANK(g), :], ACT.Sigmoid).then_inc(g_ev, 1)

        @block.tensor
        def _(pe):
            pe.wait_ge(w_in, 64)
            pe.wait_ge(xc_d, KD)
            for g, (i, m, n) in enumerate(JOBS):
                if 4 <= g < 3 * TILES:
                    old = g - 4
                    if old < TILES:
                        pe.wait_ge(dt_ev, old + 1)
                    elif JOBS[old][0] == 1:
                        pe.wait_ge(rot_v, (old - TILES) // 2 + 1)
                    else:
                        pe.wait_ge(rot_s, (old - TILES) // 2 + 1)
                if i == 3:
                    pe.wait_ge(swap_d, 1)
                for k in range(KD):
                    last = nc.tensor.matmul(PS[:, GBANK(g), :], IP[:, k, i * D + m * P:i * D + (m + 1) * P],
                                            XC[:, k, n * NB:(n + 1) * NB], start=(k == 0), stop=(k == KD - 1))
                last.then_inc(mm, 1)
            pe.wait_ge(fin, 1)
            for g in range(TILES):
                m, n = g // NH, g % NH
                for k in range(KD):
                    last = nc.tensor.matmul(PS[:, g % 4, :], KM[:, k, m * P:(m + 1) * P],
                                            VR[:, k, n * NB:(n + 1) * NB], start=(k == 0), stop=(k == KD - 1))
                last.then_inc(mix_mm, 1)
            pe.wait_ge(mix_d, TILES)
            pe.wait_ge(g_ev, TILES)
            for i in range(NT):
                if i >= 4:
                    pe.wait_ge(y_ev, i - 3)
                for k in range(KD):
                    last = nc.tensor.matmul(PS[:, 4 + i % 4, 0:D], GT[:, k, i * P:(i + 1) * P],
                                            OP[:, k, :], start=(k == 0), stop=(k == KD - 1))
                last.then_inc(y_mm, 1)
    s.end()


def softmax_attention(core, q, k, v, bq, bk, bv, wo, bo, rope, swapped, dst):
    nc, XT, PS = core.nc, core.XT, core.PS
    HD = 16
    HEADS = D // HD
    HK = HEADS // KD
    s = Stage(core, "attn")
    W = s.sb("W", [P, 4, KD, D])
    WS = s.sb("WS", [P, 2, KD, D])
    BC = s.sb("BC", [P, 2, KD])
    BS = s.sb("BS", [P, 2, KD])
    BV = s.sb("BV", [P, 2, D])
    TRIG = s.sb("TRIG", [P, 2, T])
    QK = s.sb("QK", [P, 2, KD, N])
    RS = s.sb("RS", [P, 2, NB])
    HMASK = s.sb("HMASK", [P, HK])
    KM = s.sb("KM", [P, KD, HK, N])
    V = s.sb("V", [P, NT, HEADS, HD + 1])
    LOW = s.sb("LOW", [P, 4, P], BF16)
    IB = s.sb("IB", [P, P], BF16)
    NM = s.sb("NM", [P, 4, 4])
    PR = s.sb("PR", [P, 4, NB])
    PT = s.sb("PT", [P, 4, NB])
    REC = s.sb("REC", [P, 2, HEADS])
    ON = s.sb("ON", [P, NT, HEADS, HD])
    OT = s.sb("OT", [P, KD, N])
    w_in, b_in, consts, mm, ev, rot, km_d, v_mm, v_ev, s_mm, max_d, exp_d, t_mm, t_ev, o_mm, o_ev, ot_mm, ot_ev, y_mm, y_ev, chain_v, chain_p, swap_d, bo_d, rs_d = (
        s.sem(n) for n in (
            "w_in", "b_in", "consts", "mm", "ev", "rot", "km_d", "v_mm", "v_ev", "s_mm", "max_d", "exp_d", "t_mm", "t_ev",
            "o_mm", "o_ev", "ot_mm", "ot_ev", "y_mm", "y_ev", "chain_v", "chain_p", "swap_d", "bo_d", "rs_d"))
    COPIES = 2 if rope is not None else 1
    JOBS = [(i, m, n, c) for i in range(2) for m in range(KD) for n in range(NH) for c in range(COPIES)]
    NJ = len(JOBS)
    UNITS = []
    for b in range(B):
        for qt in range(2):
            per = 4 if qt == 0 else 2
            for kt in range(KD):
                for h in range(0, HK, per):
                    UNITS.append((b, qt, kt, h, per))
    NU = len(UNITS)
    W_IN = 16 * (4 + (rope is not None))
    B_IN = 16 * (3 + (bo is not None) + 2 * (rope is not None))
    k_ready = rot if rope is not None else ev
    k_count = lambda kk: NH * KD + NH * (kk + 1)
    km_pool = s.sem("km_pool")
    last_unit = {2 * b + qt: u for u, (b, qt, kt, h, per) in enumerate(UNITS)}
    first_unit = {}
    for u, (b, qt, kt, h, per) in enumerate(UNITS):
        first_unit.setdefault(2 * b + qt, u)

    with nc.Block() as block:
        @block.sync
        def _(sp):
            for i, w in enumerate((q, k, v, wo)):
                sp.dma_start(W[:, i], w.rearrange("(k p) n -> p k n", p=P)).then_inc(w_in, 16)
            if rope is not None:
                sp.dma_start(TRIG[:], rope.rearrange("c p t -> p c t")).then_inc(w_in, 16)
                for i, t in enumerate(swapped):
                    sp.dma_start(BS[:, i], t.rearrange("(k p) -> p k", p=P),
                                 allow_slow_non_contiguous=True).then_inc(b_in, 16)
            for i, t in enumerate((bq, bk)):
                sp.dma_start(BC[:, i], t.rearrange("(k p) -> p k", p=P),
                             allow_slow_non_contiguous=True).then_inc(b_in, 16)
            row = lambda t: t.rearrange("(o n) -> o n", o=1).broadcast_to([P, D])
            sp.dma_start(BV[:, 0], row(bv)).then_inc(b_in, 16)
            if bo is not None:
                sp.dma_start(BV[:, 1], row(bo)).then_inc(b_in, 16)
            sp.wait_ge(w_in, W_IN)
            sp.wait_ge(b_in, B_IN)

        @block.gpsimd
        def _(pool):
            c = Chain(pool, chain_p)
            c.then(nc.gpsimd.memset(LOW[:], 0.0))
            nc.gpsimd.memset(V[:, :, :, HD:], 1.0).then_inc(consts, 1)
            c.then(nc.gpsimd.tensor_copy(IB[:], core.ident[:]))
            c.then(nc.gpsimd.affine_select(out=LOW[:], in_=LOW[:], compare_op=ALU.is_ge, fill=-1e30, base=0,
                                           pattern=[[0, 4], [-1, P]], channel_multiplier=1))
            nc.gpsimd.memset(NM[:], 0.0).then_inc(consts, 1)
            if rope is not None:
                pool.wait_ge(w_in, W_IN)
                for i in range(2):
                    for kk in range(KD):
                        x = W[:, i, kk].rearrange("p (h a d) -> p h a d", a=2, d=HD // 2)
                        y = WS[:, i, kk].rearrange("p (h a d) -> p h a d", a=2, d=HD // 2)
                        nc.gpsimd.tensor_copy(y[:, :, 0], x[:, :, 1])
                        last = nc.gpsimd.tensor_copy(y[:, :, 1], x[:, :, 0])
                last.then_inc(swap_d, 1)
            if bo is not None:
                pool.wait_ge(b_in, B_IN)
                nc.gpsimd.tensor_tensor(dst[:], dst[:], BV[:, 1].unsqueeze(1).broadcast_to([P, NT, D]),
                                        ALU.add).then_inc(bo_d, 1)
            pool.wait_ge(km_d, 1)
            for kk in range(KD):
                pool.wait_ge(k_ready, k_count(kk))
                for h in range(0, 2):
                    last = nc.gpsimd.tensor_scalar(KM[:, kk, h], QK[:, 1, kk], HMASK[:, h:h + 1], None, ALU.mult)
                last.then_inc(km_pool, 1)

        @block.tensor
        def _(pe):
            pe.wait_ge(w_in, W_IN)
            for g, (i, m, n, cp) in enumerate(JOBS):
                if cp == 1 and g == 1:
                    pe.wait_ge(swap_d, 1)
                if g >= 4:
                    pe.wait_ge(ev, g - 3)
                w = WS if cp else W
                for kk in range(KD):
                    last = nc.tensor.matmul(PS[:, g % 4, :], w[:, i, kk, m * P:(m + 1) * P],
                                            XT[:, kk, n * NB:(n + 1) * NB], start=(kk == 0), stop=(kk == KD - 1))
                last.then_inc(mm, 1)
            for i in range(NT):
                if i >= 4:
                    pe.wait_ge(v_ev, i - 3)
                for kk in range(KD):
                    last = nc.tensor.matmul(PS[:, 4 + i % 4, 0:D], XT[:, kk, i * P:(i + 1) * P],
                                            W[:, 2, kk, :], start=(kk == 0), stop=(kk == KD - 1))
                last.then_inc(v_mm, 1)
            pe.wait_ge(ev, NJ)
            pe.wait_ge(v_ev, NT)
            pe.wait_ge(km_d, 3)
            pe.wait_ge(km_pool, KD)
            pe.wait_ge(chain_p, 3)

            def scores(u):
                b, qt, kt, h, per = UNITS[u]
                bank = PS[:, u % 3, :]
                if u >= 3:
                    pe.wait_ge(exp_d, u - 2)
                keys = (qt + 1) * P
                nc.tensor.matmul(bank, QK[:, 0, kt, b * T + qt * P:b * T + (qt + 1) * P],
                                 KM[:, kt, h:h + per, b * T:b * T + keys], start=True, stop=False)
                last = nc.tensor.matmul(bank.rearrange("p (h j) -> p h j", h=per)[:, :, qt * P:keys],
                                        IB[:], LOW[:, 0:per, :], start=False, stop=True)
                last.then_inc(s_mm, 1)

            def turn(u):
                pe.wait_ge(exp_d, u + 1)
                if u >= 2:
                    pe.wait_ge(t_ev, u - 1)
                for i in range(4):
                    last = nc.tensor.transpose(PS[:, 3 + u % 2, i * P:(i + 1) * P],
                                               PR[:, u % 4, i * P:(i + 1) * P], core.ident[:])
                last.then_inc(t_mm, 1)

            def values(u):
                b, qt, kt, h, per = UNITS[u]
                i = 2 * b + qt
                pe.wait_ge(t_ev, u + 1)
                if i >= 2 and u == first_unit[i]:
                    pe.wait_ge(o_ev, i - 1)
                for j in range(per):
                    o = PS[:, 5 + i % 2, (kt * HK + h + j) * (HD + 1):(kt * HK + h + j + 1) * (HD + 1)]
                    for t in range(qt + 1):
                        last = nc.tensor.matmul(o, PT[:, u % 4, (j * (qt + 1) + t) * P:(j * (qt + 1) + t + 1) * P],
                                                V[:, 2 * b + t, kt * HK + h + j, :], start=(t == 0), stop=(t == qt))
                last.then_inc(o_mm, 1)

            scores(0)
            scores(1)
            for u in range(NU):
                if u + 2 < NU:
                    scores(u + 2)
                turn(u)
                if u >= 1:
                    values(u - 1)
            values(NU - 1)
            pe.wait_ge(o_ev, NT)
            for kk in range(KD):
                for n in range(NH):
                    for i in range(4):
                        last = nc.tensor.transpose(PS[:, 2 * kk + n, i * P:(i + 1) * P],
                                                   ON[:, 4 * n + i].rearrange("p h d -> p (h d)")[:, kk * P:(kk + 1) * P],
                                                   core.ident[:])
                    last.then_inc(ot_mm, 1)
            pe.wait_ge(ot_ev, KD * NH)
            for i in range(NT):
                if i >= 4:
                    pe.wait_ge(y_ev, i - 3)
                for kk in range(KD):
                    last = nc.tensor.matmul(PS[:, 4 + i % 4, 0:D], OT[:, kk, i * P:(i + 1) * P],
                                            W[:, 3, kk, :], start=(kk == 0), stop=(kk == KD - 1))
                last.then_inc(y_mm, 1)

        @block.scalar
        def _(act):
            if rope is None:
                act.wait_ge(b_in, B_IN)
                for g, (i, m, n, cp) in enumerate(JOBS):
                    act.wait_ge(mm, g + 1)
                    nc.scalar.activation(QK[:, i, m, n * NB:(n + 1) * NB], PS[:, g % 4, :], ACT.Identity,
                                         bias=BC[:, i, m:m + 1]).then_inc(ev, 1)
            act.wait_ge(km_d, 1)
            for kk in range(KD):
                act.wait_ge(k_ready, k_count(kk))
                for h in range(2, 4):
                    last = nc.scalar.activation(KM[:, kk, h], QK[:, 1, kk], ACT.Copy, scale=HMASK[:, h:h + 1])
            last.then_inc(km_d, 1)
            for u, (b, qt, kt, h, per) in enumerate(UNITS):
                act.wait_ge(max_d, u + 1)
                if u >= 4:
                    act.wait_ge(t_mm, u - 3)
                w = NB // per
                for j in range(per):
                    last = nc.scalar.activation(PR[:, u % 4, j * w:(j + 1) * w], PS[:, u % 3, j * w:(j + 1) * w],
                                                ACT.Exp, bias=NM[:, u % 4, j:j + 1])
                last.then_inc(exp_d, 1)

        @block.vector
        def _(dve):
            c = Chain(dve, chain_v)
            c.then(nc.vector.tensor_reduce(HMASK[:], core.ident[:].rearrange("p (h d) -> p h d", d=HD), AX.X, ALU.add))
            nc.vector.tensor_scalar(HMASK[:], HMASK[:], float(HD) ** -0.5, None, ALU.mult).then_inc(km_d, 1)
            if rope is not None:
                dve.wait_ge(w_in, W_IN)
                dve.wait_ge(b_in, B_IN)
                two = lambda t: t.rearrange("p (b t) -> p b t", t=T)
                trig = lambda x: TRIG[:, x].unsqueeze(1).broadcast_to([P, NB // T, T])
                for g, (i, m, n, cp) in enumerate(JOBS):
                    dve.wait_ge(mm, g + 1)
                    o = QK[:, i, m, n * NB:(n + 1) * NB]
                    if cp == 0:
                        nc.vector.scalar_tensor_tensor(two(o), two(PS[:, g % 4, :]), BC[:, i, m:m + 1], trig(0),
                                                       ALU.add, ALU.mult).then_inc(ev, 1)
                    else:
                        r = g // 2 % 2
                        nc.vector.scalar_tensor_tensor(two(RS[:, r]), two(PS[:, g % 4, :]), BS[:, i, m:m + 1], trig(1),
                                                       ALU.add, ALU.mult).then_inc(ev, 1)
                        dve.wait_ge(ev, g + 1)
                        nc.vector.tensor_tensor(o, o, RS[:, r], ALU.add).then_inc(rot, 1)
            else:
                dve.wait_ge(b_in, B_IN)
            for i in range(NT):
                dve.wait_ge(v_mm, i + 1)
                nc.vector.tensor_tensor(V[:, i, :, 0:HD], PS[:, 4 + i % 4, 0:D].rearrange("p (h d) -> p h d", d=HD),
                                        BV[:, 0].rearrange("p (h d) -> p h d", d=HD), ALU.add).then_inc(v_ev, 1)
            dve.wait_ge(k_ready, k_count(KD - 1))
            dve.wait_ge(km_d, 1)
            for kk in range(KD):
                for h in range(4, HK):
                    last = nc.vector.tensor_scalar(KM[:, kk, h], QK[:, 1, kk], HMASK[:, h:h + 1], None, ALU.mult)
            last.then_inc(km_d, 1)
            dve.wait_ge(consts, 2)

            def evacuate(u):
                b, qt, kt, h, per = UNITS[u]
                dve.wait_ge(t_mm, u + 1)
                if u >= 4:
                    dve.wait_ge(o_mm, u - 3)
                nc.vector.tensor_copy(PT[:, u % 4, :], PS[:, 3 + u % 2, :]).then_inc(t_ev, 1)

            def normalise(i):
                dve.wait_ge(o_mm, last_unit[i] + 1)
                o = PS[:, 5 + i % 2, 0:HEADS * (HD + 1)].rearrange("p (h d) -> p h d", d=HD + 1)
                c.then(nc.vector.reciprocal(REC[:, i % 2], o[:, :, HD]))
                nc.vector.tensor_tensor(ON[:, i], o[:, :, 0:HD],
                                        REC[:, i % 2].unsqueeze(2).broadcast_to([P, HEADS, HD]),
                                        ALU.mult).then_inc(o_ev, 1)

            done = 0
            for u, (b, qt, kt, h, per) in enumerate(UNITS):
                dve.wait_ge(s_mm, u + 1)
                if u >= 4:
                    dve.wait_ge(exp_d, u - 3)
                nc.vector.tensor_reduce(NM[:, u % 4, 0:per], PS[:, u % 3, :].rearrange("p (h j) -> p h j", h=per),
                                        AX.X, ALU.max, negate=True).then_inc(max_d, 1)
                if u >= 1:
                    evacuate(u - 1)
                if done < NT and u >= last_unit[done] + 3:
                    normalise(done)
                    done += 1
            evacuate(NU - 1)
            for i in range(done, NT):
                normalise(i)
            for g in range(KD * NH):
                kk, n = g // NH, g % NH
                dve.wait_ge(ot_mm, g + 1)
                nc.vector.tensor_copy(OT[:, kk, n * NB:(n + 1) * NB], PS[:, g, :]).then_inc(ot_ev, 1)
            if bo is not None:
                dve.wait_ge(bo_d, 1)
            for i in range(NT):
                dve.wait_ge(y_mm, i + 1)
                nc.vector.tensor_tensor(dst[:, i, :], PS[:, 4 + i % 4, 0:D], dst[:, i, :],
                                        ALU.add).then_inc(y_ev, 1)
    s.end()


def routed_ffn(core):
    nc, a, X, XN, XT, PS = core.nc, core.a, core.X, core.XN, core.XT, core.PS
    I, SH = 176, 704
    HID = E * I + SH
    TILES = -(-HID // P)
    R = E + 1
    s = Stage(core, "rffn")
    WG = s.sb("WG", [P, KD, R])
    logit = s.sb("logit", [P, NT, E])
    prob = s.sb("prob", [P, NT, E])
    weight = s.sb("weight", [P, NT, R])
    rank = s.sb("rank", [P, E])
    s.top_m = s.sb("top_m", [P, NT])
    s.top_eq = s.sb("top_eq", [P, NT, E])
    s.top_oh = s.sb("top_oh", [P, 2, NT, E])
    s.top_rest = s.sb("top_rest", [P, NT, E])
    mx = s.sb("mx", [P, NT])
    WT = s.sb("WT", [NT * R, P])
    CB = s.sb("CB", [P, TILES, N])
    UP = 2 * KD * P
    W = s.sb("W", [P, TILES, UP + D])
    UW = [s.sb(f"UW{q}", [P, 2, UP], PART) for q in range(2)]
    DW = [s.sb(f"DW{q}", [P, 2, D], PART) for q in range(2)]
    XP = [s.sb(f"XP{q}", [P, KD, N], PART) for q in range(2)]
    HP = [s.sb(f"HP{q}", [P, 2, N], PART) for q in range(2)]
    PASSES = ((0, 0), (0, 1), (1, 0))
    SG = s.sb("SG", [P, 2, NB])
    SU = s.sb("SU", [P, 2, NB])
    HF = s.sb("HF", [P, 2, NB])
    YT = XN[:].rearrange("p i d -> p (i d)").rearrange("p (k n) -> p k n", k=KD)
    scratch = nc.dram_tensor(f"routes_{s.tag}", (R, NT, P), FP32, kind="Internal").ap()
    g_in, r_mm, log_d, sub_d, exp_d, chain_v, route_d, wt_mm, wt_d, wt_out, res_d = (s.sem(n) for n in (
        "g_in", "r_mm", "log_d", "sub_d", "exp_d", "chain_v", "route_d", "wt_mm", "wt_d", "wt_out", "res_d"))
    xh_d, xl_d, uh_d, ul_d, dh_d, dl_d, hh_d, hl_d = (s.sem(n) for n in (
        "xh_d", "xl_d", "uh_d", "ul_d", "dh_d", "dl_d", "hh_d", "hl_d"))
    GROUPS = (0, 1, 3, 7, 11, TILES)
    w_in = [s.sem(f"w_in{i}") for i in range(len(GROUPS) - 1)]
    r_in = [s.sem(f"r_in{i}") for i in range(len(GROUPS) - 1)]
    up_mm, silu_d, su_d, h_d, dn_mm, yt_ev, y_mm = (s.sem(n) for n in (
        "up_mm", "silu_d", "su_d", "h_d", "dn_mm", "yt_ev", "y_mm"))
    PIECES = []
    for m in range(TILES):
        u = m * P
        while u < (m + 1) * P:
            r = min(u // I, E)
            end = (m + 1) * P if r == E else min((r + 1) * I, (m + 1) * P)
            PIECES.append((m, u - m * P, end - m * P, r))
            u = end

    pieces = lambda i: 16 * sum(GROUPS[i] <= p[0] < GROUPS[i + 1] for p in PIECES)

    def arrived(engine, sems, count, m):
        if m in GROUPS:
            engine.wait_ge(sems[GROUPS.index(m)], count(GROUPS.index(m)))

    def tiles(engine, body, ahead):
        starts = [g - ahead for g in GROUPS[:-1]]
        m = 0
        while m < TILES:
            end = min([g for g in starts if g > m] + [TILES - 1 if m < TILES - 1 else TILES])
            if m % 2 == 1 and m not in starts and (end - m) // 2 >= 2:
                with engine.Fori(0, (end - m) // 2) as j:
                    body(2 * j + m, 1)
                    body(2 * j + m + 1, 0)
                m += (end - m) // 2 * 2
            else:
                body(m, m % 2)
                m += 1

    with nc.Block() as block:
        @block.sync
        def _(sp):
            sp.dma_start(WG[:, :, 0:E], a["L1_ffn_w_router"].rearrange("(k p) e -> p k e", p=P)).then_inc(g_in, 16)
            sp.dma_start(WG[:, :, E:R], a["L1_ffn_w_sh_eg"].rearrange("(k p) e -> p k e", p=P),
                         allow_slow_non_contiguous=True).then_inc(g_in, 16)

            def load(i):
                at = slice(GROUPS[i], GROUPS[i + 1])
                sp.dma_start(W[:, at], a["L1_ffn_tiles"][:, at]).then_inc(w_in[i], 16)

            load(0)
            load(1)
            load(2)
            sp.wait_ge(g_in, 32)
            sp.wait_ge(wt_d, 1)
            for i in range(NT):
                sp.dma_start(scratch[:, i, :], WT[i * R:(i + 1) * R, :]).then_inc(wt_out, 16)
            sp.wait_ge(wt_out, 16 * NT)
            for i in range(len(GROUPS) - 1):
                if i > 2:
                    load(i)
                for m, lo, hi, r in PIECES:
                    if GROUPS[i] <= m < GROUPS[i + 1]:
                        sp.dma_start(CB[lo:hi, m, :], scratch[r:r + 1].rearrange("o i p -> o (i p)")
                                     .broadcast_to([hi - lo, N])).then_inc(r_in[i], 16)
            for i in range(len(GROUPS) - 1):
                sp.wait_ge(w_in[i], 16)
                sp.wait_ge(r_in[i], pieces(i))

        @block.gpsimd
        def _(pool):
            def up_weights(m, r):
                pool.wait_ge(uh_d, m + 1)
                nc.gpsimd.tensor_tensor(UW[1][:, r], W[:, bass.ds(m, 1), 0:UP].rearrange("p o n -> p (o n)"), UW[0][:, r],
                                        ALU.subtract).then_inc(ul_d, 1)

            def tile(m, r):
                if not (isinstance(m, int) and m == TILES - 1):
                    up_weights(m + 1, 1 - r)
                for n in range(NH):
                    x = slice(n * NB, (n + 1) * NB)
                    pool.wait_ge(hh_d, NH * m + n + 1)
                    nc.gpsimd.tensor_tensor(HP[1][:, r, x], HF[:, n, :], HP[0][:, r, x], ALU.subtract).then_inc(hl_d, 1)
                pool.wait_ge(dh_d, m + 1)
                nc.gpsimd.tensor_tensor(DW[1][:, r], W[:, bass.ds(m, 1), UP:].rearrange("p o n -> p (o n)"), DW[0][:, r],
                                        ALU.subtract).then_inc(dl_d, 1)

            up_weights(0, 0)
            nc.gpsimd.tensor_tensor(X[:], X[:], XN[:], ALU.add).then_inc(res_d, 1)
            tiles(pool, tile, 0)

        @block.tensor
        def _(pe):
            pe.wait_ge(g_in, 32)
            for i in range(NT):
                for k in range(KD):
                    last = nc.tensor.matmul(PS[:, 7, i * R:(i + 1) * R], XT[:, k, i * P:(i + 1) * P],
                                            WG[:, k, :], start=(k == 0), stop=(k == KD - 1))
            last.then_inc(r_mm, 1)
            pe.wait_ge(route_d, 1)
            nc.tensor.transpose(PS[0:NT * R, 6, 0:P], weight[:].rearrange("p i r -> p (i r)"),
                                core.ident[:]).then_inc(wt_mm, 1)
            pe.wait_ge(wt_d, 1)

            pe.wait_ge(xh_d, 1)
            pe.wait_ge(xl_d, 1)

            def up(m, r, first):
                pe.wait_ge(uh_d, m + 1)
                pe.wait_ge(ul_d, m + 1)
                for n in range(NH):
                    if not first:
                        pe.wait_ge(h_d, NH * m - NH + n + 1)
                    for q in range(2):
                        for k in range(KD):
                            for step, (qw, qx) in enumerate(PASSES):
                                last = nc.tensor.matmul(PS[:, 4 + 2 * n + q, :],
                                                        UW[qw][:, r, (q * KD + k) * P:(q * KD + k + 1) * P],
                                                        XP[qx][:, k, n * NB:(n + 1) * NB], start=(k + step == 0),
                                                        stop=(k == KD - 1 and step == 2))
                    last.then_inc(up_mm, 1)

            def down(m, r, start, stop):
                pe.wait_ge(dh_d, m + 1)
                pe.wait_ge(dl_d, m + 1)
                for n in range(NH):
                    pe.wait_ge(hh_d, NH * m + n + 1)
                    pe.wait_ge(hl_d, NH * m + n + 1)
                    for q in range(KD):
                        for step, (qw, qx) in enumerate(PASSES):
                            last = nc.tensor.matmul(PS[:, n * KD + q, :], DW[qw][:, r, q * P:(q + 1) * P],
                                                    HP[qx][:, r, n * NB:(n + 1) * NB], start=start and step == 0,
                                                    stop=stop and step == 2)
                last.then_inc(dn_mm, 1)

            up(0, 0, True)
            up(1, 1, False)
            down(0, 0, True, False)
            with pe.Fori(1, TILES // 2) as j:
                up(2 * j, 0, False)
                down(2 * j - 1, 1, False, False)
                up(2 * j + 1, 1, False)
                down(2 * j, 0, False, False)
            up(TILES - 1, 0, False)
            down(TILES - 2, 1, False, False)
            down(TILES - 1, 0, False, True)
            for i in range(NT):
                pe.wait_ge(yt_ev, KD * (i // 4 + 1))
                for k in range(KD):
                    last = nc.tensor.transpose(PS[:, 4 + i // 2, (i % 2) * D + k * P:(i % 2) * D + (k + 1) * P],
                                               YT[:, k, i * P:(i + 1) * P], core.ident[:])
                if i % 2:
                    last.then_inc(y_mm, 1)

        @block.scalar
        def _(act):
            nc.scalar.copy(XP[0][:], XT[:]).then_inc(xh_d, 1)
            act.wait_ge(r_mm, 1)
            l = PS[:, 7, 0:NT * R].rearrange("p (i e) -> p i e", e=R)
            nc.scalar.activation(weight[:, :, E:R], l[:, :, E:R], ACT.Sigmoid)
            nc.scalar.activation(logit[:], l[:, :, 0:E], ACT.Copy).then_inc(log_d, 1)
            act.wait_ge(sub_d, 1)
            nc.scalar.activation(prob[:], logit[:], ACT.Exp).then_inc(exp_d, 1)
            act.wait_ge(wt_mm, 1)
            nc.scalar.copy(WT[:], PS[0:NT * R, 6, 0:P]).then_inc(wt_d, 1)

            def up_weights(m, r):
                if isinstance(m, int):
                    arrived(act, w_in, lambda i: 16, m)
                    if m >= 2:
                        act.wait_ge(up_mm, NH * m - NH)
                else:
                    act.wait_ge(up_mm, NH * m - NH)
                nc.scalar.copy(UW[0][:, r], W[:, bass.ds(m, 1), 0:UP].rearrange("p o n -> p (o n)")).then_inc(uh_d, 1)

            def tile(m, r):
                last_tile = isinstance(m, int) and m == TILES - 1
                early = isinstance(m, int) and m < 2
                if not last_tile:
                    up_weights(m + 1, 1 - r)
                for n in range(NH):
                    act.wait_ge(up_mm, NH * m + n + 1)
                    if not (early and m == 0):
                        act.wait_ge(h_d, NH * m + n - 1)
                    nc.scalar.activation(SG[:, n, :], PS[:, 4 + 2 * n, :], ACT.Silu).then_inc(silu_d, 1)
                    if n:
                        hidden(m, r, n - 1, early)
                hidden(m, r, NH - 1, early)
                nc.scalar.copy(DW[0][:, r], W[:, bass.ds(m, 1), UP:].rearrange("p o n -> p (o n)")).then_inc(dh_d, 1)

            def hidden(m, r, n, early):
                if n == 0 and not early:
                    act.wait_ge(dn_mm, m - 1)
                act.wait_ge(h_d, NH * m + n + 1)
                nc.scalar.copy(HP[0][:, r, n * NB:(n + 1) * NB], HF[:, n, :]).then_inc(hh_d, 1)

            up_weights(0, 0)
            tiles(act, tile, 1)
            act.wait_ge(res_d, 1)
            for n in range(NH):
                act.wait_ge(dn_mm, TILES)
                for q in range(KD):
                    nc.scalar.copy(YT[:, q, n * NB:(n + 1) * NB], PS[:, n * KD + q, :]).then_inc(yt_ev, 1)

        @block.vector
        def _(dve):
            c = Chain(dve, chain_v)
            for e in range(E):
                last = nc.vector.memset(rank[:, e:e + 1], float(E - e))
            c.then(last)
            dve.wait_ge(xh_d, 1)
            nc.vector.tensor_tensor(XP[1][:], XT[:], XP[0][:], ALU.subtract).then_inc(xl_d, 1)
            dve.wait_ge(log_d, 1)
            c.then(nc.vector.tensor_reduce(mx[:], logit[:], AX.X, ALU.max))
            nc.vector.tensor_tensor(logit[:], logit[:], mx[:].unsqueeze(2).broadcast_to([P, NT, E]),
                                    ALU.subtract).then_inc(sub_d, 1)
            dve.wait_ge(exp_d, 1)
            c.then(nc.vector.tensor_reduce(mx[:], prob[:], AX.X, ALU.add))
            c.then(nc.vector.reciprocal(mx[:], mx[:]))
            c.then(nc.vector.tensor_tensor(prob[:], prob[:], mx[:].unsqueeze(2).broadcast_to([P, NT, E]), ALU.mult))
            top2(core, s, dve, c, prob, weight[:, :, 0:E], rank).then_inc(route_d, 1)

            def tile(m, r):
                first = isinstance(m, int) and m == 0
                if isinstance(m, int):
                    arrived(dve, r_in, pieces, m)
                for n in range(NH):
                    cols = slice(n * NB, (n + 1) * NB)
                    dve.wait_ge(up_mm, NH * m + n + 1)
                    nc.vector.tensor_tensor(SU[:, n, :], PS[:, 5 + 2 * n, :], CB[:, bass.ds(m, 1), cols]
                                            .rearrange("p o n -> p (o n)"), ALU.mult).then_inc(su_d, 1)
                    dve.wait_ge(silu_d, NH * m + n + 1)
                    dve.wait_ge(su_d, NH * m + n + 1)
                    if not first:
                        dve.wait_ge(hl_d, NH * m + n - 1)
                    nc.vector.tensor_tensor(HF[:, n, :], SG[:, n, :], SU[:, n, :], ALU.mult).then_inc(h_d, 1)

            tiles(dve, tile, 0)
            dve.wait_ge(res_d, 1)
            for i in range(NT):
                dve.wait_ge(y_mm, i // 2 + 1)
                nc.vector.tensor_tensor(X[:, i, :], PS[:, 4 + i // 2, (i % 2) * D:(i % 2 + 1) * D], X[:, i, :], ALU.add)
    s.end()


def delta_attention(core):
    nc, a, X, XT, PS = core.nc, core.a, core.X, core.XT, core.PS
    YT = core.XN[:].rearrange("p i d -> p (i d)").rearrange("p (k n) -> p k n", k=KD)
    H, HD, TAPS = 16, 128, 4
    BT, OC, C = 64, 32, 8
    NBLK, NO, NI = T // BT, BT // OC, OC // C
    BH = H * B
    GB_ = 16
    NG = BH // GB_
    SB_ = 4
    NS = BH // SB_
    WIN = BT + TAPS - 1
    NW = BH * BT // NB
    outer = Stage(core, "delta")
    sb = outer.sb
    XP = sb("XP", [P, KD, B, T + TAPS - 1])
    KQ = sb("KQ", [P, 2, NO, BH, OC])
    V = sb("V", [P, BH, BT])
    A = sb("A", [P, BH, BT])
    S = sb("S", [P, BH, HD])
    F = sb("F", [P, BH, 2 * OC])
    WC = sb("WC", [P, BH, OC])
    DS = sb("DS", [P, BH, NI, C])
    AJ = sb("AJ", [P, BH, NI])
    AO = sb("AO", [P, BH])
    MIX = sb("MIX", [P, 3072])
    WG = sb("WG", [P, 4, KD * P])
    PR = sb("PR", [P, BH * C * C])
    BE = sb("BE", [P, BH, OC])
    CW = sb("CW", [P, 3, H, TAPS])
    CB = sb("CB", [P, 4, H])
    WB = sb("WB", [P, KD, H])
    BB = sb("BB", [H, 1])
    BETA = sb("BETA", [H, B, T])
    LN = sb("LN", [P, 3])
    ONES = sb("ONES", [P, P])
    SEL = sb("SEL", [P, 2 * NW - 1])
    M16 = sb("M16", [P, GB_])
    M4 = sb("M4", [P, SB_])
    WH = MIX[:, 0:2048].rearrange("p (r i k n) -> p r i k n", r=2, i=4, k=KD)
    KR = MIX[:, 0:1024].rearrange("p (r q k) -> p r q k", r=2, q=SB_)
    BD = MIX[0:H, 1024:].rearrange("p (h b t) -> p h b t", h=H, b=B)
    ST = PR[:, BH * C * C - 3 * NB:].rearrange("p (r n) -> p r n", r=3)
    WT = PR[:, BH * C * C - 3 * NB - 2 * P:BH * C * C - 3 * NB].rearrange("p (r n) -> p r n", r=2)
    TMP = PR[:, 0:6 * B * BT].rearrange("p (r i b t) -> p r i b t", r=2, i=3, b=B)
    room = XT[:].rearrange("p k n -> p (k n)")
    T1 = room[:, 0:BH * (2 * C - 1)]
    U = room[:, 960:960 + BH * C].rearrange("p (n t) -> p n t", t=C)
    WJ = room[:, 1472:1472 + NG * P].rearrange("p (g v) -> p g v", g=NG)
    E1 = room[:, 1984:1984 + BH]
    WO = F[:].rearrange("p n w -> p (n w)").rearrange("p (h k n) -> p h k n", h=H, k=KD)
    KC = WG[:].rearrange("p r n -> p (r n)")[:, 0:BH * C]
    ROWS = MIX[0:NW, 1024:1024 + NW * P].rearrange("p (g n) -> p g n", g=NW)
    SQ, INV = KQ[:, 0].rearrange("p o n t -> p (o n t)"), KQ[0:NW, 1, 0].rearrange("p n t -> p (n t)")[:, 0:NB]
    VF, AF = (t[:].rearrange("p n t -> p (n t)") for t in (V, A))
    fcol = lambda t: F[:, :, t]

    c_in, z_mm, beta_d = (outer.sem(n) for n in ("c_in", "z_mm", "beta_d"))
    CIN = 16 * (3 + 3 + 1 + 1 + 1 + 2)
    with nc.Block() as block:
        @block.sync
        def _(sp):
            pre = "L1_attn_b_"
            for i, n in enumerate("qkv"):
                sp.dma_start(CW[:, i], a[pre + n + "conv_w"].rearrange("(h p) t -> p h t", p=P)).then_inc(c_in, 16)
                sp.dma_start(CB[:, i], a[pre + n + "conv_b"].rearrange("(h p) -> p h", p=P),
                             allow_slow_non_contiguous=True).then_inc(c_in, 16)
            sp.dma_start(CB[:, 3], a[pre + "ba"].rearrange("(h p) -> p h", p=P),
                         allow_slow_non_contiguous=True).then_inc(c_in, 16)
            sp.dma_start(WB[:], a[pre + "Wb"].rearrange("(k p) h -> p k h", p=P)).then_inc(c_in, 16)
            sp.dma_start(BB[:], a[pre + "bb"].rearrange("(h o) -> h o", o=1)).then_inc(c_in, 16)
            for i, n in enumerate(("ln_g", "ln_b")):
                sp.dma_start(LN[:, i:i + 1], a[pre + n].rearrange("(p o) -> p o", o=1)).then_inc(c_in, 16)
            sp.wait_ge(c_in, CIN)

        @block.gpsimd
        def _(pool):
            nc.gpsimd.memset(XP[:, :, :, 0:TAPS - 1], 0.0)
            nc.gpsimd.memset(ONES[:], 1.0)
            nc.gpsimd.memset(SEL[:, 0:NW - 1], 0.0)
            nc.gpsimd.memset(SEL[:, NW - 1:NW], 1.0)
            nc.gpsimd.memset(SEL[:, NW:], 0.0)
            nc.gpsimd.memset(LN[:, 2:3], LN_EPS)
            nc.gpsimd.memset(DS[:, :, :, C - 1:C], 1.0)
            nc.gpsimd.memset(S[:], 0.0)

        @block.tensor
        def _(pe):
            pe.wait_ge(c_in, CIN)
            for n in range(NH):
                for k in range(KD):
                    last = nc.tensor.matmul(PS[0:H, n, :], WB[:, k, :], XT[:, k, n * NB:(n + 1) * NB],
                                            start=(k == 0), stop=(k == KD - 1))
                last.then_inc(z_mm, 1)

        @block.scalar
        def _(act):
            act.wait_ge(c_in, CIN)
            for n in range(NH):
                act.wait_ge(z_mm, n + 1)
                nc.scalar.activation(BETA[:].rearrange("h b t -> h (b t)")[:, n * NB:(n + 1) * NB], PS[0:H, n, :],
                                     ACT.Sigmoid, bias=BB[:]).then_inc(beta_d, 1)

        @block.vector
        def _(dve):
            for k in range(KD):
                nc.vector.tensor_copy(XP[:, k, :, TAPS - 1:], XT[:, k].rearrange("p (b t) -> p b t", b=B))
            nc.vector.tensor_reduce(M16[:], core.ident[:].rearrange("p (n t) -> p n t", t=C), AX.X, ALU.add)
            nc.vector.tensor_reduce(M4[:], core.ident[:].rearrange("p (n t) -> p n t", t=OC), AX.X, ALU.add)
    nc.gpsimd.sem_clear(c_in)
    nc.gpsimd.sem_clear(z_mm)
    nc.gpsimd.sem_clear(beta_d)
    nc.all_engine_barrier()

    USES = []
    for ci in range(NO * NI):
        if ci % NI < NI - 1:
            USES += [("gram", ci, g) for g in range(NG)] + [("turn", ci, 0)] + [("rest", ci, g) for g in range(NG)]
    use = {key: i for i, key in enumerate(USES)}
    slot = lambda key: 4 + 2 * (use[key] % 2)

    def one_block(n):
        s = Stage(core, "block")
        names = ["p_mm", "tap0", "tap_c", "conv_d", "act_d", "raw_d", "a_d", "k_d", "bd_d", "be_mm", "be_d", "pr_d",
                 "g_mm", "step", "ds_d", "w_d", "gram_mm", "gram_d", "turn_mm", "turn_d", "rest_mm", "fr_d", "add_d",
                 "dec_d", "wdec_d", "rows_mm", "rows_d", "up_mm", "sadd_d", "st_mm", "st_d", "f_mm", "f_d", "o_d", "gate_mm",
                 "gate_d", "kc_d", "wc_d", "mean_mm", "cen_d", "sq_d", "var_mm", "root_d", "inv_d", "spread_mm", "scaled_d", "out_d", "yo_mm", "chain_v", "chain_p"]
        (p_mm, tap0, tap_c, conv_d, act_d, raw_d, a_d, k_d, bd_d, be_mm, be_d, pr_d, g_mm, step, ds_d, w_d, gram_mm,
         gram_d, turn_mm, turn_d, rest_mm, fr_d, add_d, dec_d, wdec_d, rows_mm, rows_d, up_mm, sadd_d, st_mm, st_d, f_mm,
         f_d, o_d, gate_mm, gate_d, kc_d, wc_d, mean_mm, cen_d, sq_d, var_mm, root_d, inv_d, spread_mm, scaled_d, out_d, yo_mm, chain_v, chain_p) = (
            s.sem(x) for x in names)
        wh_in = [s.sem("wh_in0"), s.sem("wh_in1")]
        wg_in = [s.sem(f"wg_in{i}") for i in range(4)]
        wo_in = [s.sem(f"wo_in{i}") for i in range(4)]
        width = lambda t: 2 * (C - t) - 1
        prod = lambda t: PR[:, BH * sum(map(width, range(t))):BH * sum(map(width, range(t + 1)))].rearrange(
            "p (n w) -> p n w", n=BH)
        rest = lambda jj: 2 * (OC - (jj + 1) * C)
        with nc.Block() as block:
            @block.sync
            def _(sp):
                outs = a["L1_attn_b_outs"]

                def load(h, r):
                    sp.dma_start(WH[:, r].rearrange("p i k n -> p (i k n)"), a["L1_attn_b_heads"][h]).then_inc(wh_in[r], 16)

                for h in range(H):
                    if h >= 2:
                        sp.wait_ge(p_mm, 4 * (h - 1))
                    load(h, h % 2)
                sp.wait_ge(gram_mm, NG * (NI - 1) * NO)
                for h in range(H):
                    if h >= 4:
                        sp.wait_ge(gate_mm, h - 3)
                    sp.dma_start(WG[:, h % 4], outs[h, :, 0:KD * P]).then_inc(wg_in[h % 4], 16)
                    if h == 3:
                        sp.wait_ge(o_d, NO * NI)
                        for q in range(4):
                            at = slice(H // 4 * q, H // 4 * (q + 1))
                            sp.dma_start(WO[:, at].rearrange("p h k n -> p h (k n)"),
                                         outs[at, :, KD * P:].rearrange("h p n -> p h n")).then_inc(wo_in[q], 16)
                for r in range(2):
                    sp.wait_ge(wh_in[r], 16 * H // 2)
                for r in range(4):
                    sp.wait_ge(wg_in[r], 16 * H // 4)
                    sp.wait_ge(wo_in[r], 16)

            @block.gpsimd
            def _(pool):
                c = Chain(pool, chain_p)

                def beta_rows(o):
                    for b in range(B):
                        last = nc.gpsimd.tensor_tensor(BD[:, :, b],
                                                       BETA[:, b:b + 1, bass.ds(n * BT + o * OC, OC)].broadcast_to([H, H, OC]),
                                                       core.ident[0:H, 0:H].unsqueeze(2).broadcast_to([H, H, OC]), ALU.mult)
                    last.then_inc(bd_d, 1)

                def decays(o):
                    av = A[:, :, o * OC:(o + 1) * OC].rearrange("p n (j t) -> p n j t", t=C)
                    if o:
                        pool.wait_ge(w_d, o * NI)
                    for t in reversed(range(C - 1)):
                        last = nc.gpsimd.tensor_tensor(DS[:, :, :, t], DS[:, :, :, t + 1], av[:, :, :, t + 1], ALU.mult)
                        if t:
                            c.then(last)
                    last.then_inc(ds_d, 1)
                    pool.wait_ge(ds_d, o + 1)
                    c.then(nc.gpsimd.tensor_tensor(AJ[:], DS[:, :, :, 0], av[:, :, :, 0], ALU.mult))
                    c.then(nc.gpsimd.tensor_tensor(AO[:], AJ[:, :, 0], AJ[:, :, 1], ALU.mult))
                    for i in range(2, NI):
                        c.then(nc.gpsimd.tensor_tensor(AO[:], AO[:], AJ[:, :, i], ALU.mult))

                def products(ci):
                    o, at = ci // NI, ci % NI * C
                    for t in range(C):
                        if ci:
                            pool.wait_ge(g_mm, C * (ci - 1) + t + 1)
                        if ci % NI == 0 and t == 2:
                            decays(o)
                            pool.wait_ge(f_mm, NS * (o + 1))
                        out = prod(t)
                        k_t = KQ[:, 0, o, :, at + t:at + t + 1]
                        if t < C - 1:
                            nc.gpsimd.tensor_tensor(out[:, :, 1::2], k_t.broadcast_to([P, BH, C - t - 1]),
                                                    KQ[:, 0, o, :, at + t + 1:at + C], ALU.mult)
                        nc.gpsimd.tensor_tensor(out[:, :, 0::2], k_t.broadcast_to([P, BH, C - t]),
                                                KQ[:, 1, o, :, at + t:at + C], ALU.mult).then_inc(pr_d, 1)

                pool.wait_ge(p_mm, 4 * H)
                beta_rows(0)
                for o in range(NO):
                    if o == 0:
                        pool.wait_ge(act_d, 3 * H)
                        nc.gpsimd.tensor_scalar(KQ[:, 0], KQ[:, 0], float(HD) ** -0.5, None, ALU.mult).then_inc(k_d, 1)
                        pool.wait_ge(k_d, 1)
                        pool.wait_ge(a_d, 1)
                    for jj in range(NI):
                        ci = o * NI + jj
                        if ci == 0:
                            products(0)
                        if jj < NI - 1:
                            if jj == 0:
                                pool.wait_ge(f_d, NS * (o + 1))
                            else:
                                pool.wait_ge(add_d, NG * ((NI - 1) * o + jj))
                            r = F[:, :, 2 * (jj + 1) * C:]
                            nc.gpsimd.tensor_tensor(r, r, AJ[:, :, jj:jj + 1].broadcast_to([P, BH, rest(jj)]),
                                                    ALU.mult).then_inc(fr_d, 1)
                        if jj == NI - 1 and o + 1 < NO:
                            pool.wait_ge(rest_mm, NG * ((NI - 1) * o + 2))
                            beta_rows(o + 1)
                        elif jj == NI - 1:
                            pool.wait_ge(be_mm, 4 * NO)
                            nc.gpsimd.tensor_copy(ROWS, core.ident[0:NW, 0:NW].unsqueeze(2).broadcast_to([NW, NW, P])).then_inc(bd_d, 1)
                        if jj:
                            pool.wait_ge(wc_d, ci)
                            r = WC[:, :, 0:jj * C]
                            last = nc.gpsimd.tensor_tensor(r, r, AJ[:, :, jj:jj + 1].broadcast_to([P, BH, jj * C]), ALU.mult)
                            last.then_inc(wdec_d, 1)
                            pool.wait_ge(wdec_d, (NI - 1) * o + jj)
                        if jj >= NI - 2:
                            pool.wait_ge(st_mm, NS * (o + 1))
                            q = slice((jj - NI + 2) * BH // 2, (jj - NI + 3) * BH // 2)
                            nc.gpsimd.tensor_tensor(S[:, q, :], S[:, q, :], AO[:, q].unsqueeze(2).broadcast_to([P, BH // 2, HD]),
                                                    ALU.mult).then_inc(dec_d, 1)
                        if ci + 1 < NO * NI:
                            products(ci + 1)

            @block.tensor
            def _(pe):
                def head(h):
                    r = h % 2
                    pe.wait_ge(wh_in[r], 16 * (h // 2 + 1))
                    if h >= 2:
                        pe.wait_ge(conv_d, 3 * (h - 1))
                        pe.wait_ge(raw_d, h - 1)
                    for i in range(3):
                        for k in range(KD):
                            last = nc.tensor.matmul(PS[:, 4 * r + i, 0:B * WIN], WH[:, r, i, k, :],
                                                    XP[:, k, :, bass.ds(n * BT, WIN)], start=(k == 0), stop=(k == KD - 1))
                        last.then_inc(p_mm, 1)
                    for k in range(KD):
                        last = nc.tensor.matmul(PS[:, 4 * r + 3, 0:B * BT], WH[:, r, 3, k, :],
                                                XP[:, k, :, bass.ds(n * BT + TAPS - 1, BT)],
                                                start=(k == 0), stop=(k == KD - 1))
                    last.then_inc(p_mm, 1)

                def beta(o):
                    pe.wait_ge(bd_d, o + 1)
                    for q in range(4):
                        nc.tensor.matmul(PS[:, q, :], ONES[0:H, :], BD[:, 4 * q:4 * q + 4].rearrange("p h b t -> p (h b t)"),
                                         start=True, stop=True).then_inc(be_mm, 1)

                def rows(o, g):
                    u = NS * o + g
                    at = slice(SB_ * g, SB_ * g + SB_)
                    if g >= 2:
                        pe.wait_ge(rows_d, u - 1)
                    nc.tensor.transpose(PS[:, g % 2, 0:P], KQ[:, 0, o, at, :], core.ident[:])
                    nc.tensor.transpose(PS[:, g % 2, P:2 * P], WC[:, at, :], core.ident[:]).then_inc(rows_mm, 1)

                def update(o, g):
                    u = NS * o + g
                    pe.wait_ge(rows_d, u + 1)
                    if g >= 2:
                        pe.wait_ge(sadd_d, u - 1)
                    nc.tensor.matmul(PS[:, 2 + g % 2, :], WT[:, g % 2, :], KR[:, g % 2].rearrange("p q k -> p (q k)"),
                                     start=True, stop=True).then_inc(up_mm, 1)

                def state_t(o, g):
                    u = NS * o + g
                    if o:
                        pe.wait_ge(sadd_d, NS * (o - 1) + g + 1)
                    if g >= 2:
                        pe.wait_ge(st_d, u - 1)
                    for i in range(SB_):
                        last = nc.tensor.transpose(PS[:, 4 + g % 2, i * P:(i + 1) * P], S[:, SB_ * g + i, :], core.ident[:])
                    last.then_inc(st_mm, 1)

                def columns(o, g):
                    u = NS * o + g
                    pe.wait_ge(st_d, u + 1)
                    if g >= 2:
                        pe.wait_ge(f_d, u - 1)
                    for i in range(SB_):
                        last = nc.tensor.matmul(PS[:, 6 + g % 2, i * 2 * OC:(i + 1) * 2 * OC].rearrange("p (t q) -> p t q", q=2), ST[:, g % 3, i * P:(i + 1) * P],
                                                KQ[:, :, o, SB_ * g + i, :].rearrange("p q t -> p t q"), start=True, stop=True)
                    last.then_inc(f_mm, 1)

                def claim(key):
                    if use[key] >= 2:
                        kind, ci, g = USES[use[key] - 2]
                        cj = ci // NI * (NI - 1) + ci % NI
                        if kind == "gram":
                            pe.wait_ge(gram_d, NG * cj + g + 1)
                        elif kind == "turn":
                            pe.wait_ge(turn_d, cj + 1)
                        else:
                            pe.wait_ge(add_d, NG * cj + g + 1)

                def inner(ci, t):
                    pe.wait_ge(pr_d, C * ci + t + 1)
                    if C * ci + t >= 2:
                        pe.wait_ge(step, C * ci + t - 1)
                    for i in range(2):
                        last = nc.tensor.matmul(PS[:, 2 * (t % 2) + i, 0:32 * width(t)], ONES[:],
                                                prod(t)[:, 32 * i:32 * (i + 1), :].rearrange("p n w -> p (n w)"),
                                                start=True, stop=True)
                    last.then_inc(g_mm, 1)

                def gram(ci, g):
                    o, jj = ci // NI, ci % NI
                    key = ("gram", ci, g)
                    claim(key)
                    if g == 0:
                        pe.wait_ge(kc_d, (NI - 1) * o + jj + 1)
                    for i in range(2):
                        q = GB_ * g + 8 * i
                        last = nc.tensor.matmul(
                            PS[:, slot(key) + i, 0:8 * rest(jj)].rearrange("p (n t q) -> p n t q", n=8, q=2),
                            KC[:, GB_ * g * C:GB_ * (g + 1) * C],
                            KQ[:, :, o, q:q + 8, (jj + 1) * C:].rearrange("p q n t -> p n t q"), start=True, stop=True)
                    last.then_inc(gram_mm, 1)

                def span(o):
                    for jj in range(NI):
                        ci = o * NI + jj
                        for t in range(0 if jj == 0 else 1, C):
                            inner(ci, t)
                            if jj < NI - 1 and 2 <= t < 2 + NG:
                                gram(ci, t - 2)
                        if jj < NI - 1:
                            inner(ci + 1, 0)
                        if jj < NI - 1:
                            cj = (NI - 1) * o + jj
                            key = ("turn", ci, 0)
                            claim(key)
                            pe.wait_ge(w_d, ci + 1)
                            for g in range(NG):
                                last = nc.tensor.transpose(PS[:, slot(key), g * P:(g + 1) * P],
                                                           U[:, GB_ * g:GB_ * (g + 1), :], core.ident[:])
                            last.then_inc(turn_mm, 1)
                            pe.wait_ge(turn_d, cj + 1)
                            w = rest(jj)
                            for g in range(NG):
                                key = ("rest", ci, g)
                                claim(key)
                                pe.wait_ge(gram_d, NG * cj + g + 1)
                                for i in range(2):
                                    last = nc.tensor.matmul(PS[:, slot(key) + i, 0:8 * w], WJ[:, g, :],
                                                            MIX[:, (GB_ * g + 8 * i) * w:(GB_ * g + 8 * i + 8) * w],
                                                            start=True, stop=True)
                                last.then_inc(rest_mm, 1)

                def gate(h):
                    pe.wait_ge(wg_in[h % 4], 16 * (h // 4 + 1))
                    if h >= 2:
                        pe.wait_ge(gate_d, h - 1)
                    for k in range(KD):
                        last = nc.tensor.matmul(PS[:, 4 + h % 2, 0:B * BT], WG[:, h % 4, k * P:(k + 1) * P],
                                                XP[:, k, :, bass.ds(n * BT + TAPS - 1, BT)],
                                                start=(k == 0), stop=(k == KD - 1))
                    last.then_inc(gate_mm, 1)

                def mean(g):
                    if g == 0:
                        pe.wait_ge(o_d, NO * NI)
                    if g >= 2:
                        pe.wait_ge(cen_d, g - 1)
                    nc.tensor.matmul(PS[:, 6 + g % 2, :], ONES[:], VF[:, g * NB:(g + 1) * NB], start=True,
                                     stop=True).then_inc(mean_mm, 1)

                def variance(g):
                    if g == 0:
                        pe.wait_ge(gate_d, H)
                    pe.wait_ge(sq_d, g + 1)
                    last = nc.tensor.matmul(PS[0:NW, 4, :], SEL[:, NW - 1 - g:2 * NW - 1 - g], SQ[:, g * NB:(g + 1) * NB],
                                            start=(g == 0), stop=(g == NW - 1))
                    if g == NW - 1:
                        last.then_inc(var_mm, 1)

                def spread(g):
                    if g == 0:
                        pe.wait_ge(cen_d, NW)
                        pe.wait_ge(inv_d, 1)
                        pe.wait_ge(bd_d, NO + 1)
                    if g >= 4:
                        pe.wait_ge(scaled_d, g - 3)
                    nc.tensor.matmul(PS[:, 4 + g % 4, :], ROWS[:, g, :], INV, start=True, stop=True).then_inc(spread_mm, 1)

                for h in range(H):
                    head(h)
                pe.wait_ge(act_d, 3 * H)
                pe.wait_ge(raw_d, H)
                beta(0)
                pe.wait_ge(k_d, 1)
                for g in range(NS + 1):
                    if g < NS:
                        state_t(0, g)
                    if g >= 1:
                        columns(0, g - 1)
                pe.wait_ge(be_d, 4)
                for o in range(NO):
                    pe.wait_ge(f_d, NS * (o + 1))
                    span(o)
                    pe.wait_ge(wc_d, NI * (o + 1))
                    pe.wait_ge(wdec_d, (NI - 1) * (o + 1))
                    pe.wait_ge(step, C * NI * (o + 1))
                    pe.wait_ge(add_d, NG * (NI - 1) * (o + 1))
                    more = o + 1 < NO
                    for g in range(NS + 4):
                        if g < NS:
                            rows(o, g)
                            if not more:
                                gate(g)
                                if g % 2:
                                    mean(g // 2)
                        if 1 <= g < NS + 1:
                            update(o, g - 1)
                        if more and 3 <= g < NS + 3:
                            state_t(o + 1, g - 3)
                        if more and g >= 4:
                            columns(o + 1, g - 4)
                    pe.wait_ge(rows_d, NS * (o + 1))
                    pe.wait_ge(sadd_d, NS * (o + 1))
                    if more:
                        beta(o + 1)
                        pe.wait_ge(be_d, 4 * (o + 2))
                for g in range(NW):
                    variance(g)
                for g in range(NW):
                    spread(g)
                for h in range(H):
                    pe.wait_ge(out_d, h // 2 + 1)
                    if h % 4 == 0:
                        pe.wait_ge(wo_in[h // 4], 16)
                    for k in range(KD):
                        last = nc.tensor.matmul(PS[:, k, 0:B * BT], WO[:, h, k, :],
                                                VF[:, h * B * BT:(h + 1) * B * BT], start=(h == 0), stop=(h == H - 1))
                    last.then_inc(yo_mm, 1)

            @block.scalar
            def _(act):
                def taps(h):
                    r = h % 2
                    win = lambda bank: PS[:, bank, 0:B * WIN].rearrange("p (b t) -> p b t", b=B)
                    for i in range(3):
                        act.wait_ge(p_mm, 4 * h + i + 1)
                        if h >= 2:
                            act.wait_ge(act_d, 3 * (h - 2) + i + 1)
                        nc.scalar.activation(TMP[:, r, i], win(4 * r + i)[:, :, TAPS - 1:], ACT.Identity,
                                             bias=CB[:, i, h:h + 1], scale=CW[:, i, h, TAPS - 1:TAPS]).then_inc(tap0, 1)
                    act.wait_ge(p_mm, 4 * h + 4)
                    nc.scalar.activation(A[:, B * h:B * h + B].rearrange("p b t -> p (b t)"), PS[:, 4 * r + 3, 0:B * BT],
                                         ACT.Identity, bias=CB[:, 3, h:h + 1]).then_inc(raw_d, 1)

                def silus(h):
                    at = slice(B * h, B * h + B)
                    for i, out in enumerate((KQ[:, 1, :, at, :], KQ[:, 0, :, at, :], V[:, at, :])):
                        act.wait_ge(conv_d, 3 * h + i + 1)
                        x = TMP[:, h % 2, i]
                        if i < 2:
                            x = x.rearrange("p b (o t) -> p o b t", o=NO)
                        nc.scalar.activation(out, x, ACT.Silu).then_inc(act_d, 1)

                for h in range(H + 1):
                    if h < H:
                        taps(h)
                    if h >= 1:
                        silus(h - 1)
                act.wait_ge(raw_d, H)
                nc.scalar.activation(AF, AF, ACT.Sigmoid).then_inc(a_d, 1)

                def beta(o):
                    for q in range(4):
                        act.wait_ge(be_mm, 4 * o + q + 1)
                        nc.scalar.copy(BE[:, GB_ * q:GB_ * q + GB_, :].rearrange("p n t -> p (n t)"),
                                       PS[:, q, :]).then_inc(be_d, 1)

                def rows(o, g):
                    act.wait_ge(rows_mm, NS * o + g + 1)
                    if g >= 2:
                        act.wait_ge(up_mm, NS * o + g - 1)
                    for q in range(SB_):
                        nc.scalar.activation(KR[:, g % 2, q, :], PS[:, g % 2, 0:P], ACT.Copy, scale=M4[:, q:q + 1])
                    nc.scalar.copy(WT[:, g % 2, :], PS[:, g % 2, P:2 * P]).then_inc(rows_d, 1)

                def gate(h):
                    act.wait_ge(gate_mm, h + 1)
                    nc.scalar.activation(AF[:, h * B * BT:(h + 1) * B * BT], PS[:, 4 + h % 2, 0:B * BT],
                                         ACT.Sigmoid).then_inc(gate_d, 1)

                def f_copy(o, g):
                    act.wait_ge(f_mm, NS * o + g + 1)
                    nc.scalar.copy(F[:, SB_ * g:SB_ * (g + 1), :].rearrange("p n w -> p (n w)"),
                                   PS[:, 6 + g % 2, 0:SB_ * 2 * OC]).then_inc(f_d, 1)

                beta(0)
                for g in range(NS):
                    f_copy(0, g)
                for o in range(NO):
                    for jj in range(NI):
                        ci = o * NI + jj
                        if jj < NI - 1:
                            cj = (NI - 1) * o + jj
                            w = rest(jj)
                            if ci == 0:
                                act.wait_ge(k_d, 1)
                            if cj:
                                act.wait_ge(gram_mm, NG * cj)
                            nc.scalar.copy(KC.rearrange("p (n t) -> p n t", t=C),
                                           KQ[:, 0, o, :, jj * C:(jj + 1) * C]).then_inc(kc_d, 1)
                            if cj and jj == 0:
                                act.wait_ge(up_mm, NS * o)
                            elif jj:
                                act.wait_ge(rest_mm, NG * cj)
                            for g in range(NG):
                                act.wait_ge(gram_mm, NG * cj + g + 1)
                                key = ("gram", ci, g)
                                for m in range(GB_):
                                    last = nc.scalar.activation(
                                        MIX[:, (GB_ * g + m) * w:(GB_ * g + m + 1) * w],
                                        PS[:, slot(key) + m // 8, (m % 8) * w:(m % 8 + 1) * w], ACT.Copy,
                                        scale=M16[:, m:m + 1])
                                last.then_inc(gram_d, 1)
                            act.wait_ge(turn_mm, cj + 1)
                            key = ("turn", ci, 0)
                            nc.scalar.copy(WJ.rearrange("p g v -> p (g v)"), PS[:, slot(key), :]).then_inc(turn_d, 1)
                        act.wait_ge(w_d, ci + 1)
                        if o and jj == 0:
                            act.wait_ge(rows_mm, NS * o)
                        nc.scalar.copy(WC[:, :, jj * C:(jj + 1) * C], U).then_inc(wc_d, 1)
                        nc.scalar.copy(V[:, :, o * OC + jj * C:o * OC + (jj + 1) * C],
                                       F[:, :, 2 * jj * C + 1:2 * (jj + 1) * C:2]).then_inc(o_d, 1)
                    for g in range(NS + 4):
                        if g < NS:
                            rows(o, g)
                            if o + 1 == NO:
                                gate(g)
                        if o + 1 < NO and g >= 4:
                            f_copy(o + 1, g - 4)
                    if o + 1 < NO:
                        beta(o + 1)
                act.wait_ge(rows_mm, NS * NO)
                for g in range(NW):
                    act.wait_ge(cen_d, g + 1)
                    nc.scalar.activation(SQ[:, g * NB:(g + 1) * NB], VF[:, g * NB:(g + 1) * NB], ACT.Square).then_inc(sq_d, 1)
                act.wait_ge(var_mm, 1)
                nc.scalar.activation(INV, PS[0:NW, 4, :], ACT.Sqrt, bias=LN[0:NW, 2:3], scale=1.0 / HD).then_inc(root_d, 1)
                act.wait_ge(yo_mm, H)
                for k in range(KD):
                    nc.scalar.copy(YT[:, k].rearrange("p (b t) -> p b t", b=B)[:, :, bass.ds(n * BT, BT)],
                                   PS[:, k, 0:B * BT].rearrange("p (b t) -> p b t", b=B))

            @block.vector
            def _(dve):
                c = Chain(dve, chain_v)

                def head(h):
                    r = h % 2
                    win = lambda bank: PS[:, bank, 0:B * WIN].rearrange("p (b t) -> p b t", b=B)
                    for tau in range(TAPS - 1):
                        for i in range(3):
                            if tau == 0:
                                dve.wait_ge(tap0, 3 * h + i + 1)
                            else:
                                dve.wait_ge(tap_c, 6 * h + 3 * (tau - 1) + i + 1)
                            nc.vector.scalar_tensor_tensor(TMP[:, r, i], win(4 * r + i)[:, :, tau:tau + BT],
                                                           CW[:, i, h, tau:tau + 1], TMP[:, r, i], ALU.mult,
                                                           ALU.add).then_inc(conv_d if tau == TAPS - 2 else tap_c, 1)

                def chunk(o, jj):
                    ci = o * NI + jj
                    at = o * OC + jj * C
                    base = 2 * jj * C
                    if ci:
                        dve.wait_ge(wc_d, ci)
                    for t in range(C):
                        w = width(t)
                        cols_ = F[:, :, base + 2 * t + 1:base + 2 * C]
                        nc.vector.tensor_tensor(E1, fcol(base + 2 * t), V[:, :, at + t], ALU.subtract)
                        c.then(nc.vector.tensor_tensor(cols_, cols_, A[:, :, at + t:at + t + 1].broadcast_to([P, BH, w]), ALU.mult))
                        c.then(nc.vector.tensor_tensor(U[:, :, t], E1, BE[:, :, jj * C + t], ALU.mult))
                        dve.wait_ge(g_mm, C * ci + t + 1)
                        t1 = T1[:, 0:BH * w].rearrange("p (n w) -> p n w", w=w)
                        halves = lambda x: x.rearrange("p (i n) w -> p i n w", i=2)
                        g = PS[:, 2 * (t % 2):2 * (t % 2) + 2, 0:32 * w].rearrange("p i (n w) -> p i n w", w=w)
                        nc.vector.tensor_tensor(halves(t1), g, halves(U[:, :, t:t + 1]).broadcast_to([P, 2, 32, w]),
                                                ALU.mult).then_inc(step, 1)
                        dve.wait_ge(step, C * ci + t + 1)
                        c.then(nc.vector.tensor_tensor(cols_, cols_, t1, ALU.subtract))
                    if jj == 0:
                        dve.wait_ge(ds_d, o + 1)
                    nc.vector.scalar_tensor_tensor(U, U, -1.0, DS[:, :, jj], ALU.mult,
                                                   ALU.mult).then_inc(w_d, 1)
                    if jj < NI - 1:
                        cj = (NI - 1) * o + jj
                        w = rest(jj)
                        dve.wait_ge(fr_d, cj + 1)
                        for g in range(NG):
                            key = ("rest", ci, g)
                            dve.wait_ge(rest_mm, NG * cj + g + 1)
                            r = F[:, GB_ * g:GB_ * (g + 1), 2 * (jj + 1) * C:].rearrange("p (i n) w -> p i n w", i=2)
                            nc.vector.tensor_tensor(r, r, PS[:, slot(key):slot(key) + 2, 0:8 * w]
                                                    .rearrange("p i (n w) -> p i n w", w=w), ALU.add).then_inc(add_d, 1)
                        dve.wait_ge(add_d, NG * (cj + 1))

                for h in range(H):
                    head(h)

                def state_copy(o, g):
                    dve.wait_ge(st_mm, NS * o + g + 1)
                    if g >= 3:
                        dve.wait_ge(f_mm, NS * o + g - 2)
                    nc.vector.tensor_copy(ST[:, g % 3, :], PS[:, 4 + g % 2, :]).then_inc(st_d, 1)

                def centre(g):
                    if g == 0:
                        dve.wait_ge(o_d, NO * NI)
                    dve.wait_ge(mean_mm, g + 1)
                    x = VF[:, g * NB:(g + 1) * NB]
                    nc.vector.scalar_tensor_tensor(x, PS[:, 6 + g % 2, :], -1.0 / HD, x, ALU.mult, ALU.add).then_inc(cen_d, 1)

                for g in range(NS):
                    state_copy(0, g)
                dve.wait_ge(a_d, 1)
                dve.wait_ge(act_d, 3 * H)
                for o in range(NO):
                    dve.wait_ge(f_d, NS * (o + 1))
                    dve.wait_ge(be_d, 4 * (o + 1))
                    for jj in range(NI):
                        chunk(o, jj)
                    dve.wait_ge(dec_d, 2 * (o + 1))
                    for g in range(NS + 2):
                        if g < NS:
                            dve.wait_ge(up_mm, NS * o + g + 1)
                            x = S[:, SB_ * g:SB_ * (g + 1), :].rearrange("p n k -> p (n k)")
                            nc.vector.tensor_tensor(x, x, PS[:, 2 + g % 2, :], ALU.add).then_inc(sadd_d, 1)
                            if o + 1 == NO and g % 2:
                                centre(g // 2)
                        if o + 1 < NO and g >= 2:
                            state_copy(o + 1, g - 2)
                dve.wait_ge(gate_d, H)
                dve.wait_ge(root_d, 1)
                nc.vector.reciprocal(INV, INV).then_inc(inv_d, 1)
                for g in range(NW):
                    x = slice(g * NB, (g + 1) * NB)
                    dve.wait_ge(spread_mm, g + 1)
                    nc.vector.scalar_tensor_tensor(VF[:, x], PS[:, 4 + g % 4, :], LN[:, 0:1], VF[:, x], ALU.mult,
                                                   ALU.mult).then_inc(scaled_d, 1)
                    dve.wait_ge(scaled_d, g + 1)
                    nc.vector.scalar_tensor_tensor(VF[:, x], VF[:, x], LN[:, 1:2], AF[:, x], ALU.add,
                                                   ALU.mult).then_inc(out_d, 1)
        for sem in s.sems:
            nc.gpsimd.sem_clear(sem)
        nc.all_engine_barrier()
        s.ctx.close()

    with nc.Fori(0, NBLK) as n:
        one_block(n)

    t_mm = outer.sem("t_mm")
    with nc.Block() as block:
        @block.tensor
        def _(pe):
            for i in range(NT):
                for k in range(KD):
                    last = nc.tensor.transpose(PS[:, i // 2, (i % 2) * D + k * P:(i % 2) * D + (k + 1) * P],
                                               YT[:, k, i * P:(i + 1) * P], core.ident[:])
                if i % 2:
                    last.then_inc(t_mm, 1)

        @block.vector
        def _(dve):
            for i in range(NT):
                dve.wait_ge(t_mm, i // 2 + 1)
                nc.vector.tensor_tensor(X[:, i, :], PS[:, i // 2, (i % 2) * D:(i % 2 + 1) * D], X[:, i, :], ALU.add)
    outer.end()


def program(nc, args, out):
    with ExitStack() as ctx:
        core = Core(nc, ctx, args)
        setup(core)

        def sub1():
            norm(core, rms_eps=float(np.finfo(np.float32).eps))
            linear_attention(core)

        def sub2():
            norm(core)
            moe(core)

        def sub3():
            norm(core, rms_eps=1e-6, weight=args["L0_attn_b_norm_scale"])
            conv_scan(core)

        def sub5():
            norm(core)
            qkv, b = args["L1_attn_a_W_qkv"], args["L1_attn_a_b_qkv"]
            softmax_attention(core, qkv[:, 0:D], qkv[:, D:2 * D], qkv[:, 2 * D:3 * D], b[0:D], b[D:2 * D], b[2 * D:3 * D],
                              args["L1_attn_a_W_out"], args["L1_attn_a_b_out"], None, None, core.X)

        def sub6():
            w = lambda n: args["L1_ffn_" + n]
            norm(core, rms_eps=1e-6, weight=w("w_ln1"))
            softmax_attention(core, w("wq"), w("wk"), w("wv"), w("bq"), w("bk"), w("bv"), w("wo"), None,
                              args["trig1"], (w("bq_swapped"), w("bk_swapped")), core.XN)
            norm(core, layer=False, rms_eps=1e-6, weight=w("w_ln2"))
            routed_ffn(core)

        def sub7():
            norm(core)
            delta_attention(core)

        subs = [sub1, sub2, sub3, sub2, sub5, sub6, sub7, sub6]
        for f in subs[START:STOP]:
            f()
        finish(core, out)


TURNED = ("L0_attn_a_Wq", "L0_attn_a_Wk", "L0_attn_a_Wv", "L0_attn_a_Wg", "L0_attn_a_Wp",
          "L0_attn_b_in_proj_w", "L0_attn_b_out_proj_w", "L1_attn_a_W_qkv", "L1_attn_a_W_out")


def trig_table(base, head=16):
    inv = (np.float32(1.0) / np.float32(base) ** (np.arange(0, head, 2, dtype=np.float32) / np.float32(head)))
    angle = np.arange(T, dtype=np.float32)[:, None] * inv.astype(np.float32)[None, :]
    cos, sin = np.cos(angle).T, np.sin(angle).T
    return np.ascontiguousarray(np.stack([np.tile(np.concatenate([cos, cos]), (P // head, 1)),
                                          np.tile(np.concatenate([-sin, sin]), (P // head, 1))]).astype(np.float32))


def kernel(**inputs):
    import concourse.bacc as bacc
    from concourse.bass_utils import run_bass_kernel_spmd

    nc = bacc.Bacc("TRN2", target_bir_lowering=False, num_devices=1)
    arrays, args = {}, {}
    for name, a in inputs.items():
        a = np.asarray(a)
        if name in TURNED:
            a = a.T
        a = np.ascontiguousarray(a)
        arrays[f"in_{name}"] = a
        args[name] = nc.dram_tensor(f"in_{name}", a.shape, mybir.dt.from_np(a.dtype), kind="ExternalInput").ap()
    rows = np.ascontiguousarray(np.repeat(np.asarray(inputs["L0_attn_b_head_mix"]), 16, axis=0))
    swap = lambda n: np.ascontiguousarray(np.asarray(inputs[n]).reshape(-1, 2, 8)[:, ::-1].reshape(-1))
    hidden = 17 * P
    f = lambda n: np.asarray(inputs["L1_ffn_" + n])
    up = np.zeros((2, D, hidden), np.float32)
    for i, (routed, shared) in enumerate((("w_gate_e", "w_sh_gate"), ("w_up_e", "w_sh_up"))):
        up[i, :, :E * 176] = f(routed).transpose(1, 0, 2).reshape(D, -1)
        up[i, :, E * 176:E * 176 + 704] = f(shared)
    down = np.zeros((hidden, D), np.float32)
    down[:E * 176] = f("w_down_e").reshape(-1, D)
    down[E * 176:E * 176 + 704] = f("w_sh_down")
    tiles = np.ascontiguousarray(np.concatenate([up.reshape(2, KD, P, 17, P).transpose(2, 3, 0, 1, 4).reshape(P, 17, -1),
                                                 down.reshape(17, P, D).transpose(1, 0, 2)], axis=2))
    g = lambda n: np.asarray(inputs["L1_attn_b_" + n]).reshape(KD, P, 16, P).transpose(2, 1, 0, 3)
    heads = np.ascontiguousarray(np.stack([g("Wq"), g("Wk"), g("Wv"), g("Wa")], axis=2).reshape(16, P, -1))
    wo = np.asarray(inputs["L1_attn_b_Wo"]).reshape(16, P, KD, P)
    outs = np.ascontiguousarray(np.concatenate([g("Wg"), wo], axis=2).reshape(16, P, -1))
    for name, a in (("L1_attn_b_heads", heads), ("L1_attn_b_outs", outs), ("L1_ffn_tiles", tiles),
                    ("L1_ffn_bq_swapped", swap("L1_ffn_bq")), ("L1_ffn_bk_swapped", swap("L1_ffn_bk")),
                    ("L0_attn_b_head_rows", rows), ("trig0", trig_table(10000.0)), ("trig1", trig_table(1e6))):
        arrays[f"in_{name}"] = a
        args[name] = nc.dram_tensor(f"in_{name}", a.shape, FP32, kind="ExternalInput").ap()
    out = nc.dram_tensor("out_0_dram", (B, T, D), FP32, kind="ExternalOutput").ap()
    program(nc, args, out)
    r = run_bass_kernel_spmd(nc, [arrays], core_ids=[0])
    return r.results[0]["out_0_dram"]
```
